# Optimizing a Trainium2 kernel written in Bass

```python
import numpy as np
import jax
import jax.numpy as jnp

def _softmax(x, axis=-1):
    return jax.nn.softmax(x, axis=axis)

def _gelu(x):
    return jax.nn.gelu(x, approximate=True)

def _silu(x):
    return jax.nn.silu(x)

def _sigmoid(x):
    return jax.nn.sigmoid(x)

def _layernorm(x, axis=-1, eps=1e-05):
    m = jnp.mean(x, axis=axis, keepdims=True)
    v = jnp.var(x, axis=axis, keepdims=True)
    return (x - m) / jnp.sqrt(v + eps)

def _scatter_add(tgt, idx, src, axis=0):
    return tgt.at[idx].add(src)

def _segment_sum(src, seg, n):
    return jax.ops.segment_sum(src, seg, n)
kernel_name = 'mk_adaln_d1_jaxref_r8_c7fc19'

def setup_inputs(seed: int=0):
    np.random.seed(seed)
    _w = jnp.asarray

    def _L0_attn_setup():
        import jax, jax.numpy as jnp
        import numpy as np
        DIM = 256
        HEAD_DIM = 128
        NH = DIM // HEAD_DIM
        CHUNK = 128

        def _forward(x, Wq, bq, Wk, bk, Wv, bv, Wbeta, bbeta, Walpha, balpha):
            B, T, D = x.shape
            H, S, C = (NH, HEAD_DIM, CHUNK)
            q = (x @ Wq + bq).reshape(B, T, H, S)
            k = (x @ Wk + bk).reshape(B, T, H, S)
            v = (x @ Wv + bv).reshape(B, T, H, S)
            k = k / jnp.maximum(jnp.linalg.norm(k, axis=-1, keepdims=True), 1e-12)
            alpha_val = jax.nn.sigmoid(x @ Walpha + balpha).reshape(B, T, H, 1)
            beta = jax.nn.softplus(x @ Wbeta + bbeta).reshape(B, T, H, 1)
            pad = -T % C

            def padt(t):
                return jnp.pad(t, ((0, 0), (0, pad), (0, 0), (0, 0))) if pad else t
            qp, kp, vp = (padt(q), padt(k), padt(v))
            ap, bp = (padt(alpha_val), padt(beta))
            Tp = T + pad
            n = Tp // C

            def ch(t):
                return t.reshape(B, n, C, H, t.shape[-1]).transpose(0, 1, 3, 2, 4)
            qc, kc, vc, bc = (ch(qp), ch(kp), ch(vp), ch(bp))
            cla = jnp.cumsum(jnp.log(ch(ap) + 1e-06), axis=3)
            decay = jnp.exp(cla - jnp.swapaxes(cla, -1, -2))
            causal = jnp.tril(jnp.ones((C, C), dtype=bool))
            decay = jnp.where(causal, decay, 0.0)
            attn = jnp.einsum('bnhcd,bnhed->bnhce', qc, kc) * jnp.swapaxes(bc, -1, -2) * decay
            y_local = jnp.einsum('bnhce,bnhed->bnhcd', attn, vc)
            chunk_decay = jnp.exp(cla)
            cla_end = cla[:, :, :, -1:, :]
            total_decay = jnp.exp(cla_end)
            decay_to_end = jnp.exp(cla_end - cla)
            kw = kc * bc * decay_to_end
            delta = jnp.einsum('bnhcd,bnhce->bnhde', vc, kw)
            state0 = jnp.zeros((B, H, S, S), x.dtype)

            def step(state, inp):
                q_i, yloc_i, cd_i, td_i, d_i = inp
                y_glob = jnp.einsum('bhce,bhde->bhcd', q_i, state) * cd_i
                new_state = state * td_i + d_i
                return (new_state, y_glob + yloc_i)
            xs = (jnp.moveaxis(qc, 1, 0), jnp.moveaxis(y_local, 1, 0), jnp.moveaxis(chunk_decay, 1, 0), jnp.moveaxis(total_decay, 1, 0), jnp.moveaxis(delta, 1, 0))
            final_state, y_chunks = jax.lax.scan(step, state0, xs)
            y = jnp.moveaxis(y_chunks, 0, 1)
            y = y.transpose(0, 1, 3, 2, 4).reshape(B, Tp, D)[:, :T, :]
            surprise = jnp.linalg.norm(y_local, axis=-1).mean(axis=-1)
            surprise = surprise.reshape(B, -1, 1).mean(axis=1, keepdims=True)
            return (y, final_state, surprise, alpha_val)

        def _reference_tuple_inner(x, Wq, bq, Wk, bk, Wv, bv, Wbeta, bbeta, Walpha, balpha):
            return _forward(x, Wq, bq, Wk, bk, Wv, bv, Wbeta, bbeta, Walpha, balpha)
        key = jax.random.key(seed)
        ks = jax.random.split(key, 6)
        B, T = (2, 512)
        s = 1.0 / np.sqrt(DIM)

        def lin(k, out_dim):
            k1, k2 = jax.random.split(k)
            W = jax.random.uniform(k1, (DIM, out_dim), minval=-s, maxval=s, dtype=jnp.float32)
            b = jax.random.uniform(k2, (out_dim,), minval=-s, maxval=s, dtype=jnp.float32)
            return (W, b)
        Wq, bq = lin(ks[0], NH * HEAD_DIM)
        Wk, bk = lin(ks[1], NH * HEAD_DIM)
        Wv, bv = lin(ks[2], NH * HEAD_DIM)
        Wbeta, bbeta = lin(ks[3], NH)
        Walpha, _ = lin(ks[4], NH)
        balpha = jnp.full((NH,), 2.0, dtype=jnp.float32)
        x = jax.random.normal(ks[5], (B, T, DIM), dtype=jnp.float32)
        return {'x': x, 'Wq': Wq, 'bq': bq, 'Wk': Wk, 'bk': bk, 'Wv': Wv, 'bv': bv, 'Wbeta': Wbeta, 'bbeta': bbeta, 'Walpha': Walpha, 'balpha': balpha}
    _L0_attn_in = _L0_attn_setup()

    def _L0_ffn_setup():
        import jax, jax.numpy as jnp
        import numpy as np
        TOP_K = 4
        key = jax.random.key(seed)
        ks = jax.random.split(key, 5)
        H, I, E = (256, 96, 32)
        s = 0.02
        return {'hidden_states': jax.random.normal(ks[0], (1, 128, H), jnp.float32), 'router_w': jax.random.normal(ks[1], (E, H), jnp.float32) * s, 'gate_w': jax.random.normal(ks[2], (E, I, H), jnp.float32) * s, 'up_w': jax.random.normal(ks[3], (E, I, H), jnp.float32) * s, 'down_w': jax.random.normal(ks[4], (E, H, I), jnp.float32) * s}
    _L0_ffn_in = _L0_ffn_setup()
    _L0_c = _w((lambda *s: np.random.randn(*s).astype(np.float32) * 0.05)(8, 256))
    _L0_wmod = _w((lambda *s: np.random.randn(*s).astype(np.float32) * 0.05)(256, 6 * 256) * 256 ** (-0.5))
    _d = {'L0_attn_x': _L0_attn_in['x'], 'L0_attn_Wq': _L0_attn_in['Wq'], 'L0_attn_bq': _L0_attn_in['bq'], 'L0_attn_Wk': _L0_attn_in['Wk'], 'L0_attn_bk': _L0_attn_in['bk'], 'L0_attn_Wv': _L0_attn_in['Wv'], 'L0_attn_bv': _L0_attn_in['bv'], 'L0_attn_Wbeta': _L0_attn_in['Wbeta'], 'L0_attn_bbeta': _L0_attn_in['bbeta'], 'L0_attn_Walpha': _L0_attn_in['Walpha'], 'L0_attn_balpha': _L0_attn_in['balpha'], 'L0_ffn_router_w': _L0_ffn_in['router_w'], 'L0_ffn_gate_w': _L0_ffn_in['gate_w'], 'L0_ffn_up_w': _L0_ffn_in['up_w'], 'L0_ffn_down_w': _L0_ffn_in['down_w'], 'L0_c': _L0_c, 'L0_wmod': _L0_wmod}
    _x0 = _d['L0_attn_x']
    _d['L0_attn_x'] = jax.random.normal(jax.random.fold_in(jax.random.key(seed), 1), (8, 512, 256), dtype=_x0.dtype)
    del _x0
    return _d

def reference(L0_attn_x, L0_attn_Wq, L0_attn_bq, L0_attn_Wk, L0_attn_bk, L0_attn_Wv, L0_attn_bv, L0_attn_Wbeta, L0_attn_bbeta, L0_attn_Walpha, L0_attn_balpha, L0_ffn_router_w, L0_ffn_gate_w, L0_ffn_up_w, L0_ffn_down_w, L0_c, L0_wmod):

    def _L0_attn_ref(x, Wq, bq, Wk, bk, Wv, bv, Wbeta, bbeta, Walpha, balpha):
        import jax, jax.numpy as jnp
        import numpy as np
        DIM = 256
        HEAD_DIM = 128
        NH = DIM // HEAD_DIM
        CHUNK = 128

        def _forward(x, Wq, bq, Wk, bk, Wv, bv, Wbeta, bbeta, Walpha, balpha):
            B, T, D = x.shape
            H, S, C = (NH, HEAD_DIM, CHUNK)
            q = (x @ Wq + bq).reshape(B, T, H, S)
            k = (x @ Wk + bk).reshape(B, T, H, S)
            v = (x @ Wv + bv).reshape(B, T, H, S)
            k = k / jnp.maximum(jnp.linalg.norm(k, axis=-1, keepdims=True), 1e-12)
            alpha_val = jax.nn.sigmoid(x @ Walpha + balpha).reshape(B, T, H, 1)
            beta = jax.nn.softplus(x @ Wbeta + bbeta).reshape(B, T, H, 1)
            pad = -T % C

            def padt(t):
                return jnp.pad(t, ((0, 0), (0, pad), (0, 0), (0, 0))) if pad else t
            qp, kp, vp = (padt(q), padt(k), padt(v))
            ap, bp = (padt(alpha_val), padt(beta))
            Tp = T + pad
            n = Tp // C

            def ch(t):
                return t.reshape(B, n, C, H, t.shape[-1]).transpose(0, 1, 3, 2, 4)
            qc, kc, vc, bc = (ch(qp), ch(kp), ch(vp), ch(bp))
            cla = jnp.cumsum(jnp.log(ch(ap) + 1e-06), axis=3)
            decay = jnp.exp(cla - jnp.swapaxes(cla, -1, -2))
            causal = jnp.tril(jnp.ones((C, C), dtype=bool))
            decay = jnp.where(causal, decay, 0.0)
            attn = jnp.einsum('bnhcd,bnhed->bnhce', qc, kc) * jnp.swapaxes(bc, -1, -2) * decay
            y_local = jnp.einsum('bnhce,bnhed->bnhcd', attn, vc)
            chunk_decay = jnp.exp(cla)
            cla_end = cla[:, :, :, -1:, :]
            total_decay = jnp.exp(cla_end)
            decay_to_end = jnp.exp(cla_end - cla)
            kw = kc * bc * decay_to_end
            delta = jnp.einsum('bnhcd,bnhce->bnhde', vc, kw)
            state0 = jnp.zeros((B, H, S, S), x.dtype)

            def step(state, inp):
                q_i, yloc_i, cd_i, td_i, d_i = inp
                y_glob = jnp.einsum('bhce,bhde->bhcd', q_i, state) * cd_i
                new_state = state * td_i + d_i
                return (new_state, y_glob + yloc_i)
            xs = (jnp.moveaxis(qc, 1, 0), jnp.moveaxis(y_local, 1, 0), jnp.moveaxis(chunk_decay, 1, 0), jnp.moveaxis(total_decay, 1, 0), jnp.moveaxis(delta, 1, 0))
            final_state, y_chunks = jax.lax.scan(step, state0, xs)
            y = jnp.moveaxis(y_chunks, 0, 1)
            y = y.transpose(0, 1, 3, 2, 4).reshape(B, Tp, D)[:, :T, :]
            surprise = jnp.linalg.norm(y_local, axis=-1).mean(axis=-1)
            surprise = surprise.reshape(B, -1, 1).mean(axis=1, keepdims=True)
            return (y, final_state, surprise, alpha_val)

        def _reference_tuple_inner(x, Wq, bq, Wk, bk, Wv, bv, Wbeta, bbeta, Walpha, balpha):
            return _forward(x, Wq, bq, Wk, bk, Wv, bv, Wbeta, bbeta, Walpha, balpha)
        return _reference_tuple_inner(x, Wq, bq, Wk, bk, Wv, bv, Wbeta, bbeta, Walpha, balpha)[0]

    def _L0_ffn_ref(hidden_states, router_w, gate_w, up_w, down_w):
        import jax, jax.numpy as jnp
        import numpy as np
        TOP_K = 4
        B, S, H = hidden_states.shape
        E = router_w.shape[0]
        x = hidden_states.reshape(-1, H)
        logits = x @ router_w.T
        probs = jax.nn.softmax(logits.astype(jnp.float32), axis=-1)
        rw, sel = jax.lax.top_k(probs, TOP_K)
        rw = rw / jnp.sum(rw, axis=-1, keepdims=True)
        rw = rw.astype(x.dtype)

        def body(acc, expert):
            gw, uw, dw, e = expert
            w_tok = jnp.sum(jnp.where(sel == e, rw, 0.0), axis=-1)
            h = jax.nn.silu(x @ gw.T) * (x @ uw.T)
            y = h @ dw.T
            return (acc + w_tok[:, None] * y, None)
        acc0 = jnp.zeros_like(x)
        out, _ = jax.lax.scan(body, acc0, (gate_w, up_w, down_w, jnp.arange(E)))
        return out.reshape(B, S, H)
    x = L0_attn_x
    mod = (_silu(L0_c) @ L0_wmod).reshape(L0_c.shape[0], 6, 1, -1)
    sa, ca, ga, sb, cb, gb = (mod[:, 0], mod[:, 1], mod[:, 2], mod[:, 3], mod[:, 4], mod[:, 5])
    ga = (2 * (ga >= 0) - 1) * jnp.maximum(jnp.abs(ga), 0.25)
    gb = (2 * (gb >= 0) - 1) * jnp.maximum(jnp.abs(gb), 0.25)
    h = _layernorm(x, axis=-1) * (1 + ca) + sa
    x = x + ga * _L0_attn_ref(h, L0_attn_Wq, L0_attn_bq, L0_attn_Wk, L0_attn_bk, L0_attn_Wv, L0_attn_bv, L0_attn_Wbeta, L0_attn_bbeta, L0_attn_Walpha, L0_attn_balpha)
    h = _layernorm(x, axis=-1) * (1 + cb) + sb
    x = x + gb * _L0_ffn_ref(h, L0_ffn_router_w, L0_ffn_gate_w, L0_ffn_up_w, L0_ffn_down_w)
    return x

_drawn_inputs = setup_inputs


def setup_inputs(seed=0):
    import zlib

    import numpy as np

    out = dict(_drawn_inputs(seed))
    spreads = {'L0_attn_balpha': (2.0, 0.6)}
    factors = {'L0_attn_bq': 6.516,
     'L0_attn_bk': 7.102,
     'L0_attn_bv': 6.384,
     'L0_attn_bbeta': 8.0,
     'L0_attn_Walpha': 3.146,
     'L0_ffn_router_w': 8.0,
     'L0_ffn_gate_w': 8.0,
     'L0_ffn_up_w': 8.0,
     'L0_ffn_down_w': 8.0}
    for name, (base, spread) in spreads.items():
        noise = np.random.default_rng([zlib.crc32(name.encode()), seed]).standard_normal(out[name].shape)
        drawn = base * np.exp(spread * noise) if base else spread * noise
        out[name] = jnp.asarray(drawn.astype(out[name].dtype))
    for name, factor in factors.items():
        out[name] = (out[name] * factor).astype(out[name].dtype)
    return out
```

```python
from contextlib import ExitStack

import concourse.bass as bass
from concourse import mybir

F32 = mybir.dt.float32
BF16 = mybir.dt.bfloat16
I32 = mybir.dt.int32
U32 = mybir.dt.uint32
ALU = mybir.AluOpType
ACT = mybir.ActivationFunctionType
AX = mybir.AxisListType.X

P = 128
TOP_K = 4
SLOTS = 8
TAIL = 4
NO_ROW = 1 << 20
MAGIC = float(0x5F3759DF)
LN_EPS = 1e-5
NORM_MIN_SQ = 1e-24
ALPHA_EPS = 1e-6


class Chain:

    def __init__(self, eng, sem, per):
        self.eng, self.sem, self.per = eng, sem, per

    def begin(self, round_):
        self.base, self.n = round_ * self.per, 0

    def done(self, ins):
        ins.then_inc(self.sem, 1)
        self.n += 1

    def reached(self):
        return self.sem, self.base + self.n

    def wait(self):
        self.eng.wait_ge(*self.reached())

    def then(self, ins):
        self.done(ins)
        self.wait()

    def end(self):
        assert self.n == self.per, (self.n, self.per)


def build(nc, x, wqk, wv, wab, bqk, bv, bab, cT, wmod, rw, gu, dw, out):
    NB, T, D = x.shape
    E = rw.shape[2]
    I = dw.shape[0]
    KT = D // P
    NC = T // P
    H = D // P
    NU = NC * H
    NT = NB * NC
    N = NB * T
    ROW = D + 2
    REGION = N + P
    TRASH = E * REGION
    NBLK = N * TOP_K // P + E
    NMOD = 5
    assert KT == 2 and H == 2 and NC == 4 and NB == 8 and E == 32 and NBLK % SLOTS == 0

    routed = nc.dram_tensor("routed_rows", [TRASH + P, ROW], F32).ap()
    weighted = nc.dram_tensor("weighted_rows", [N * TOP_K, D], F32).ap()
    mod_rows = nc.dram_tensor("mod_rows", [NB, NMOD * D], F32).ap()

    ctx = ExitStack()
    with ctx:
        def sb(name, shape, dt=F32, c=ctx):
            return c.enter_context(nc.sbuf_tensor(name, shape, dt))

        def sem(name):
            return ctx.enter_context(nc.semaphore(name))

        bank = [ctx.enter_context(nc.psum_tensor(f"bank{i}", [P, 512], F32)) for i in range(8)]

        x_all = sb("x_all", [P, NT, D])
        ident = sb("ident", [P, P])
        ones_be = sb("ones_be", [P, E])
        base = sb("base", [P, E])
        region0 = sb("region0", [P, E])
        iota_i = sb("iota_i", [P, E], I32)
        iota_e = sb("iota_e", [P, E])

        phase_a = ExitStack()

        def sa(name, shape, dt=F32):
            return sb(name, shape, dt, phase_a)

        wqk_sb = sa("wqk_sb", [P, KT, 4 * P])
        wv_sb = sa("wv_sb", [P, KT, D])
        wvb = sa("wvb", [P, 2, KT, D + 4])
        bqk_sb = sa("bqk_sb", [P, 4])
        bv8 = sa("bv8", [NB, D])
        bab_sb = sa("bab_sb", [P, 4])
        cT_sb = sa("cT_sb", [P, KT, NB])
        c_act = sa("c_act", [P, 2, KT, NB])
        rw_sb = sa("rw_sb", [P, KT, E])
        mod_b = sa("mod_b", [P, NB, 4 * D])
        mod8 = sa("mod8", [NB, NMOD, D])
        gate8 = sa("gate8", [NB, 2, 2, D])
        scaleT = sa("scaleT", [P, KT, NB])
        shiftT = sa("shiftT", [P, KT, NB])
        tri_incl = sa("tri_incl", [P, P])
        tri_strict = sa("tri_strict", [P, P], BF16)
        ones_bf = sa("ones_bf", [P, P], BF16)
        xn = sa("xn", [P, NC, D])
        hT = sa("hT", [P, KT, T])
        qT = sa("qT", [P, 2, H, T])
        kT = sa("kT", [P, 2, H, T])
        qsT = sa("qsT", [P, H, T])
        v_sb = sa("v_sb", [P, 2, NC, D])
        kw = sa("kw", [P, NC, D])
        decay = sa("decay", [P, NU, P])
        cdecay = sa("cdecay", [P, NU, P])
        junk = sa("junk", [P, NU, P])
        attnT = sa("attnT", [P, 2, H, P])
        state = sa("state", [P, H, P])
        rows = sa("rows", [P, 2, NC, TOP_K, ROW])
        h2T = sa("h2T", [P, KT, T])
        xn2 = sa("xn2", [P, NC, D])
        pad_rows = sa("pad_rows", [P, ROW])
        zt = sa("zt", [P, NC, 4])
        zz = sa("zz", [P, NC, 4])
        ez = sa("ez", [P, NC, 4])
        lnin = sa("lnin", [P, NC, 4])
        lnout = sa("lnout", [P, NC, 4])
        beta = sa("beta", [P, NC, H])
        ncla = sa("ncla", [P, NU])
        s_attn = sa("s_attn", [P, NU])
        s_kw = sa("s_kw", [P, NU])
        stats = sa("stats", [P, 2 * NC, 6])
        mv = sa("mv", [P, 2 * NC, 2])
        ksum = sa("ksum", [P, NU])
        NR = 2 * NC + NU
        rs_in = sa("rs_in", [P, NR])
        rs_y = sa("rs_y", [P, NR])
        rs_t = sa("rs_t", [P, NR])
        rs_h = sa("rs_h", [P, NR], I32)
        rs_f = sa("rs_f", [P, NR])
        logits = sa("logits", [P, NC, E])
        top8 = sa("top8", [P, NC, 8])
        idx8 = sa("idx8", [P, NC, 8], U32)
        idxf = sa("idxf", [P, NC, TOP_K])
        etop = sa("etop", [P, NC, TOP_K])
        esum = sa("esum", [P, NC])
        onehot = sa("onehot", [P, NC, TOP_K, E])
        picked = sa("picked", [P, NC, TOP_K, E])
        mask = sa("mask", [P, NC + 1, E], BF16)
        slot_e = sa("slot_e", [P, NC, E])
        slot_f = sa("slot_f", [P, NC, TOP_K])
        slot_u = sa("slot_u", [P, 2, NC * TOP_K], U32)
        ids = sa("ids", [P, NC, TOP_K], I32)

        wmod_sb = rows[:, :, :, :, :].rearrange("p a c k f -> p (a c k f)")[:, 0:KT * 6 * D]\
            .rearrange("p (k f) -> p k f", k=KT)

        attn_ready = sem("attn_ready")
        base_ready = sem("base_ready")
        bidx_ready = sem("bidx_ready")
        c_exp = sem("c_exp")
        c_silu = sem("c_silu")
        cdecay_done = sem("cdecay_done")
        cla_done = sem("cla_done")
        cols_ready = sem("cols_ready")
        constants = sem("constants")
        decay_done = sem("decay_done")
        dve_h2 = sem("dve_h2")
        dve_norms = sem("dve_norms")
        dve_pos = sem("dve_pos")
        dve_pre = sem("dve_pre")
        dve_scalars = sem("dve_scalars")
        dve_table = sem("dve_table")
        dve_top = sem("dve_top")
        etop_exp = sem("etop_exp")
        etop_ready = sem("etop_ready")
        ez_ready = sem("ez_ready")
        first_sum = sem("first_sum")
        gated = sem("gated")
        gu_done = sem("gu_done")
        h2T_done = sem("h2T_done")
        h2T_evac = sem("h2T_evac")
        h2_ready = sem("h2_ready")
        hT_ready = sem("hT_ready")
        hhT_done = sem("hhT_done")
        hhT_evac = sem("hhT_evac")
        hh_ready = sem("hh_ready")
        kTk_done = sem("kTk_done")
        ksum_ready = sem("ksum_ready")
        kw_done = sem("kw_done")
        la_ready = sem("la_ready")
        lnin_ready = sem("lnin_ready")
        loaded = sem("loaded")
        logits_done = sem("logits_done")
        logits_read = sem("logits_read")
        mask_ready = sem("mask_ready")
        masked = sem("masked")
        meta_read = sem("meta_read")
        mod_mm = sem("mod_mm")
        mod_spread = sem("mod_spread")
        mod_stored = sem("mod_stored")
        ncla_ready = sem("ncla_ready")
        out_ready = sem("out_ready")
        pad_made = sem("pad_made")
        pads_ready = sem("pads_ready")
        pads_stored = sem("pads_stored")
        pool_made = sem("pool_made")
        pos_done = sem("pos_done")
        qk_done = sem("qk_done")
        qk_evac = sem("qk_evac")
        qs_ready = sem("qs_ready")
        rows8_ready = sem("rows8_ready")
        rows_copied = sem("rows_copied")
        scores_done = sem("scores_done")
        second_sum = sem("second_sum")
        silu_done = sem("silu_done")
        skw_ready = sem("skw_ready")
        slots_ready = sem("slots_ready")
        state_ready = sem("state_ready")
        table_loaded = sem("table_loaded")
        table_ready = sem("table_ready")
        table_stored = sem("table_stored")
        v_done = sem("v_done")
        v_evac = sem("v_evac")
        weights_loaded = sem("weights_loaded")
        wvb_ready = sem("wvb_ready")
        x1_done = sem("x1_done")
        x_loaded = sem("x_loaded")
        xeT_done = sem("xeT_done")
        xeT_evac = sem("xeT_evac")
        xnT_done = sem("xnT_done")
        xn_ready = sem("xn_ready")
        y_done = sem("y_done")
        ye_done = sem("ye_done")
        ye_ready = sem("ye_ready")
        z_ready = sem("z_ready")
        scattered = [sem(f"scattered{i}") for i in range(2)]
        xe_loaded = [sem(f"xe_loaded{i}") for i in range(SLOTS)]
        y_stored = [sem(f"y_stored{i}") for i in range(SLOTS)]
        g_loaded = [sem(f"g_loaded{i}") for i in range(TAIL)]
        out_stored = [sem(f"out_stored{i}") for i in range(TAIL)]

        def steps(eng, body):
            for s in (0, 1):
                body(s, s // 2, s % 2, True, s >= 1, False)
            with eng.Fori(1, NB // 2) as j:
                for par in range(2):
                    body(2 * j + par, j, par, True, True, True)
            for s in (NB, NB + 1):
                body(s, s // 2, s % 2, False, s == NB, True)

        def wait(eng, sem_, value):
            if not (isinstance(value, int) and value <= 0):
                eng.wait_ge(sem_, value)

        def wait_apart(eng, reached, *waits):
            waits = [(sem_, value if isinstance(value, int) else eng.to_reg(value)) for sem_, value in waits]
            eng.wait_ge(*reached)
            for sem_, value in waits:
                wait(eng, sem_, value)

        def unit(u):
            return slice((u % 4) * P, (u % 4 + 1) * P)

        with nc.Block() as block:

            @block.sync
            def _(sp):
                sp.dma_start(cT_sb[:, :, :], cT).then_inc(loaded, 16)
                sp.dma_start(wmod_sb, wmod).then_inc(loaded, 16)
                sp.dma_start(bv8[:, :], bv.broadcast_to([NB, D])).then_inc(loaded, 16)
                sp.dma_start(x_all[:, 0:NC, :], x[0].rearrange("(c p) f -> p c f", p=P)).then_inc(x_loaded, 16)
                sp.dma_start(wqk_sb[:, :, :], wqk).then_inc(loaded, 16)
                sp.dma_start(wv_sb[:, :, :], wv).then_inc(loaded, 16)
                for par in range(2):
                    sp.dma_start(wvb[:, par, :, D:D + 4], wab).then_inc(loaded, 16)
                sp.dma_start(bqk_sb[:, :], bqk).then_inc(loaded, 16)
                sp.dma_start(bab_sb[:, :], bab.broadcast_to([P, 4])).then_inc(loaded, 16)
                sp.dma_start(rw_sb[:, :, :], rw).then_inc(loaded, 16)
                sp.wait_ge(x_loaded, 16)
                sp.dma_start(x_all[:, NC:2 * NC, :], x[1].rearrange("(c p) f -> p c f", p=P)).then_inc(x_loaded, 16)
                sp.wait_ge(rows8_ready, 1)
                sp.dma_start(mod_rows, mod8[:, :, :].rearrange("p a b -> p (a b)")).then_inc(mod_stored, 16)
                sp.wait_ge(mod_stored, 16)
                sp.dma_start(mod_b[:, :, :], mod_rows[:, 0:4 * D].partition_broadcast(P)).then_inc(mod_spread, 16)
                for b in range(2, NB):
                    sp.wait_ge(x_loaded, 16 * b)
                    sp.dma_start(x_all[:, b * NC:(b + 1) * NC, :],
                                 x[b].rearrange("(c p) f -> p c f", p=P)).then_inc(x_loaded, 16)

            @block.gpsimd
            def _(pool):
                for t, v in ((ident, 0.0), (tri_incl, 1.0), (tri_strict, 1.0), (ones_bf, 1.0)):
                    pool.memset(t[:, :], v).then_inc(pool_made, 1)
                pool.memset(pad_rows[:, :], 0.0).then_inc(pads_ready, 1)
                pool.wait_ge(pool_made, 4)
                for t, op, fill, cm, st in ((ident, ALU.not_equal, 1.0, 1, -1), (tri_incl, ALU.is_ge, 0.0, -1, 1),
                                            (tri_strict, ALU.is_gt, 0.0, -1, 1)):
                    pool.affine_select(out=t[:, :], in_=t[:, :], compare_op=op, fill=fill, base=0,
                                       pattern=[[st, P]], channel_multiplier=cm).then_inc(pool_made, 1)
                pool.iota(iota_i[:, :], pattern=[[1, E]], base=0, channel_multiplier=0).then_inc(pool_made, 1)
                pool.iota(ids[:, :, :], pattern=[[P * TOP_K, NC], [1, TOP_K]], base=0,
                          channel_multiplier=TOP_K).then_inc(pool_made, 1)
                pool.wait_ge(pads_ready, 1)
                pool.iota(pad_rows[:, D + 1:D + 2].bitcast(I32), pattern=[[0, 1]], base=NO_ROW,
                          channel_multiplier=0).then_inc(pads_ready, 1)
                pool.wait_ge(pool_made, 9)
                pool.tensor_copy(iota_e[:, :], iota_i[:, :]).then_inc(constants, 1)

                pool.wait_ge(pads_ready, 2)
                for par in range(2):
                    half = slice(par * P // 2, (par + 1) * P // 2)
                    pool.dma_start(routed[TRASH:TRASH + P, :][half], pad_rows[half, :]).then_inc(scattered[par], 16)

                def step(s, j, par, f, a, r):
                    if f:
                        wait_apart(pool, (pool_made, 9), (decay_done, s + 1))
                        pool.affine_select(out=decay[:, :, :], in_=decay[:, :, :], compare_op=ALU.is_ge, fill=0.0,
                                           base=0, pattern=[[0, NU], [1, P]], channel_multiplier=-1)\
                            .then_inc(masked, 1)
                    if r:
                        wait_apart(pool, (pool_made, 9), (slots_ready, s - 1), (rows_copied, s - 1))
                        for c in range(NC):
                            for k in range(TOP_K):
                                u = c * TOP_K + k
                                pool.indirect_dma_start(
                                    out=routed, out_offset=bass.IndirectOffsetOnAxis(ap=slot_u[:, par, u:u + 1], axis=0),
                                    in_=rows[:, par, c, k, :], in_offset=None).then_inc(scattered[par], 16)
                steps(pool, step)
                for par in range(2):
                    pool.wait_ge(scattered[par], 16 + 16 * NC * TOP_K * NB // 2)

            @block.scalar
            def _(act):
                act.wait_ge(loaded, 16 * 10)
                act.activation(c_act[:, 0, :, :], cT_sb[:, :, :], ACT.Exp, scale=-1.0).then_inc(c_exp, 1)

                def step(s, j, par, f, a, r):
                    if f:
                        act.wait_ge(xnT_done, s + 1)
                        act.wait_ge(cols_ready, 2)
                        for kt in range(KT):
                            ins = act.activation(hT[:, kt, :], bank[kt][:, :], ACT.Identity,
                                                 scale=scaleT[:, kt, bass.ds(s, 1)], bias=shiftT[:, kt, bass.ds(s, 1)])
                        ins.then_inc(hT_ready, 1)
                    if r:
                        act.wait_ge(h2T_done, s - 1)
                        for kt in range(KT):
                            ins = act.activation(h2T[:, kt, :], bank[2 + kt][:, :], ACT.Copy)
                        ins.then_inc(h2T_evac, 1)
                    if f:
                        for g in range(4):
                            act.wait_ge(qk_done, 4 * s + g + 1)
                            dst = (qT if g < H else kT)[:, par, g % H, :]
                            act.activation(dst, bank[2 + g % 2][:, :], ACT.Identity, bias=bqk_sb[:, g:g + 1])\
                                .then_inc(qk_evac, 1)
                    if r:
                        act.wait_ge(etop_ready, s - 1)
                        act.activation(etop[:, :, :], etop[:, :, :], ACT.Exp).then_inc(etop_exp, 1)
                        for c in range(NC):
                            ins = act.activation(rows[:, par, c, 1:TOP_K, 0:D],
                                                 rows[:, par, c, 0:1, 0:D].broadcast_to([P, TOP_K - 1, D]), ACT.Copy)
                        ins.then_inc(rows_copied, 1)
                    if f:
                        act.wait_ge(z_ready, s + 1)
                        act.activation(ez[:, :, :], zz[:, :, :], ACT.Exp, scale=-1.0).then_inc(ez_ready, 1)
                        act.wait_ge(lnin_ready, s + 1)
                        act.activation(lnout[:, :, :], lnin[:, :, :], ACT.Ln).then_inc(la_ready, 1)
                        act.wait_ge(kTk_done, s + 1)
                        wait(act, ksum_ready, s)
                        for u in range(NU):
                            ins = act.activation(junk[:, u, :], bank[2 + u // 4][:, unit(u)],
                                                 ACT.Square, accum_out=ksum[:, u:u + 1])
                        ins.then_inc(ksum_ready, 1)
                        act.wait_ge(cla_done, s + 1)
                        wait(act, x1_done, NC * s)
                        act.wait_ge(ncla_ready, s + 1)
                        for u in range(NU):
                            ins = act.activation(decay[:, u, :], bank[u // 4][:, unit(u)], ACT.Exp, bias=ncla[:, u:u + 1])
                        ins.then_inc(decay_done, 1)
                        for q in range(2):
                            ins = act.activation(cdecay[:, 4 * q:4 * q + 4, :].rearrange("p a b -> p (a b)"),
                                                 bank[q][:, :], ACT.Exp)
                        ins.then_inc(cdecay_done, 1)
                        act.wait_ge(skw_ready, s + 1)
                        for u in range(NU):
                            ins = act.activation(kw[:, u // H, (u % H) * P:(u % H + 1) * P],
                                                 bank[2 + u // 4][:, unit(u)], ACT.Copy, scale=s_kw[:, u:u + 1])
                        ins.then_inc(kw_done, 1)
                steps(act, step)

            @block.tensor
            def _(pe):
                pe.wait_ge(constants, 1)
                pe.wait_ge(c_silu, 3)
                for i in range(3):
                    for kt in range(KT):
                        pe.matmul(bank[i][0:NB, :], c_act[:, 1, kt, :], wmod_sb[:, kt, i * 512:(i + 1) * 512],
                                  start=kt == 0, stop=kt == KT - 1)
                for i in range(4):
                    for kt in range(KT):
                        ins = pe.matmul(bank[3][:, i * NB:(i + 1) * NB], wmod_sb[:, kt, i * P:(i + 1) * P],
                                        c_act[:, 1, kt, :], start=kt == 0, stop=kt == KT - 1)
                ins.then_inc(mod_mm, 1)
                pe.wait_ge(rows8_ready, 1)
                pe.wait_ge(cols_ready, 2)

                def step(s, j, par, f, a, r):
                    if f:
                        pe.wait_ge(xn_ready, s + 1)
                        wait(pe, cdecay_done, s)
                        for kt in range(KT):
                            for c in range(NC):
                                ins = pe.transpose(bank[kt][:, c * P:(c + 1) * P], xn[:, c, kt * P:(kt + 1) * P], ident[:, :])
                        ins.then_inc(xnT_done, 1)
                    if r:
                        pe.wait_ge(h2_ready, s - 1)
                        pe.wait_ge(kw_done, s if f else NB)
                        for kt in range(KT):
                            for c in range(NC):
                                ins = pe.transpose(bank[2 + kt][:, c * P:(c + 1) * P],
                                                   rows[:, par, c, 0, kt * P:(kt + 1) * P], ident[:, :])
                        ins.then_inc(h2T_done, 1)
                    for c in range(NC):
                        t = NC * (s - 1) + c
                        if a:
                            wait(pe, attn_ready, t)
                            if c == 0:
                                pe.wait_ge(qk_evac, 4 * s)
                                pe.wait_ge(ncla_ready, s)
                            for h in range(H):
                                ins = pe.matmul(bank[6][:, (c % 2) * D + h * P:(c % 2) * D + (h + 1) * P],
                                                kT[:, 1 - par, h, c * P:(c + 1) * P],
                                                qT[:, 1 - par, h, c * P:(c + 1) * P], start=True, stop=True)
                            ins.then_inc(scores_done, 1)
                        if f:
                            if c == 0:
                                pe.wait_ge(hT_ready, s + 1)
                                if r:
                                    pe.wait_ge(h2T_evac, s - 1)
                                else:
                                    wait(pe, kw_done, s)
                            if c >= 2:
                                pe.wait_ge(qk_evac, 4 * s + c - 1)
                            for kt in range(KT):
                                ins = pe.matmul(bank[2 + c % 2][:, :], wqk_sb[:, kt, c * P:(c + 1) * P], hT[:, kt, :],
                                                start=kt == 0, stop=kt == KT - 1)
                            ins.then_inc(qk_done, 1)
                        if r and c == 0:
                            pe.wait_ge(h2T_evac, s - 1)
                            pe.wait_ge(base_ready, s - 1)
                            for i in range(NC):
                                for kt in range(KT):
                                    ins = pe.matmul(bank[4][:, i * E:(i + 1) * E],
                                                    h2T[:, kt, i * P:(i + 1) * P], rw_sb[:, kt, :],
                                                    start=kt == 0, stop=kt == KT - 1)
                            ins.then_inc(logits_done, 1)
                        if a:
                            y = bank[5 if c % 2 else 7]
                            pe.wait_ge(attn_ready, t + 1)
                            wait(pe, x1_done, t - 1)
                            if c == 0:
                                pe.wait_ge(v_evac, NC * s)
                                pe.wait_ge(kw_done, s)
                            if c == 1:
                                pe.wait_ge(qs_ready, s)
                            if c > 0:
                                pe.wait_ge(state_ready, (NC - 1) * (s - 1) + c)
                            for h in range(H):
                                hs = slice(h * P, (h + 1) * P)
                                ins = pe.matmul(y[:, hs], attnT[:, c % 2, h, :], v_sb[:, 1 - par, c, hs],
                                                start=True, stop=c == 0)
                                if c > 0:
                                    ins = pe.matmul(y[:, hs], qsT[:, h, c * P:(c + 1) * P], state[:, h, :],
                                                    start=False, stop=True)
                            if c < NC - 1:
                                for h in range(H):
                                    hs = slice(h * P, (h + 1) * P)
                                    ins = pe.matmul(y[:, D + h * P:D + (h + 1) * P], kw[:, c, hs],
                                                    v_sb[:, 1 - par, c, hs], start=True, stop=True)
                            ins.then_inc(y_done, 1)
                        if f:
                            if c == 0:
                                pe.wait_ge(wvb_ready, s + 1)
                                if r:
                                    pe.wait_ge(logits_read, s - 1)
                            wait(pe, v_evac, NC * s + c)
                            for kt in range(KT):
                                ins = pe.matmul(bank[4][:, 0:D + 4], hT[:, kt, c * P:(c + 1) * P], wvb[:, par, kt, :],
                                                start=kt == 0, stop=kt == KT - 1)
                            ins.then_inc(v_done, 1)
                    if f:
                        pe.wait_ge(qk_evac, 4 * s + 4)
                        for u in range(NU):
                            c, h = u // H, u % H
                            ins = pe.transpose(bank[2 + u // 4][:, unit(u)], kT[:, par, h, c * P:(c + 1) * P], ident[:, :])
                        ins.then_inc(kTk_done, 1)
                        pe.wait_ge(la_ready, s + 1)
                        wait(pe, attn_ready, NC * s)
                        pe.matmul(bank[6][:, 0:NU].rearrange("p (a b) -> p a b", b=H), tri_incl[:, :],
                                  lnout[:, :, 0:H], start=True, stop=True)
                        for u in range(NU):
                            ins = pe.matmul(bank[u // 4][:, unit(u)],
                                            lnout[:, u // H, u % H:u % H + 1].broadcast_to([P, P]), tri_incl[:, :],
                                            start=True, stop=True)
                        ins.then_inc(cla_done, 1)
                    if r:
                        pe.wait_ge(mask_ready, s - 1)
                        pe.wait_ge(v_evac, NC * (s + 1) if f else NC * NB)
                        pe.wait_ge(logits_read, s - 1)
                        pos = bank[4][:, 0:(NC + 1) * E].rearrange("p (a b) -> p a b", b=E)
                        pe.matmul(pos, tri_strict[:, :], mask[:, :, :], start=True, stop=False)
                        for i in range(NC):
                            ins = pe.matmul(pos[:, i + 1:, :], ones_bf[:, :],
                                            mask[:, i:i + 1, :].broadcast_to([P, NC - i, E]),
                                            start=False, stop=i == NC - 1)
                        ins.then_inc(pos_done, 1)
                steps(pe, step)

            @block.vector
            def _(dve):
                tail_chain = Chain(dve, dve_norms, 4 * NC + 13)
                pre = Chain(dve, dve_pre, 10)
                zc = Chain(dve, dve_scalars, 5)
                h2c = Chain(dve, dve_h2, NC + 1)
                topc = Chain(dve, dve_top, 2 * NC + 2)
                posc = Chain(dve, dve_pos, 8)

                def rsqrt():
                    ch = tail_chain
                    ch.then(dve.tensor_scalar(rs_h[:, :], rs_in[:, :].bitcast(I32), 1, None, ALU.logical_shift_right))
                    ch.then(dve.tensor_scalar(rs_y[:, :].bitcast(I32), rs_h[:, :], -1.0, MAGIC, ALU.mult, ALU.add))
                    for _i in range(3):
                        ch.then(dve.scalar_tensor_tensor(out=rs_t[:, :], in0=rs_y[:, :], scalar=-0.5, in1=rs_y[:, :],
                                                         op0=ALU.mult, op1=ALU.mult))
                        ch.then(dve.tensor_tensor(rs_t[:, :], rs_t[:, :], rs_in[:, :], ALU.mult))
                        ch.then(dve.scalar_tensor_tensor(out=rs_y[:, :], in0=rs_t[:, :], scalar=1.5, in1=rs_y[:, :],
                                                         op0=ALU.add, op1=ALU.mult))

                def norms(s, before, after, keys):
                    ch = tail_chain
                    ch.begin(s + 1)
                    for use, at, t0 in ((before, 0, NC * ((s + 1) % NB)), (after, NC, NC * (s - 1))):
                        for c in range(NC):
                            tile = x_all[:, bass.ds(t0 + c, 1), :] if use else x_all[:, c:c + 1, :]
                            ch.done(dve.bn_stats(stats[:, at + c, :], tile.rearrange("p a f -> p (a f)")))
                    wait_apart(dve, (constants, 1), ch.reached())
                    for i in range(2 * NC):
                        ch.done(dve.bn_aggr(mv[:, i, :], stats[:, i, :]))
                    ch.wait()
                    ch.done(dve.tensor_scalar(rs_in[:, 0:2 * NC], mv[:, :, 1], LN_EPS, None, ALU.add))
                    if keys:
                        dve.wait_ge(ksum_ready, s + 1)
                        ch.done(dve.tensor_scalar(rs_in[:, 2 * NC:NR], ksum[:, :], NORM_MIN_SQ, None, ALU.max))
                    else:
                        ch.done(dve.memset(rs_in[:, 2 * NC:NR], 1.0))
                    ch.wait()
                    rsqrt()
                    ch.end()

                def normalise_input(b, at):
                    wait(dve, xnT_done, b)
                    for c in range(NC):
                        ins = dve.tensor_scalar(xn[:, c:c + 1, :], x_all[:, bass.ds(NC * at + c, 1), :],
                                                mv[:, c, 0:1], rs_y[:, c:c + 1], ALU.subtract, ALU.mult)
                    ins.then_inc(xn_ready, 1)

                dve.wait_ge(c_exp, 1)
                dve.tensor_scalar(c_act[:, 0, :, :], c_act[:, 0, :, :], 1.0, None, ALU.add).then_inc(c_silu, 1)
                dve.wait_ge(c_silu, 1)
                dve.reciprocal(c_act[:, 1, :, :], c_act[:, 0, :, :]).then_inc(c_silu, 1)
                dve.wait_ge(c_silu, 2)
                dve.tensor_tensor(c_act[:, 1, :, :], c_act[:, 1, :, :], cT_sb[:, :, :], ALU.mult).then_inc(c_silu, 1)
                dve.memset(mask[:, NC, :], 0.0).then_inc(c_silu, 1)
                dve.wait_ge(constants, 1)
                pre.begin(0)
                pre.done(dve.tensor_scalar(region0[:, :], iota_e[:, :], float(REGION), None, ALU.mult))
                dve.tensor_scalar(base[:, :], iota_e[:, :], float(REGION), None, ALU.mult).then_inc(base_ready, 1)
                dve.wait_ge(mod_mm, 1)
                cols = bank[3][:, 0:4 * NB].rearrange("p (i k b) -> p i k b", i=2, b=NB)
                dve.tensor_copy(shiftT[:, :, :], cols[:, 0, :, :]).then_inc(cols_ready, 1)
                dve.tensor_scalar(scaleT[:, :, :], cols[:, 1, :, :], 1.0, None, ALU.add).then_inc(cols_ready, 1)
                for i, (g, at) in enumerate(((bank[1][0:NB, 0:D], 0), (bank[2][0:NB, D:2 * D], 4))):
                    pre.then(dve.tensor_scalar(gate8[:, i, 0, :], g, -1.0, None, ALU.mult))
                    pre.done(dve.scalar_tensor_tensor(out=gate8[:, i, 0, :], in0=g, scalar=0.25, in1=gate8[:, i, 0, :],
                                                      op0=ALU.max, op1=ALU.max))
                    pre.then(dve.tensor_scalar(gate8[:, i, 1, :], g, 0.0, 2.0, ALU.is_ge, ALU.mult))
                    pre.then(dve.scalar_tensor_tensor(out=mod8[:, at, :], in0=gate8[:, i, 1, :], scalar=-1.0,
                                                      in1=gate8[:, i, 0, :], op0=ALU.add, op1=ALU.mult))
                pre.done(dve.tensor_tensor(mod8[:, 1, :], mod8[:, 0, :], bv8[:, :], ALU.mult))
                pre.done(dve.tensor_scalar(mod8[:, 2, :], bank[2][0:NB, 0:D], 1.0, None, ALU.add))
                pre.wait()
                dve.tensor_copy(mod8[:, 3, :], bank[1][0:NB, D:2 * D]).then_inc(rows8_ready, 1)
                dve.wait_ge(x_loaded, 16)
                norms(-1, True, False, False)
                normalise_input(0, 0)

                def step(s, j, par, f, a, r):
                    if f:
                        dve.wait_ge(mod_spread, 16)
                        wait(dve, v_done, NC * (s - 1))
                        dve.tensor_tensor(wvb[:, par, :, 0:D], wv_sb[:, :, :],
                                          mod_b[:, bass.ds(s, 1), 0:D].broadcast_to([P, KT, D]), ALU.mult)\
                            .then_inc(wvb_ready, 1)
                        zc.begin(s)
                    for c in range(NC):
                        t = NC * (s - 1) + c
                        if a:
                            dve.wait_ge(scores_done, t + 1)
                            if c == 0:
                                dve.wait_ge(masked, s)
                                dve.wait_ge(skw_ready, s)
                            wait(dve, y_done, t - 1)
                            for h in range(H):
                                u = c * H + h
                                ins = dve.scalar_tensor_tensor(
                                    out=attnT[:, c % 2, h, :], in0=bank[6][:, (c % 2) * D + h * P:(c % 2) * D + (h + 1) * P],
                                    scalar=s_attn[:, u:u + 1], in1=decay[:, u, :], op0=ALU.mult, op1=ALU.mult)
                            ins.then_inc(attn_ready, 1)
                        if r and c == 0:
                            dve.wait_ge(logits_done, s - 1)
                            dve.tensor_copy(logits[:, :, :].rearrange("p a b -> p (a b)"), bank[4][:, 0:NC * E])\
                                .then_inc(logits_read, 1)
                        if f:
                            dve.wait_ge(v_done, NC * s + c + 1)
                            dve.tensor_tensor(v_sb[:, par, c:c + 1, :], bank[4][:, 0:D].rearrange("p (a f) -> p a f", a=1),
                                              mod_b[:, bass.ds(s, 1), D:2 * D], ALU.add)
                            dve.tensor_tensor(zt[:, c, :], bank[4][:, D:D + 4], bab_sb[:, :], ALU.add)\
                                .then_inc(v_evac, 1)
                        if a:
                            y = bank[5 if c % 2 else 7]
                            dve.wait_ge(y_done, t + 1)
                            if c < NC - 1:
                                wait(dve, state_ready, (NC - 1) * (s - 1) + c)
                                for h in range(H):
                                    u = c * H + h
                                    delta = y[:, D + h * P:D + (h + 1) * P]
                                    if c == 0:
                                        ins = dve.tensor_copy(state[:, h, :], delta)
                                    else:
                                        ins = dve.scalar_tensor_tensor(
                                            out=state[:, h, :], in0=state[:, h, :], scalar=cdecay[:, u, P - 1:P],
                                            in1=delta, op0=ALU.mult, op1=ALU.add)
                                ins.then_inc(state_ready, 1)
                            xt = x_all[:, bass.ds(t, 1), :]
                            dve.tensor_tensor(xt, y[:, 0:D].rearrange("p (a f) -> p a f", a=1), xt, ALU.add)\
                                .then_inc(x1_done, 1)
                    if f:
                        dve.wait_ge(v_evac, NC * (s + 1))
                        zc.done(dve.tensor_copy(zz[:, :, 0:H], zt[:, :, 0:H]))
                        dve.scalar_tensor_tensor(out=zz[:, :, H:4], in0=zt[:, :, H:4], scalar=-1.0, in1=zt[:, :, H:4],
                                                 op0=ALU.mult, op1=ALU.max).then_inc(z_ready, 1)
                    if r:
                        top_experts(s, par)
                    if f:
                        dve.wait_ge(ez_ready, s + 1)
                        zc.then(dve.tensor_scalar(lnin[:, :, :], ez[:, :, :], 1.0, None, ALU.add))
                        zc.then(dve.reciprocal(lnin[:, :, 0:H], lnin[:, :, 0:H]))
                        dve.tensor_scalar(lnin[:, :, 0:H], lnin[:, :, 0:H], ALPHA_EPS, None, ALU.add)\
                            .then_inc(lnin_ready, 1)
                        dve.wait_ge(la_ready, s + 1)
                        zc.done(dve.scalar_tensor_tensor(out=beta[:, :, :], in0=zt[:, :, H:4], scalar=0.0,
                                                         in1=lnout[:, :, H:4], op0=ALU.max, op1=ALU.add))
                        dve.wait_ge(cla_done, s + 1)
                        dve.tensor_scalar(ncla[:, :], bank[6][:, 0:NU], -1.0, None, ALU.mult).then_inc(ncla_ready, 1)
                    if f or a:
                        if f:
                            dve.wait_ge(x_loaded, 16 * ((s + 1) % NB) + 16)
                        if a:
                            dve.wait_ge(x1_done, NC * s)
                        norms(s, f, a, f)
                    if f:
                        zc.done(dve.tensor_tensor(s_attn[:, :], beta[:, :, :].rearrange("p a b -> p (a b)"),
                                                  rs_y[:, 2 * NC:NR], ALU.mult))
                        zc.wait()
                        dve.wait_ge(masked, s + 1)
                        dve.tensor_tensor(s_kw[:, :], s_attn[:, :], decay[:, :, P - 1], ALU.mult).then_inc(skw_ready, 1)
                        zc.end()
                        dve.wait_ge(cdecay_done, s + 1)
                        dve.tensor_tensor(
                            qsT[:, :, P:T].rearrange("p h (c t) -> p h c t", t=P),
                            qT[:, par, :, P:T].rearrange("p h (c t) -> p h c t", t=P),
                            cdecay[:, H:NU, :].rearrange("p (c h) t -> p h c t", h=H), ALU.mult).then_inc(qs_ready, 1)
                    if f:
                        normalise_input(s + 1, (s + 1) % NB)
                    if a:
                        h2c.begin(s - 1)
                        wait(dve, h2_ready, s - 1)
                        for c in range(NC):
                            h2c.done(dve.tensor_scalar(xn2[:, c:c + 1, :], x_all[:, bass.ds(NC * (s - 1) + c, 1), :],
                                                       mv[:, NC + c, 0:1], rs_y[:, NC + c:NC + c + 1],
                                                       ALU.subtract, ALU.mult))
                        h2c.wait()
                        h2c.then(dve.tensor_tensor(xn2[:, :, :], xn2[:, :, :],
                                                   mod_b[:, bass.ds(s - 1, 1), 2 * D:3 * D].broadcast_to([P, NC, D]),
                                                   ALU.mult))
                        dve.wait_ge(scattered[1 - par], 16 + 16 * NC * TOP_K * (j if par else j - 1))
                        dve.tensor_tensor(rows[:, 1 - par, :, 0, 0:D], xn2[:, :, :],
                                          mod_b[:, bass.ds(s - 1, 1), 3 * D:4 * D].broadcast_to([P, NC, D]),
                                          ALU.add).then_inc(h2_ready, 1)
                        h2c.end()
                    if r:
                        places(s, par)

                def top_experts(s, par):
                    ch = topc
                    ch.begin(s - 2)
                    wait_apart(dve, (constants, 1), (logits_read, s - 1))
                    for c in range(NC):
                        ch.done(dve.max(top8[:, c, :], logits[:, c, :]))
                    wait_apart(dve, (constants, 1), ch.reached())
                    for c in range(NC):
                        ch.done(dve.max_index(idx8[:, c, :], top8[:, c, :], logits[:, c, :]))
                    dve.tensor_tensor(etop[:, :, :], top8[:, :, 0:TOP_K],
                                      top8[:, :, 0:1].broadcast_to([P, NC, TOP_K]), ALU.subtract).then_inc(etop_ready, 1)
                    ch.wait()
                    ch.then(dve.tensor_copy(idxf[:, :, :], idx8[:, :, 0:TOP_K]))
                    ch.then(dve.tensor_tensor(
                        onehot[:, :, :, :].rearrange("p c k e -> p (c k) e"),
                        iota_e[:, :].unsqueeze(1).broadcast_to([P, NC * TOP_K, E]),
                        idxf[:, :, :].rearrange("p c k -> p (c k)").unsqueeze(2).broadcast_to([P, NC * TOP_K, E]),
                        ALU.is_equal))
                    dve.tensor_reduce(mask[:, 0:NC, :], onehot[:, :, :, :].rearrange("p c k e -> p c e k"), AX, ALU.max)\
                        .then_inc(mask_ready, 1)
                    ch.end()

                def places(s, par):
                    ch = posc
                    ch.begin(s - 2)
                    dve.wait_ge(etop_exp, s - 1)
                    ch.then(dve.tensor_reduce(esum[:, :], etop[:, :, :], AX, ALU.add))
                    ch.then(dve.reciprocal(esum[:, :], esum[:, :]))
                    ch.done(dve.tensor_tensor(rows[:, par, :, :, D], etop[:, :, :],
                                              esum[:, :].unsqueeze(2).broadcast_to([P, NC, TOP_K]), ALU.mult))
                    ch.then(dve.tensor_copy(rows[:, par, :, :, D + 1:D + 2].rearrange("p c k o -> p (c k o)").bitcast(I32),
                                            ids[:, :, :].rearrange("p c k -> p (c k)")))
                    ch.done(dve.tensor_scalar(ids[:, :, :], ids[:, :, :], float(T * TOP_K), None, ALU.add))
                    dve.wait_ge(pos_done, s - 1)
                    dve.wait_ge(base_ready, s - 1)
                    ch.then(dve.tensor_tensor(slot_e[:, :, :], bank[4][:, 0:NC * E].rearrange("p (a b) -> p a b", b=E),
                                              base[:, :].unsqueeze(1).broadcast_to([P, NC, E]), ALU.add))
                    dve.tensor_tensor(base[:, :], bank[4][:, NC * E:(NC + 1) * E], base[:, :], ALU.add)\
                        .then_inc(base_ready, 1)
                    ch.then(dve.tensor_tensor(picked[:, :, :, :], onehot[:, :, :, :],
                                              slot_e[:, :, :].unsqueeze(2).broadcast_to([P, NC, TOP_K, E]), ALU.mult))
                    ch.then(dve.tensor_reduce(slot_f[:, :, :], picked[:, :, :, :], AX, ALU.add))
                    dve.tensor_copy(slot_u[:, par, :], slot_f[:, :, :].rearrange("p c k -> p (c k)"))\
                        .then_inc(slots_ready, 1)
                    ch.end()

                steps(dve, step)
        phase_a.close()

        phase_b = ExitStack()

        def se(name, shape, dt=F32):
            return sb(name, shape, dt, phase_b)

        gu_sb = se("gu_sb", [P, E, KT * 2 * I])
        dw_sb = se("dw_sb", [I, E, D])
        gb_sb = se("gb_sb", [P, NB, D])
        pad_block = se("pad_block", [P, ROW])
        counts = se("counts", [P, E])
        counts_i = se("counts_i", [P, E], I32)
        blocks_i = se("blocks_i", [P, E], I32)
        blocks = se("blocks", [P, E])
        ones_f = se("ones_f", [P, E])
        ends = se("ends", [P, E])
        NG = -(-NBLK // P)
        bidx_i = se("bidx_i", [P, NG], I32)
        bidx = se("bidx", [P, NG])
        passed = se("passed", [P, NG, E])
        starts = se("starts", [P, NG, E])
        expert = se("expert", [P, NG])
        first = se("first", [P, NG])
        table = se("table", [P, 2, NG])
        table_i = se("table_i", [P, 2, NG], I32)
        table_row = se("table_row", [1, 2, NG, P], I32)
        free_row = se("free_row", [1, E], I32)
        xe = se("xe", [P, SLOTS, ROW])
        meta = se("meta", [P, SLOTS, 2])
        xeT = se("xeT", [P, 2, KT, P])
        gate = se("gate", [P, 2, I])
        hh = se("hh", [P, 2, I])
        hhT = se("hhT", [I, 2, P])
        ye = se("ye", [P, SLOTS, D])
        yk = se("yk", [P, TAIL, TOP_K * D])
        ysum = se("ysum", [P, TAIL, 2 * D])
        ysum2 = se("ysum2", [P, TAIL, D])
        res = se("res", [P, TAIL, D])
        table_dram = nc.dram_tensor("table_dram", [2 * NG, P], I32).ap()

        def block_steps(eng, body):
            for i in range(SLOTS):
                body(i, 0, i)
            with eng.Fori(1, NBLK // SLOTS) as j:
                for q in range(SLOTS):
                    body(SLOTS * j + q, j, q)
            for q in range(3):
                body(NBLK + q, NBLK // SLOTS, q)

        def table_entry(which, i):
            flat = table_row[:, :, :, :].rearrange("o a g p -> o (a g p)")
            return flat[0:1, bass.ds(i + which * NG * P, 1)]

        def has(i, lag):
            return not isinstance(i, int) or 0 <= i - lag < NBLK

        with nc.Block() as block:

            @block.sync
            def _(sp):
                sp.dma_start(gu_sb[:, :, :], gu).then_inc(weights_loaded, 16)
                sp.dma_start(dw_sb[:, :, :], dw).then_inc(weights_loaded, 16)
                sp.dma_start(gb_sb[:, :, :], mod_rows[:, 4 * D:5 * D].partition_broadcast(P)).then_inc(weights_loaded, 16)
                sp.wait_ge(table_ready, 2)
                with nc.allow_non_contiguous_dma(reason="a small table is turned over"):
                    sp.dma_start(table_dram.rearrange("j p -> p j"), table_i[:, :, :].rearrange("p a g -> p (a g)"))\
                        .then_inc(table_stored, 16)
                sp.wait_ge(table_stored, 16)
                sp.dma_start(table_row[:, :, :, :].rearrange("o a g p -> o (a g p)"),
                             table_dram.rearrange("(o j) p -> o (j p)", o=1)).then_inc(table_loaded, 16)
                sp.wait_ge(pad_made, 2)
                with sp.Fori(0, E) as e:
                    row = sp.value_load(free_row[0:1, bass.ds(e, 1)], min_val=0, max_val=TRASH - P)
                    sp.dma_start(routed[bass.ds(row, P), :], pad_block[:, :]).then_inc(pads_stored, 16)
                sp.wait_ge(pads_stored, 16 * E)
                sp.wait_ge(table_loaded, 16)

                def load(i, j, q):
                    if not has(i, 0):
                        return
                    row = sp.value_load(table_entry(0, i), min_val=0, max_val=TRASH)
                    wait(sp, xeT_done, i - SLOTS + 1)
                    wait(sp, meta_read, i - SLOTS + 1)
                    sp.dma_start(xe[:, q, :], routed[bass.ds(row, P), :]).then_inc(xe_loaded[q], 16)
                block_steps(sp, load)

            @block.gpsimd
            def _(pool):
                pool.memset(pad_block[:, :], 0.0).then_inc(pad_made, 1)
                pool.memset(ones_f[:, :], 1.0).then_inc(bidx_ready, 1)
                pool.iota(bidx_i[:, :], pattern=[[P, NG]], base=0, channel_multiplier=1).then_inc(bidx_ready, 1)
                pool.wait_ge(pad_made, 1)
                pool.iota(pad_block[:, D + 1:D + 2].bitcast(I32), pattern=[[0, 1]], base=NO_ROW,
                          channel_multiplier=0).then_inc(pad_made, 1)

                def store(i, j, q):
                    if not has(i, 0):
                        return
                    wait_apart(pool, (pad_made, 2), (ye_ready, i + 1))
                    pool.indirect_dma_start(
                        out=weighted, out_offset=bass.IndirectOffsetOnAxis(ap=meta[:, q, 1:2].bitcast(U32), axis=0),
                        in_=ye[:, q, :], in_offset=None, bounds_check=N * TOP_K - 1, oob_is_err=False)\
                        .then_inc(y_stored[q], 16)
                block_steps(pool, store)

            @block.vector
            def _(dve):
                ch = Chain(dve, dve_table, 99)
                ch.begin(0)
                ch.then(dve.tensor_tensor(counts[:, :], base[:, :], region0[:, :], ALU.subtract))
                ch.done(dve.tensor_scalar(counts_i[:, :], counts[:, :], float(P - 1), None, ALU.add))
                dve.tensor_copy(free_row[:, :], base[0:1, :]).then_inc(table_ready, 1)
                ch.wait()
                ch.then(dve.tensor_scalar(blocks_i[:, :], counts_i[:, :], P.bit_length() - 1, None, ALU.logical_shift_right))
                ch.then(dve.tensor_copy(blocks[:, :], blocks_i[:, :]))
                dve.wait_ge(bidx_ready, 2)
                ch.done(dve.tensor_copy(bidx[:, :], bidx_i[:, :]))
                ch.then(dve.tensor_tensor_scan(ends[:, :], ones_f[:, :], blocks[:, :], 0.0, ALU.mult, ALU.add))
                ends_b = ends[:, :].unsqueeze(1).broadcast_to([P, NG, E])
                ch.then(dve.tensor_tensor(passed[:, :, :], ends_b, bidx[:, :].unsqueeze(2).broadcast_to([P, NG, E]), ALU.is_le))
                ch.done(dve.tensor_tensor(starts[:, :, :], passed[:, :, :], ends_b, ALU.mult))
                ch.then(dve.tensor_reduce(expert[:, :], passed[:, :, :], AX, ALU.add))
                ch.then(dve.tensor_reduce(first[:, :], starts[:, :, :], AX, ALU.max))
                ch.then(dve.tensor_tensor(first[:, :], bidx[:, :], first[:, :], ALU.subtract))
                ch.then(dve.tensor_scalar(first[:, :], first[:, :], float(P), None, ALU.mult))
                ch.then(dve.scalar_tensor_tensor(out=table[:, 0, :], in0=expert[:, :], scalar=float(REGION),
                                                 in1=first[:, :], op0=ALU.mult, op1=ALU.add))
                ch.done(dve.tensor_scalar(table[:, 0, :], table[:, 0, :], float(TRASH), None, ALU.min))
                ch.then(dve.tensor_scalar(table[:, 1, :], expert[:, :], float(E - 1), None, ALU.min))
                dve.tensor_copy(table_i[:, :, :], table[:, :, :]).then_inc(table_ready, 1)

                def step(i, j, q):
                    p1, p2 = (q - 1) % 2, q % 2
                    if has(i, 0):
                        dve.wait_ge(xeT_done, i + 1)
                        wait(dve, gu_done, i - 1)
                        if not (isinstance(j, int) and j == 0):
                            dve.wait_ge(y_stored[q], 16 * j)
                        dve.tensor_copy(meta[:, q, :].bitcast(I32), xe[:, q, D:D + 2].bitcast(I32)).then_inc(meta_read, 1)
                        dve.tensor_copy(xeT[:, q % 2, :, :].rearrange("p k t -> p (k t)"), bank[q % 2][:, 0:D])\
                            .then_inc(xeT_evac, 1)
                    if has(i, 1):
                        dve.wait_ge(silu_done, i)
                        wait(dve, hhT_done, i - 2)
                        dve.tensor_tensor(hh[:, p1, :], bank[2 + p1][:, I:2 * I], gate[:, p1, :], ALU.mult)\
                            .then_inc(hh_ready, 1)
                    if has(i, 2):
                        dve.wait_ge(hhT_done, i - 1)
                        wait(dve, ye_done, i - 3)
                        dve.tensor_copy(hhT[:, p2, :], bank[4 + p2][0:I, 0:P]).then_inc(hhT_evac, 1)
                block_steps(dve, step)

            @block.scalar
            def _(act):
                def step(i, j, q):
                    p1 = (q - 1) % 2
                    if has(i, 1):
                        act.wait_ge(gu_done, i)
                        wait(act, hh_ready, i - 2)
                        act.activation(gate[:, p1, :], bank[2 + p1][:, 0:I], ACT.Silu).then_inc(silu_done, 1)
                    if has(i, 3):
                        q3 = (q - 3) % SLOTS
                        act.wait_ge(ye_done, i - 2)
                        act.activation(ye[:, q3, :], bank[6 + p1][:, 0:D], ACT.Copy, scale=meta[:, q3, 0:1])\
                            .then_inc(ye_ready, 1)
                block_steps(act, step)

            @block.tensor
            def _(pe):
                pe.wait_ge(weights_loaded, 16 * 3)
                pe.wait_ge(table_loaded, 16)

                def step(i, j, q):
                    p0, p1 = q % 2, (q - 1) % 2
                    if has(i, 0):
                        pe.wait_ge(xe_loaded[q], 16 * (j + 1))
                        wait(pe, xeT_evac, i - 1)
                        for kt in range(KT):
                            ins = pe.transpose(bank[p0][:, kt * P:(kt + 1) * P], xe[:, q, kt * P:(kt + 1) * P], ident[:, :])
                        ins.then_inc(xeT_done, 1)
                    if has(i, 1):
                        e = pe.value_load(table_entry(1, i - 1), min_val=0, max_val=E - 1)
                        pe.wait_ge(xeT_evac, i)
                        wait(pe, hh_ready, i - 2)
                        for kt in range(KT):
                            ins = pe.matmul(bank[2 + p1][:, 0:2 * I], xeT[:, p1, kt, :],
                                            gu_sb[:, bass.ds(e, 1), kt * 2 * I:(kt + 1) * 2 * I].rearrange("p a f -> p (a f)"),
                                            start=kt == 0, stop=kt == KT - 1)
                        ins.then_inc(gu_done, 1)
                    if has(i, 2):
                        pe.wait_ge(hh_ready, i - 1)
                        wait(pe, hhT_evac, i - 3)
                        pe.transpose(bank[4 + p0][0:I, 0:P], hh[:, p0, :], ident[:, :]).then_inc(hhT_done, 1)
                    if has(i, 3):
                        e = pe.value_load(table_entry(1, i - 3), min_val=0, max_val=E - 1)
                        pe.wait_ge(hhT_evac, i - 2)
                        wait(pe, ye_ready, i - 4)
                        pe.matmul(bank[6 + p1][:, 0:D], hhT[:, p1, :],
                                  dw_sb[:, bass.ds(e, 1), :].rearrange("p a f -> p (a f)"), start=True, stop=True)\
                            .then_inc(ye_done, 1)
                block_steps(pe, step)

        with nc.Block() as block:

            @block.sync
            def _(sp):
                for q in range(SLOTS):
                    sp.wait_ge(y_stored[q], 16 * NBLK // SLOTS)

                def load(j, c):
                    if not isinstance(j, int):
                        sp.wait_ge(first_sum, NC * j + c - TAIL + 1)
                    sp.dma_start(yk[:, c, :], weighted[bass.ds((NC * j + c) * P * TOP_K, P * TOP_K), :]
                                 .rearrange("(p k) f -> p (k f)", k=TOP_K)).then_inc(g_loaded[c], 16)
                for c in range(NC):
                    load(0, c)
                with sp.Fori(1, NB) as j:
                    for c in range(NC):
                        load(j, c)

            @block.vector
            def _(dve):
                def combine(j, c):
                    t = NC * j + c
                    if not isinstance(j, int):
                        dve.wait_ge(second_sum, t - TAIL + 1)
                        dve.wait_ge(out_stored[c], 16 * j)
                    dve.wait_ge(g_loaded[c], 16 * j + 16)
                    dve.tensor_tensor(ysum[:, c, :], yk[:, c, 0:2 * D], yk[:, c, 2 * D:4 * D], ALU.add)\
                        .then_inc(first_sum, 1)
                    dve.wait_ge(first_sum, t + 1)
                    dve.tensor_tensor(ysum2[:, c, :], ysum[:, c, 0:D], ysum[:, c, D:2 * D], ALU.add)\
                        .then_inc(second_sum, 1)
                    dve.wait_ge(second_sum, t + 1)
                    dve.tensor_tensor(res[:, c:c + 1, :], ysum2[:, c:c + 1, :], gb_sb[:, bass.ds(j, 1), :], ALU.mult)\
                        .then_inc(gated, 1)
                    dve.wait_ge(gated, t + 1)
                    dve.tensor_tensor(res[:, c:c + 1, :], res[:, c:c + 1, :], x_all[:, bass.ds(t, 1), :], ALU.add)\
                        .then_inc(out_ready, 1)
                for c in range(NC):
                    combine(0, c)
                with dve.Fori(1, NB) as j:
                    for c in range(NC):
                        combine(j, c)

            @block.scalar
            def _(act):
                flat = out.rearrange("b t f -> (b t) f")
                with act.Fori(0, NB) as j:
                    for c in range(NC):
                        act.wait_ge(out_ready, NC * j + c + 1)
                        act.dma_start(flat[bass.ds((NC * j + c) * P, P), :], res[:, c, :]).then_inc(out_stored[c], 16)
                for c in range(NC):
                    act.wait_ge(out_stored[c], 16 * NB)
        phase_b.close()
    return nc


def kernel(L0_attn_x, L0_attn_Wq, L0_attn_bq, L0_attn_Wk, L0_attn_bk, L0_attn_Wv, L0_attn_bv, L0_attn_Wbeta,
           L0_attn_bbeta, L0_attn_Walpha, L0_attn_balpha, L0_ffn_router_w, L0_ffn_gate_w, L0_ffn_up_w,
           L0_ffn_down_w, L0_c, L0_wmod):
    import numpy as np
    import concourse.bacc as bacc
    from concourse.bass_utils import run_bass_kernel_spmd

    def on_partitions(w):
        w = np.asarray(w)
        return np.ascontiguousarray(w.reshape(-1, P, w.shape[-1]).transpose(1, 0, 2))

    D = L0_attn_x.shape[2]
    E, I, _ = L0_ffn_gate_w.shape
    gate_up = np.concatenate([np.asarray(L0_ffn_gate_w), np.asarray(L0_ffn_up_w)], axis=1)
    arrays = {
        "x": np.asarray(L0_attn_x),
        "wqk": on_partitions(np.concatenate([L0_attn_Wq, L0_attn_Wk], axis=1)),
        "wv": on_partitions(L0_attn_Wv),
        "wab": on_partitions(np.concatenate([L0_attn_Walpha, L0_attn_Wbeta], axis=1)),
        "bqk": np.ascontiguousarray(np.concatenate([L0_attn_bq, L0_attn_bk]).reshape(-1, P).T),
        "bv": np.asarray(L0_attn_bv).reshape(1, -1),
        "bab": np.concatenate([L0_attn_balpha, L0_attn_bbeta]).reshape(1, -1),
        "cT": on_partitions(np.asarray(L0_c).T),
        "wmod": on_partitions(L0_wmod),
        "rw": on_partitions(np.asarray(L0_ffn_router_w).T),
        "gu": np.ascontiguousarray(gate_up.transpose(2, 0, 1).reshape(D // P, P, E, 2 * I)
                                   .transpose(1, 2, 0, 3).reshape(P, E, D // P * 2 * I)),
        "dw": np.ascontiguousarray(np.asarray(L0_ffn_down_w).transpose(2, 0, 1)),
    }
    nc = bacc.Bacc("TRN2", target_bir_lowering=False, num_devices=1)
    aps = {n: nc.dram_tensor(f"in_{n}", a.shape, mybir.dt.from_np(a.dtype), kind="ExternalInput").ap()
           for n, a in arrays.items()}
    out = nc.dram_tensor("out", L0_attn_x.shape, F32, kind="ExternalOutput").ap()
    build(nc, **aps, out=out)
    r = run_bass_kernel_spmd(nc, [{f"in_{n}": a for n, a in arrays.items()}], core_ids=[0])
    return r.results[0]["out"]
```

```python
from contextlib import ExitStack

import concourse.bass as bass
from concourse import mybir

F32 = mybir.dt.float32
BF16 = mybir.dt.bfloat16
I32 = mybir.dt.int32
U32 = mybir.dt.uint32
ALU = mybir.AluOpType
ACT = mybir.ActivationFunctionType
AX = mybir.AxisListType.X

P = 128
TOP_K = 4
SLOTS = 8
TAIL = 4
NO_ROW = 1 << 20
MAGIC = float(0x5F3759DF)
LN_EPS = 1e-5
NORM_MIN_SQ = 1e-24
ALPHA_EPS = 1e-6


class Chain:

    def __init__(self, eng, sem, per):
        self.eng, self.sem, self.per = eng, sem, per

    def begin(self, round_):
        self.base, self.n = round_ * self.per, 0

    def done(self, ins):
        ins.then_inc(self.sem, 1)
        self.n += 1

    def reached(self):
        return self.sem, self.base + self.n

    def wait(self):
        self.eng.wait_ge(*self.reached())

    def then(self, ins):
        self.done(ins)
        self.wait()

    def end(self):
        assert self.n == self.per, (self.n, self.per)


def build(nc, x, wqk, wv, wab, bqk, bv, bab, cT, wmod, rw, gu, dw, out):
    NB, T, D = x.shape
    E = rw.shape[2]
    I = dw.shape[0]
    KT = D // P
    NC = T // P
    H = D // P
    NU = NC * H
    NT = NB * NC
    N = NB * T
    ROW = D + 2
    REGION = N + P
    TRASH = E * REGION
    NBLK = N * TOP_K // P + E
    NMOD = 5
    assert KT == 2 and H == 2 and NC == 4 and NB == 8 and E == 32 and NBLK % SLOTS == 0

    routed = nc.dram_tensor("routed_rows", [TRASH + P, ROW], F32).ap()
    weighted = nc.dram_tensor("weighted_rows", [N * TOP_K, D], F32).ap()
    mod_rows = nc.dram_tensor("mod_rows", [NB, NMOD * D], F32).ap()

    ctx = ExitStack()
    with ctx:
        def sb(name, shape, dt=F32, c=ctx):
            return c.enter_context(nc.sbuf_tensor(name, shape, dt))

        def sem(name):
            return ctx.enter_context(nc.semaphore(name))

        bank = [ctx.enter_context(nc.psum_tensor(f"bank{i}", [P, 512], F32)) for i in range(8)]

        x_all = sb("x_all", [P, NT, D])
        ident = sb("ident", [P, P])
        ones_be = sb("ones_be", [P, E])
        base = sb("base", [P, E])
        region0 = sb("region0", [P, E])
        iota_i = sb("iota_i", [P, E], I32)
        iota_e = sb("iota_e", [P, E])

        phase_a = ExitStack()

        def sa(name, shape, dt=F32):
            return sb(name, shape, dt, phase_a)

        wqk_sb = sa("wqk_sb", [P, KT, 4 * P])
        wv_sb = sa("wv_sb", [P, KT, D])
        wvb = sa("wvb", [P, 2, KT, D + 4])
        bqk_sb = sa("bqk_sb", [P, 4])
        bv8 = sa("bv8", [NB, D])
        bab_sb = sa("bab_sb", [P, 4])
        cT_sb = sa("cT_sb", [P, KT, NB])
        c_act = sa("c_act", [P, 2, KT, NB])
        rw_sb = sa("rw_sb", [P, KT, E])
        mod_b = sa("mod_b", [P, NB, 4 * D])
        mod8 = sa("mod8", [NB, NMOD, D])
        gate8 = sa("gate8", [NB, 2, 2, D])
        scaleT = sa("scaleT", [P, KT, NB])
        shiftT = sa("shiftT", [P, KT, NB])
        tri_incl = sa("tri_incl", [P, P])
        tri_strict = sa("tri_strict", [P, P], BF16)
        ones_bf = sa("ones_bf", [P, P], BF16)
        xn = sa("xn", [P, NC, D])
        hT = sa("hT", [P, KT, T])
        qT = sa("qT", [P, 2, H, T])
        kT = sa("kT", [P, 2, H, T])
        qsT = sa("qsT", [P, H, T])
        v_sb = sa("v_sb", [P, 2, NC, D])
        kw = sa("kw", [P, NC, D])
        decay = sa("decay", [P, NU, P])
        cdecay = sa("cdecay", [P, NU, P])
        attnT = sa("attnT", [P, 2, H, P])
        state = sa("state", [P, H, P])
        rows = sa("rows", [P, 2, NC, TOP_K, ROW])
        h2T = sa("h2T", [P, KT, T])
        xn2 = sa("xn2", [P, NC, D])
        pad_rows = sa("pad_rows", [P, ROW])
        zt = sa("zt", [P, NC, 4])
        zz = sa("zz", [P, NC, 4])
        ez = sa("ez", [P, NC, 4])
        lnin = sa("lnin", [P, NC, 4])
        lnout = sa("lnout", [P, NC, 4])
        beta = sa("beta", [P, NC, H])
        ncla = sa("ncla", [P, NU])
        s_attn = sa("s_attn", [P, NU])
        s_kw = sa("s_kw", [P, NU])
        end_diff = sa("end_diff", [P, NU])
        to_end = sa("to_end", [P, NU])
        stats = sa("stats", [P, NC, 6])
        mv = sa("mv", [P, NC, 2])
        stats2 = sa("stats2", [P, NC, 6])
        mv2 = sa("mv2", [P, NC, 2])
        ksum = sa("ksum", [P, NU])
        NR = NC + NU
        rs_in, rs_ln, rs_y, rs_t = (sa(n, [P, NR]) for n in ("rs_in", "rs_ln", "rs_y", "rs_t"))
        rs2_in, rs2_ln, rs2_y, rs2_t = (sa(n, [P, NC]) for n in ("rs2_in", "rs2_ln", "rs2_y", "rs2_t"))
        logits = sa("logits", [P, NC, E])
        top8 = sa("top8", [P, NC, 8])
        idx8 = sa("idx8", [P, NC, 8], U32)
        idxf = sa("idxf", [P, NC, TOP_K])
        etop = sa("etop", [P, NC, TOP_K])
        esum = sa("esum", [P, NC])
        onehot = sa("onehot", [P, NC, TOP_K, E])
        picked = sa("picked", [P, NC, TOP_K, E])
        mask = sa("mask", [P, NC + 1, E], BF16)
        slot_e = sa("slot_e", [P, NC, E])
        slot_f = sa("slot_f", [P, NC, TOP_K])
        slot_u = sa("slot_u", [P, 2, NC * TOP_K], U32)
        ids = sa("ids", [P, NC, TOP_K], I32)

        squares = xn[:, :, :].rearrange("p c (h f) -> p (c h) f", h=H)

        wmod_sb = rows[:, :, :, :, :].rearrange("p a c k f -> p (a c k f)")[:, 0:KT * 6 * D]\
            .rearrange("p (k f) -> p k f", k=KT)

        after_exp = sem("after_exp")
        after_in = sem("after_in")
        after_ln = sem("after_ln")
        attn_ready = sem("attn_ready")
        base_ready = sem("base_ready")
        bidx_ready = sem("bidx_ready")
        c_exp = sem("c_exp")
        c_silu = sem("c_silu")
        cdecay_done = sem("cdecay_done")
        claB_done = sem("claB_done")
        clas_done = sem("clas_done")
        cols_ready = sem("cols_ready")
        constants = sem("constants")
        decay_done = sem("decay_done")
        diff_ready = sem("diff_ready")
        dve_after = sem("dve_after")
        dve_before = sem("dve_before")
        dve_h2 = sem("dve_h2")
        dve_pos = sem("dve_pos")
        dve_pre = sem("dve_pre")
        dve_scalars = sem("dve_scalars")
        dve_stats2 = sem("dve_stats2")
        dve_table = sem("dve_table")
        dve_top = sem("dve_top")
        etop_exp = sem("etop_exp")
        etop_ready = sem("etop_ready")
        ez_ready = sem("ez_ready")
        first_sum = sem("first_sum")
        gated = sem("gated")
        gu_done = sem("gu_done")
        h2T_done = sem("h2T_done")
        h2T_evac = sem("h2T_evac")
        h2_ready = sem("h2_ready")
        hT_ready = sem("hT_ready")
        hhT_done = sem("hhT_done")
        hhT_evac = sem("hhT_evac")
        hh_ready = sem("hh_ready")
        kTk_done = sem("kTk_done")
        ksum_ready = sem("ksum_ready")
        kw_done = sem("kw_done")
        la_ready = sem("la_ready")
        lnin_ready = sem("lnin_ready")
        loaded = sem("loaded")
        logits_done = sem("logits_done")
        logits_read = sem("logits_read")
        mask_ready = sem("mask_ready")
        masked = sem("masked")
        meta_read = sem("meta_read")
        mod_mm = sem("mod_mm")
        mod_spread = sem("mod_spread")
        mod_stored = sem("mod_stored")
        ncla_ready = sem("ncla_ready")
        norms_exp = sem("norms_exp")
        norms_in = sem("norms_in")
        norms_ln = sem("norms_ln")
        out_ready = sem("out_ready")
        pad_made = sem("pad_made")
        pads_ready = sem("pads_ready")
        pads_stored = sem("pads_stored")
        pool_made = sem("pool_made")
        pos_done = sem("pos_done")
        qk_done = sem("qk_done")
        qk_evac = sem("qk_evac")
        qs_ready = sem("qs_ready")
        rows8_ready = sem("rows8_ready")
        rows_copied = sem("rows_copied")
        scores_done = sem("scores_done")
        second_sum = sem("second_sum")
        silu_done = sem("silu_done")
        skw_ready = sem("skw_ready")
        slots_ready = sem("slots_ready")
        state_ready = sem("state_ready")
        table_loaded = sem("table_loaded")
        table_ready = sem("table_ready")
        table_stored = sem("table_stored")
        to_end_ready = sem("to_end_ready")
        v_done = sem("v_done")
        v_evac = sem("v_evac")
        weights_loaded = sem("weights_loaded")
        wvb_ready = sem("wvb_ready")
        x1_done = sem("x1_done")
        x_loaded = sem("x_loaded")
        xeT_done = sem("xeT_done")
        xeT_evac = sem("xeT_evac")
        xnT_done = sem("xnT_done")
        xn_ready = sem("xn_ready")
        y_done = sem("y_done")
        ye_done = sem("ye_done")
        ye_ready = sem("ye_ready")
        z_ready = sem("z_ready")
        scattered = [sem(f"scattered{i}") for i in range(2)]
        xe_loaded = [sem(f"xe_loaded{i}") for i in range(SLOTS)]
        y_stored = [sem(f"y_stored{i}") for i in range(SLOTS)]
        g_loaded = [sem(f"g_loaded{i}") for i in range(TAIL)]
        out_stored = [sem(f"out_stored{i}") for i in range(TAIL)]

        def steps(eng, body):
            for s in (0, 1):
                body(s, s // 2, s % 2, True, s >= 1, False)
            with eng.Fori(1, NB // 2) as j:
                for par in range(2):
                    body(2 * j + par, j, par, True, True, True)
            for s in (NB, NB + 1):
                body(s, s // 2, s % 2, False, s == NB, True)

        def wait(eng, sem_, value):
            if not (isinstance(value, int) and value <= 0):
                eng.wait_ge(sem_, value)

        def wait_apart(eng, reached, *waits):
            waits = [(sem_, value if isinstance(value, int) else eng.to_reg(value)) for sem_, value in waits]
            eng.wait_ge(*reached)
            for sem_, value in waits:
                wait(eng, sem_, value)

        v_bank = [bank[i] for i in (4, 0, 1, 4)]

        def unit(u):
            return slice((u % 4) * P, (u % 4 + 1) * P)

        with nc.Block() as block:

            @block.sync
            def _(sp):
                sp.dma_start(cT_sb[:, :, :], cT).then_inc(loaded, 16)
                sp.dma_start(wmod_sb, wmod).then_inc(loaded, 16)
                sp.dma_start(bv8[:, :], bv.broadcast_to([NB, D])).then_inc(loaded, 16)
                sp.dma_start(x_all[:, 0:NC, :], x[0].rearrange("(c p) f -> p c f", p=P)).then_inc(x_loaded, 16)
                sp.dma_start(wqk_sb[:, :, :], wqk).then_inc(loaded, 16)
                sp.dma_start(wv_sb[:, :, :], wv).then_inc(loaded, 16)
                for par in range(2):
                    sp.dma_start(wvb[:, par, :, D:D + 4], wab).then_inc(loaded, 16)
                sp.dma_start(bqk_sb[:, :], bqk).then_inc(loaded, 16)
                sp.dma_start(bab_sb[:, :], bab.broadcast_to([P, 4])).then_inc(loaded, 16)
                sp.dma_start(rw_sb[:, :, :], rw).then_inc(loaded, 16)
                sp.wait_ge(x_loaded, 16)
                sp.dma_start(x_all[:, NC:2 * NC, :], x[1].rearrange("(c p) f -> p c f", p=P)).then_inc(x_loaded, 16)
                sp.wait_ge(rows8_ready, 1)
                sp.dma_start(mod_rows, mod8[:, :, :].rearrange("p a b -> p (a b)")).then_inc(mod_stored, 16)
                sp.wait_ge(mod_stored, 16)
                sp.dma_start(mod_b[:, :, :], mod_rows[:, 0:4 * D].partition_broadcast(P)).then_inc(mod_spread, 16)
                for b in range(2, NB):
                    sp.wait_ge(x_loaded, 16 * b)
                    sp.dma_start(x_all[:, b * NC:(b + 1) * NC, :],
                                 x[b].rearrange("(c p) f -> p c f", p=P)).then_inc(x_loaded, 16)

            @block.gpsimd
            def _(pool):
                for t, v in ((ident, 0.0), (tri_incl, 1.0), (tri_strict, 1.0), (ones_bf, 1.0)):
                    pool.memset(t[:, :], v).then_inc(pool_made, 1)
                pool.memset(pad_rows[:, :], 0.0).then_inc(pads_ready, 1)
                pool.wait_ge(pool_made, 4)
                for t, op, fill, cm, st in ((ident, ALU.not_equal, 1.0, 1, -1), (tri_incl, ALU.is_ge, 0.0, -1, 1),
                                            (tri_strict, ALU.is_gt, 0.0, -1, 1)):
                    pool.affine_select(out=t[:, :], in_=t[:, :], compare_op=op, fill=fill, base=0,
                                       pattern=[[st, P]], channel_multiplier=cm).then_inc(pool_made, 1)
                pool.iota(iota_i[:, :], pattern=[[1, E]], base=0, channel_multiplier=0).then_inc(pool_made, 1)
                pool.iota(ids[:, :, :], pattern=[[P * TOP_K, NC], [1, TOP_K]], base=0,
                          channel_multiplier=TOP_K).then_inc(pool_made, 1)
                pool.wait_ge(pads_ready, 1)
                pool.iota(pad_rows[:, D + 1:D + 2].bitcast(I32), pattern=[[0, 1]], base=NO_ROW,
                          channel_multiplier=0).then_inc(pads_ready, 1)
                pool.wait_ge(pool_made, 9)
                pool.tensor_copy(iota_e[:, :], iota_i[:, :]).then_inc(constants, 1)

                pool.wait_ge(pads_ready, 2)
                for par in range(2):
                    half = slice(par * P // 2, (par + 1) * P // 2)
                    pool.dma_start(routed[TRASH:TRASH + P, :][half], pad_rows[half, :]).then_inc(scattered[par], 16)

                def step(s, j, par, f, a, r):
                    if f:
                        wait_apart(pool, (pool_made, 9), (decay_done, s + 1))
                        pool.affine_select(out=decay[:, :, :], in_=decay[:, :, :], compare_op=ALU.is_ge, fill=0.0,
                                           base=0, pattern=[[0, NU], [1, P]], channel_multiplier=-1)\
                            .then_inc(masked, 1)
                    if r:
                        wait_apart(pool, (pool_made, 9), (slots_ready, s - 1), (rows_copied, s - 1))
                        for c in range(NC):
                            for k in range(TOP_K):
                                u = c * TOP_K + k
                                pool.indirect_dma_start(
                                    out=routed, out_offset=bass.IndirectOffsetOnAxis(ap=slot_u[:, par, u:u + 1], axis=0),
                                    in_=rows[:, par, c, k, :], in_offset=None).then_inc(scattered[par], 16)
                steps(pool, step)
                for par in range(2):
                    pool.wait_ge(scattered[par], 16 + 16 * NC * TOP_K * NB // 2)

            @block.scalar
            def _(act):
                act.preload_act_table_set("natural_log_exp_and_others")
                act.wait_ge(loaded, 16 * 10)
                act.activation(c_act[:, 0, :, :], cT_sb[:, :, :], ACT.Exp, scale=-1.0).then_inc(c_exp, 1)

                def rsqrt_start(value_in, ln, y, ready, ln_done, exp_done, round_):
                    act.wait_ge(ready, round_ + 1)
                    act.activation(ln[:, :], value_in[:, :], ACT.Ln).then_inc(ln_done, 1)
                    act.wait_ge(ln_done, round_ + 1)
                    act.activation(y[:, :], ln[:, :], ACT.Exp, scale=-0.5).then_inc(exp_done, 1)

                def modulate(b, at):
                    act.wait_ge(xnT_done, b + 1)
                    for kt in range(KT):
                        ins = act.activation(hT[:, kt, :], bank[kt][:, :], ACT.Identity,
                                             scale=scaleT[:, kt, bass.ds(at, 1)], bias=shiftT[:, kt, bass.ds(at, 1)])
                    ins.then_inc(hT_ready, 1)

                def projected(s, par, g):
                    act.wait_ge(qk_done, 4 * s + g + 1)
                    dst = (kT if g < H else qT)[:, par, g % H, :]
                    at = (g + H) % 4
                    act.activation(dst, bank[2 + g % 2][:, :], ACT.Identity, bias=bqk_sb[:, at:at + 1])\
                        .then_inc(qk_evac, 1)

                def copy_rows(par, tiles):
                    for c in tiles:
                        ins = act.activation(rows[:, par, c, 1:TOP_K, 0:D],
                                             rows[:, par, c, 0:1, 0:D].broadcast_to([P, TOP_K - 1, D]), ACT.Copy)
                    return ins

                rsqrt_start(rs_in, rs_ln, rs_y, norms_in, norms_ln, norms_exp, 0)
                act.wait_ge(cols_ready, 2)
                modulate(0, 0)

                def step(s, j, par, f, a, r):
                    if r:
                        rsqrt_start(rs2_in, rs2_ln, rs2_y, after_in, after_ln, after_exp, s - 2)
                    if f:
                        act.wait_ge(z_ready, s + 1)
                        act.activation(ez[:, :, :], zz[:, :, :], ACT.Exp, scale=-1.0).then_inc(ez_ready, 1)
                        projected(s, par, 0)
                        act.wait_ge(lnin_ready, s + 1)
                        act.activation(lnout[:, :, :], lnin[:, :, :], ACT.Ln).then_inc(la_ready, 1)
                        projected(s, par, 1)
                        act.wait_ge(diff_ready, s + 1)
                        act.activation(to_end[:, :], end_diff[:, :], ACT.Exp).then_inc(to_end_ready, 1)
                        act.wait_ge(kTk_done, s + 1)
                        act.wait_ge(norms_in, s + 1)
                        for u in range(NU):
                            ins = act.activation(squares[:, u, :], bank[u // 4][:, unit(u)],
                                                 ACT.Square, accum_out=ksum[:, u:u + 1])
                        ins.then_inc(ksum_ready, 1)
                    if r:
                        for kt in range(KT):
                            act.wait_ge(h2T_done, KT * (s - 2) + kt + 1)
                            act.activation(h2T[:, kt, :], bank[4][:, :], ACT.Copy).then_inc(h2T_evac, 1)
                    if f:
                        rsqrt_start(rs_in, rs_ln, rs_y, norms_in, norms_ln, norms_exp, s + 1)
                    if r:
                        copy_rows(par, (0, 1))
                    if f:
                        projected(s, par, 2)
                        act.wait_ge(skw_ready, s + 1)
                        if a:
                            act.wait_ge(y_done, NC * s - 1)
                        for u in range(NU):
                            ins = act.activation(kw[:, u // H, (u % H) * P:(u % H + 1) * P],
                                                 bank[u // 4][:, unit(u)], ACT.Copy, scale=s_kw[:, u:u + 1])
                        ins.then_inc(kw_done, 1)
                    if r:
                        copy_rows(par, (2, 3)).then_inc(rows_copied, 1)
                    if f:
                        projected(s, par, 3)
                    if r:
                        act.wait_ge(etop_ready, s - 1)
                        act.activation(etop[:, :, :], etop[:, :, :], ACT.Exp).then_inc(etop_exp, 1)
                    if f:
                        modulate(s + 1, (s + 1) % NB)
                        act.wait_ge(claB_done, s + 1)
                        act.wait_ge(ncla_ready, s + 1)
                        if a:
                            act.wait_ge(attn_ready, NC * s)
                        for u in range(NU):
                            ins = act.activation(decay[:, u, :], bank[2 + u // 4][:, unit(u)], ACT.Exp, bias=ncla[:, u:u + 1])
                        ins.then_inc(decay_done, 1)
                        if a:
                            act.wait_ge(x1_done, NC * s)
                        for q in range(2):
                            ins = act.activation(cdecay[:, 4 * q:4 * q + 4, :].rearrange("p a b -> p (a b)"),
                                                 bank[2 + q][:, :], ACT.Exp)
                        ins.then_inc(cdecay_done, 1)
                steps(act, step)

            @block.tensor
            def _(pe):
                pe.wait_ge(constants, 1)
                pe.wait_ge(c_silu, 3)
                for i in range(3):
                    for kt in range(KT):
                        pe.matmul(bank[i][0:NB, :], c_act[:, 1, kt, :], wmod_sb[:, kt, i * 512:(i + 1) * 512],
                                  start=kt == 0, stop=kt == KT - 1)
                for i in range(4):
                    for kt in range(KT):
                        ins = pe.matmul(bank[3][:, i * NB:(i + 1) * NB], wmod_sb[:, kt, i * P:(i + 1) * P],
                                        c_act[:, 1, kt, :], start=kt == 0, stop=kt == KT - 1)
                ins.then_inc(mod_mm, 1)
                pe.wait_ge(rows8_ready, 1)
                pe.wait_ge(cols_ready, 2)

                def transpose_input(b):
                    pe.wait_ge(xn_ready, b + 1)
                    wait(pe, kw_done, b)
                    for kt in range(KT):
                        for c in range(NC):
                            ins = pe.transpose(bank[kt][:, c * P:(c + 1) * P], xn[:, c, kt * P:(kt + 1) * P], ident[:, :])
                    ins.then_inc(xnT_done, 1)
                transpose_input(0)

                def scores(s, par, c):
                    wait(pe, attn_ready, NC * (s - 1) + c)
                    if c == 0:
                        pe.wait_ge(qk_evac, 4 * s)
                    for h in range(H):
                        ins = pe.matmul(bank[6][:, (c % 2) * D + h * P:(c % 2) * D + (h + 1) * P],
                                        kT[:, 1 - par, h, c * P:(c + 1) * P],
                                        qT[:, 1 - par, h, c * P:(c + 1) * P], start=True, stop=True)
                    ins.then_inc(scores_done, 1)

                def y_and_delta(s, par, c):
                    t = NC * (s - 1) + c
                    y = bank[5 if c % 2 else 7]
                    pe.wait_ge(attn_ready, t + 1)
                    wait(pe, x1_done, t - 1)
                    if c == 0:
                        pe.wait_ge(v_evac, NC * s)
                        pe.wait_ge(kw_done, s)
                    if c == 1:
                        pe.wait_ge(qs_ready, s)
                    if c > 0:
                        pe.wait_ge(state_ready, (NC - 1) * (s - 1) + c)
                    for h in range(H):
                        hs = slice(h * P, (h + 1) * P)
                        ins = pe.matmul(y[:, hs], attnT[:, c % 2, h, :], v_sb[:, 1 - par, c, hs],
                                        start=True, stop=c == 0)
                        if c > 0:
                            ins = pe.matmul(y[:, hs], qsT[:, h, c * P:(c + 1) * P], state[:, h, :],
                                            start=False, stop=True)
                    if c < NC - 1:
                        for h in range(H):
                            hs = slice(h * P, (h + 1) * P)
                            ins = pe.matmul(y[:, D + h * P:D + (h + 1) * P], kw[:, c, hs],
                                            v_sb[:, 1 - par, c, hs], start=True, stop=True)
                    ins.then_inc(y_done, 1)

                def project(s, g):
                    if g == 0:
                        wait(pe, cdecay_done, s)
                    if g >= 2:
                        pe.wait_ge(qk_evac, 4 * s + g - 1)
                    at = (g + H) % 4
                    for kt in range(KT):
                        ins = pe.matmul(bank[2 + g % 2][:, :], wqk_sb[:, kt, at * P:(at + 1) * P], hT[:, kt, :],
                                        start=kt == 0, stop=kt == KT - 1)
                    ins.then_inc(qk_done, 1)

                def h2_transpose(s, par, kt):
                    if kt == 0:
                        pe.wait_ge(h2_ready, s - 1)
                        pe.wait_ge(base_ready, s - 1)
                    else:
                        pe.wait_ge(h2T_evac, KT * (s - 2) + kt)
                    for c in range(NC):
                        ins = pe.transpose(bank[4][:, c * P:(c + 1) * P],
                                           rows[:, par, c, 0, kt * P:(kt + 1) * P], ident[:, :])
                    ins.then_inc(h2T_done, 1)

                def step(s, j, par, f, a, r):
                    if f:
                        pe.wait_ge(hT_ready, s + 1)
                        pe.wait_ge(wvb_ready, s + 1)
                        if r:
                            pe.wait_ge(base_ready, s - 1)
                        for c in range(NC):
                            if c == NC - 1:
                                pe.wait_ge(v_evac, NC * s + 1)
                            for kt in range(KT):
                                ins = pe.matmul(v_bank[c][:, 0:D + 4], hT[:, kt, c * P:(c + 1) * P], wvb[:, par, kt, :],
                                                start=kt == 0, stop=kt == KT - 1)
                            ins.then_inc(v_done, 1)
                    if a:
                        scores(s, par, 0)
                    if f:
                        project(s, 0)
                    if a:
                        y_and_delta(s, par, 0)
                        scores(s, par, 1)
                    if f:
                        project(s, 1)
                        pe.wait_ge(la_ready, s + 1)
                        pe.wait_ge(v_evac, NC * (s + 1))
                        pe.matmul(bank[4][:, 0:NU].rearrange("p (a b) -> p a b", b=H), tri_incl[:, :],
                                  lnout[:, :, 0:H], start=True, stop=True)
                        pe.matmul(bank[4][:, NU:2 * NU].rearrange("p (a b) -> p a b", b=H),
                                  tri_incl[:, P - 1:P].broadcast_to([P, P]),
                                  lnout[:, :, 0:H], start=True, stop=True).then_inc(clas_done, 1)
                    if a:
                        y_and_delta(s, par, 1)
                        scores(s, par, 2)
                    if f:
                        pe.wait_ge(qk_evac, 4 * s + 2)
                        for u in range(NU):
                            c, h = u // H, u % H
                            ins = pe.transpose(bank[u // 4][:, unit(u)], kT[:, par, h, c * P:(c + 1) * P], ident[:, :])
                        ins.then_inc(kTk_done, 1)
                        pe.wait_ge(diff_ready, s + 1)
                    if r:
                        h2_transpose(s, par, 0)
                    if a:
                        y_and_delta(s, par, 2)
                    if r:
                        h2_transpose(s, par, 1)
                    if a:
                        scores(s, par, 3)
                    if f:
                        project(s, 2)
                    if r:
                        pe.wait_ge(h2T_evac, KT * (s - 1))
                        for i in range(NC):
                            for kt in range(KT):
                                ins = pe.matmul(bank[4][:, i * E:(i + 1) * E],
                                                h2T[:, kt, i * P:(i + 1) * P], rw_sb[:, kt, :],
                                                start=kt == 0, stop=kt == KT - 1)
                        ins.then_inc(logits_done, 1)
                    if a:
                        y_and_delta(s, par, 3)
                    if f:
                        project(s, 3)
                        transpose_input(s + 1)
                    if r:
                        pe.wait_ge(mask_ready, s - 1)
                        pe.wait_ge(logits_read, s - 1)
                        pos = bank[4][:, 0:(NC + 1) * E].rearrange("p (a b) -> p a b", b=E)
                        pe.matmul(pos, tri_strict[:, :], mask[:, :, :], start=True, stop=False)
                        for i in range(NC):
                            ins = pe.matmul(pos[:, i + 1:, :], ones_bf[:, :],
                                            mask[:, i:i + 1, :].broadcast_to([P, NC - i, E]),
                                            start=False, stop=i == NC - 1)
                        ins.then_inc(pos_done, 1)
                    if f:
                        pe.wait_ge(qk_evac, 4 * s + 4)
                        for u in range(NU):
                            ins = pe.matmul(bank[2 + u // 4][:, unit(u)],
                                            lnout[:, u // H, u % H:u % H + 1].broadcast_to([P, P]), tri_incl[:, :],
                                            start=True, stop=True)
                        ins.then_inc(claB_done, 1)
                steps(pe, step)

            @block.vector
            def _(dve):
                before = Chain(dve, dve_before, 2 * NC + 4)
                after = Chain(dve, dve_after, NC + 3)
                stats2_chain = Chain(dve, dve_stats2, NC)
                pre = Chain(dve, dve_pre, 10)
                zc = Chain(dve, dve_scalars, 5)
                h2c = Chain(dve, dve_h2, NC + 1)
                topc = Chain(dve, dve_top, 2 * NC + 2)
                posc = Chain(dve, dve_pos, 8)

                def newton(ch, x, y, t):
                    ch.then(dve.scalar_tensor_tensor(out=t[:, :], in0=y[:, :], scalar=-0.5, in1=y[:, :],
                                                     op0=ALU.mult, op1=ALU.mult))
                    ch.then(dve.tensor_tensor(t[:, :], t[:, :], x[:, :], ALU.mult))
                    ch.then(dve.scalar_tensor_tensor(out=y[:, :], in0=t[:, :], scalar=1.5, in1=y[:, :],
                                                     op0=ALU.add, op1=ALU.mult))

                def input_stats(b, at, keys):
                    ch = before
                    ch.begin(b)
                    wait_apart(dve, (constants, 1), (x_loaded, 16 * at + 16))
                    for c in range(NC):
                        ch.done(dve.bn_stats(stats[:, c, :], x_all[:, bass.ds(NC * at + c, 1), :]
                                             .rearrange("p a f -> p (a f)")))
                    wait_apart(dve, (constants, 1), ch.reached())
                    for c in range(NC):
                        ch.done(dve.bn_aggr(mv[:, c, :], stats[:, c, :]))
                    ch.wait()
                    ch.done(dve.tensor_scalar(rs_in[:, 0:NC], mv[:, :, 1], LN_EPS, None, ALU.add))
                    if keys:
                        dve.wait_ge(ksum_ready, b)
                        dve.tensor_scalar(rs_in[:, NC:NR], ksum[:, :], NORM_MIN_SQ, None, ALU.max).then_inc(norms_in, 1)
                    else:
                        dve.memset(rs_in[:, NC:NR], 1.0).then_inc(norms_in, 1)

                def input_rsqrt(b):
                    dve.wait_ge(norms_exp, b + 1)
                    newton(before, rs_in, rs_y, rs_t)
                    before.end()

                def normalise_input(b, at):
                    for c in range(NC):
                        ins = dve.tensor_scalar(xn[:, c:c + 1, :], x_all[:, bass.ds(NC * at + c, 1), :],
                                                mv[:, c, 0:1], rs_y[:, c:c + 1], ALU.subtract, ALU.mult)
                    ins.then_inc(xn_ready, 1)

                def gate_weights(b, at, half):
                    dve.tensor_tensor(wvb[:, half, :, 0:D], wv_sb[:, :, :],
                                      mod_b[:, bass.ds(at, 1), 0:D].broadcast_to([P, KT, D]), ALU.mult)\
                        .then_inc(wvb_ready, 1)

                dve.wait_ge(c_exp, 1)
                dve.tensor_scalar(c_act[:, 0, :, :], c_act[:, 0, :, :], 1.0, None, ALU.add).then_inc(c_silu, 1)
                dve.wait_ge(c_silu, 1)
                dve.reciprocal(c_act[:, 1, :, :], c_act[:, 0, :, :]).then_inc(c_silu, 1)
                dve.wait_ge(c_silu, 2)
                dve.tensor_tensor(c_act[:, 1, :, :], c_act[:, 1, :, :], cT_sb[:, :, :], ALU.mult).then_inc(c_silu, 1)
                dve.memset(mask[:, NC, :], 0.0).then_inc(c_silu, 1)
                dve.wait_ge(constants, 1)
                pre.begin(0)
                pre.done(dve.tensor_scalar(region0[:, :], iota_e[:, :], float(REGION), None, ALU.mult))
                dve.tensor_scalar(base[:, :], iota_e[:, :], float(REGION), None, ALU.mult).then_inc(base_ready, 1)
                input_stats(0, 0, False)
                dve.wait_ge(mod_mm, 1)
                cols = bank[3][:, 0:4 * NB].rearrange("p (i k b) -> p i k b", i=2, b=NB)
                dve.tensor_copy(shiftT[:, :, :], cols[:, 0, :, :]).then_inc(cols_ready, 1)
                dve.tensor_scalar(scaleT[:, :, :], cols[:, 1, :, :], 1.0, None, ALU.add).then_inc(cols_ready, 1)
                for i, (g, at) in enumerate(((bank[1][0:NB, 0:D], 0), (bank[2][0:NB, D:2 * D], 4))):
                    pre.then(dve.tensor_scalar(gate8[:, i, 0, :], g, -1.0, None, ALU.mult))
                    pre.done(dve.scalar_tensor_tensor(out=gate8[:, i, 0, :], in0=g, scalar=0.25, in1=gate8[:, i, 0, :],
                                                      op0=ALU.max, op1=ALU.max))
                    pre.then(dve.tensor_scalar(gate8[:, i, 1, :], g, 0.0, 2.0, ALU.is_ge, ALU.mult))
                    pre.then(dve.scalar_tensor_tensor(out=mod8[:, at, :], in0=gate8[:, i, 1, :], scalar=-1.0,
                                                      in1=gate8[:, i, 0, :], op0=ALU.add, op1=ALU.mult))
                pre.done(dve.tensor_tensor(mod8[:, 1, :], mod8[:, 0, :], bv8[:, :], ALU.mult))
                pre.done(dve.tensor_scalar(mod8[:, 2, :], bank[2][0:NB, 0:D], 1.0, None, ALU.add))
                pre.wait()
                dve.tensor_copy(mod8[:, 3, :], bank[1][0:NB, D:2 * D]).then_inc(rows8_ready, 1)
                input_rsqrt(0)
                normalise_input(0, 0)
                dve.wait_ge(mod_spread, 16)
                gate_weights(0, 0, 0)

                def attend(s, c):
                    t = NC * (s - 1) + c
                    dve.wait_ge(scores_done, t + 1)
                    if c == 0:
                        dve.wait_ge(masked, s)
                        dve.wait_ge(skw_ready, s)
                    wait(dve, y_done, t - 1)
                    for h in range(H):
                        u = c * H + h
                        ins = dve.scalar_tensor_tensor(
                            out=attnT[:, c % 2, h, :], in0=bank[6][:, (c % 2) * D + h * P:(c % 2) * D + (h + 1) * P],
                            scalar=s_attn[:, u:u + 1], in1=decay[:, u, :], op0=ALU.mult, op1=ALU.mult)
                    ins.then_inc(attn_ready, 1)

                def update(s, c):
                    t = NC * (s - 1) + c
                    y = bank[5 if c % 2 else 7]
                    dve.wait_ge(y_done, t + 1)
                    if c < NC - 1:
                        wait(dve, state_ready, (NC - 1) * (s - 1) + c)
                        for h in range(H):
                            u = c * H + h
                            delta = y[:, D + h * P:D + (h + 1) * P]
                            if c == 0:
                                ins = dve.tensor_copy(state[:, h, :], delta)
                            else:
                                ins = dve.scalar_tensor_tensor(
                                    out=state[:, h, :], in0=state[:, h, :], scalar=cdecay[:, u, P - 1:P],
                                    in1=delta, op0=ALU.mult, op1=ALU.add)
                        ins.then_inc(state_ready, 1)
                    xt = x_all[:, bass.ds(t, 1), :]
                    dve.tensor_tensor(xt, y[:, 0:D].rearrange("p (a f) -> p a f", a=1), xt, ALU.add)\
                        .then_inc(x1_done, 1)

                def step(s, j, par, f, a, r):
                    if r:
                        ch = after
                        ch.begin(s - 2)
                        wait_apart(dve, (constants, 1), (dve_stats2, NC * (s - 1)))
                        for c in range(NC):
                            ch.done(dve.bn_aggr(mv2[:, c, :], stats2[:, c, :]))
                        ch.wait()
                        dve.tensor_scalar(rs2_in[:, :], mv2[:, :, 1], LN_EPS, None, ALU.add).then_inc(after_in, 1)
                    if f:
                        zc.begin(s)
                        for c in range(NC):
                            dve.wait_ge(v_done, NC * s + c + 1)
                            dve.tensor_tensor(v_sb[:, par, c:c + 1, :], v_bank[c][:, 0:D].rearrange("p (a f) -> p a f", a=1),
                                              mod_b[:, bass.ds(s, 1), D:2 * D], ALU.add)
                            dve.tensor_tensor(zt[:, c, :], v_bank[c][:, D:D + 4], bab_sb[:, :], ALU.add)\
                                .then_inc(v_evac, 1)
                        dve.wait_ge(v_evac, NC * (s + 1))
                        zc.done(dve.tensor_copy(zz[:, :, 0:H], zt[:, :, 0:H]))
                        dve.scalar_tensor_tensor(out=zz[:, :, H:4], in0=zt[:, :, H:4], scalar=-1.0, in1=zt[:, :, H:4],
                                                 op0=ALU.mult, op1=ALU.max).then_inc(z_ready, 1)
                    if a:
                        attend(s, 0)
                    if f:
                        dve.wait_ge(ez_ready, s + 1)
                        zc.then(dve.tensor_scalar(lnin[:, :, :], ez[:, :, :], 1.0, None, ALU.add))
                        zc.then(dve.reciprocal(lnin[:, :, 0:H], lnin[:, :, 0:H]))
                        dve.tensor_scalar(lnin[:, :, 0:H], lnin[:, :, 0:H], ALPHA_EPS, None, ALU.add)\
                            .then_inc(lnin_ready, 1)
                    if r:
                        dve.wait_ge(after_exp, s - 1)
                        newton(after, rs2_in, rs2_y, rs2_t)
                        after.end()
                        h2c.begin(s - 2)
                        for c in range(NC):
                            h2c.done(dve.tensor_scalar(xn2[:, c:c + 1, :], x_all[:, bass.ds(NC * (s - 2) + c, 1), :],
                                                       mv2[:, c, 0:1], rs2_y[:, c:c + 1],
                                                       ALU.subtract, ALU.mult))
                    if a:
                        update(s, 0)
                        attend(s, 1)
                        dve.wait_ge(cdecay_done, s)
                        dve.tensor_tensor(
                            qsT[:, :, P:T].rearrange("p h (c t) -> p h c t", t=P),
                            qT[:, 1 - par, :, P:T].rearrange("p h (c t) -> p h c t", t=P),
                            cdecay[:, H:NU, :].rearrange("p (c h) t -> p h c t", h=H), ALU.mult).then_inc(qs_ready, 1)
                    if f:
                        dve.wait_ge(la_ready, s + 1)
                        zc.done(dve.scalar_tensor_tensor(out=beta[:, :, :], in0=zt[:, :, H:4], scalar=0.0,
                                                         in1=lnout[:, :, H:4], op0=ALU.max, op1=ALU.add))
                        dve.wait_ge(clas_done, s + 1)
                        dve.tensor_scalar(ncla[:, :], bank[4][:, 0:NU], -1.0, None, ALU.mult).then_inc(ncla_ready, 1)
                        dve.wait_ge(ncla_ready, s + 1)
                        dve.tensor_tensor(end_diff[:, :], bank[4][:, NU:2 * NU], ncla[:, :], ALU.add)\
                            .then_inc(diff_ready, 1)
                    if r:
                        h2c.wait()
                        h2c.then(dve.tensor_tensor(xn2[:, :, :], xn2[:, :, :],
                                                   mod_b[:, bass.ds(s - 2, 1), 2 * D:3 * D].broadcast_to([P, NC, D]),
                                                   ALU.mult))
                        dve.wait_ge(scattered[par], 16 + 16 * NC * TOP_K * (j - 1))
                        dve.tensor_tensor(rows[:, par, :, 0, 0:D], xn2[:, :, :],
                                          mod_b[:, bass.ds(s - 2, 1), 3 * D:4 * D].broadcast_to([P, NC, D]),
                                          ALU.add).then_inc(h2_ready, 1)
                        h2c.end()
                    if a:
                        update(s, 1)
                        attend(s, 2)
                    if f:
                        input_stats(s + 1, (s + 1) % NB, True)
                    if a:
                        update(s, 2)
                        attend(s, 3)
                    if f:
                        input_rsqrt(s + 1)
                        zc.done(dve.tensor_tensor(s_attn[:, :], beta[:, :, :].rearrange("p a b -> p (a b)"),
                                                  rs_y[:, NC:NR], ALU.mult))
                        zc.wait()
                        dve.wait_ge(to_end_ready, s + 1)
                        dve.tensor_tensor(s_kw[:, :], s_attn[:, :], to_end[:, :], ALU.mult).then_inc(skw_ready, 1)
                        zc.end()
                    if r:
                        dve.wait_ge(logits_done, s - 1)
                        dve.tensor_copy(logits[:, :, :].rearrange("p a b -> p (a b)"), bank[4][:, 0:NC * E])\
                            .then_inc(logits_read, 1)
                    if f:
                        normalise_input(s + 1, (s + 1) % NB)
                    if r:
                        top_experts(s, par)
                    if a:
                        update(s, 3)
                    if f:
                        gate_weights(s + 1, (s + 1) % NB, 1 - par)
                    if r:
                        places(s, par)
                    if a:
                        ch = stats2_chain
                        ch.begin(s - 1)
                        wait_apart(dve, (constants, 1), (x1_done, NC * s))
                        for c in range(NC):
                            ch.done(dve.bn_stats(stats2[:, c, :], x_all[:, bass.ds(NC * (s - 1) + c, 1), :]
                                                 .rearrange("p a f -> p (a f)")))
                        ch.end()

                def top_experts(s, par):
                    ch = topc
                    ch.begin(s - 2)
                    wait_apart(dve, (constants, 1), (logits_read, s - 1))
                    for c in range(NC):
                        ch.done(dve.max(top8[:, c, :], logits[:, c, :]))
                    wait_apart(dve, (constants, 1), ch.reached())
                    dve.tensor_tensor(etop[:, :, :], top8[:, :, 0:TOP_K],
                                      top8[:, :, 0:1].broadcast_to([P, NC, TOP_K]), ALU.subtract).then_inc(etop_ready, 1)
                    for c in range(NC):
                        ch.done(dve.max_index(idx8[:, c, :], top8[:, c, :], logits[:, c, :]))
                    ch.wait()
                    ch.then(dve.tensor_copy(idxf[:, :, :], idx8[:, :, 0:TOP_K]))
                    ch.then(dve.tensor_tensor(
                        onehot[:, :, :, :].rearrange("p c k e -> p (c k) e"),
                        iota_e[:, :].unsqueeze(1).broadcast_to([P, NC * TOP_K, E]),
                        idxf[:, :, :].rearrange("p c k -> p (c k)").unsqueeze(2).broadcast_to([P, NC * TOP_K, E]),
                        ALU.is_equal))
                    dve.tensor_reduce(mask[:, 0:NC, :], onehot[:, :, :, :].rearrange("p c k e -> p c e k"), AX, ALU.max)\
                        .then_inc(mask_ready, 1)
                    ch.end()

                def places(s, par):
                    ch = posc
                    ch.begin(s - 2)
                    dve.wait_ge(etop_exp, s - 1)
                    ch.then(dve.tensor_reduce(esum[:, :], etop[:, :, :], AX, ALU.add))
                    ch.then(dve.reciprocal(esum[:, :], esum[:, :]))
                    ch.done(dve.tensor_tensor(rows[:, par, :, :, D], etop[:, :, :],
                                              esum[:, :].unsqueeze(2).broadcast_to([P, NC, TOP_K]), ALU.mult))
                    ch.then(dve.tensor_copy(rows[:, par, :, :, D + 1:D + 2].rearrange("p c k o -> p (c k o)").bitcast(I32),
                                            ids[:, :, :].rearrange("p c k -> p (c k)")))
                    ch.done(dve.tensor_scalar(ids[:, :, :], ids[:, :, :], float(T * TOP_K), None, ALU.add))
                    dve.wait_ge(pos_done, s - 1)
                    dve.wait_ge(base_ready, s - 1)
                    ch.then(dve.tensor_tensor(slot_e[:, :, :], bank[4][:, 0:NC * E].rearrange("p (a b) -> p a b", b=E),
                                              base[:, :].unsqueeze(1).broadcast_to([P, NC, E]), ALU.add))
                    dve.tensor_tensor(base[:, :], bank[4][:, NC * E:(NC + 1) * E], base[:, :], ALU.add)\
                        .then_inc(base_ready, 1)
                    ch.then(dve.tensor_tensor(picked[:, :, :, :], onehot[:, :, :, :],
                                              slot_e[:, :, :].unsqueeze(2).broadcast_to([P, NC, TOP_K, E]), ALU.mult))
                    ch.then(dve.tensor_reduce(slot_f[:, :, :], picked[:, :, :, :], AX, ALU.add))
                    dve.tensor_copy(slot_u[:, par, :], slot_f[:, :, :].rearrange("p c k -> p (c k)"))\
                        .then_inc(slots_ready, 1)
                    ch.end()

                steps(dve, step)
        phase_a.close()

        phase_b = ExitStack()

        def se(name, shape, dt=F32):
            return sb(name, shape, dt, phase_b)

        gu_sb = se("gu_sb", [P, E, KT * 2 * I])
        dw_sb = se("dw_sb", [I, E, D])
        gb_sb = se("gb_sb", [P, NB, D])
        pad_block = se("pad_block", [P, ROW])
        counts = se("counts", [P, E])
        counts_i = se("counts_i", [P, E], I32)
        blocks_i = se("blocks_i", [P, E], I32)
        blocks = se("blocks", [P, E])
        ones_f = se("ones_f", [P, E])
        ends = se("ends", [P, E])
        NG = -(-NBLK // P)
        bidx_i = se("bidx_i", [P, NG], I32)
        bidx = se("bidx", [P, NG])
        passed = se("passed", [P, NG, E])
        starts = se("starts", [P, NG, E])
        expert = se("expert", [P, NG])
        first = se("first", [P, NG])
        table = se("table", [P, 2, NG])
        table_i = se("table_i", [P, 2, NG], I32)
        table_row = se("table_row", [1, 2, NG, P], I32)
        free_row = se("free_row", [1, E], I32)
        xe = se("xe", [P, SLOTS, ROW])
        meta = se("meta", [P, SLOTS, 2])
        xeT = se("xeT", [P, 2, KT, P])
        gate = se("gate", [P, 2, I])
        hh = se("hh", [P, 2, I])
        hhT = se("hhT", [I, 2, P])
        ye = se("ye", [P, SLOTS, D])
        yk = se("yk", [P, TAIL, TOP_K * D])
        ysum = se("ysum", [P, TAIL, 2 * D])
        ysum2 = se("ysum2", [P, TAIL, D])
        res = se("res", [P, TAIL, D])
        table_dram = nc.dram_tensor("table_dram", [2 * NG, P], I32).ap()

        def block_steps(eng, body):
            for i in range(SLOTS):
                body(i, 0, i)
            with eng.Fori(1, NBLK // SLOTS) as j:
                for q in range(SLOTS):
                    body(SLOTS * j + q, j, q)
            for q in range(3):
                body(NBLK + q, NBLK // SLOTS, q)

        def table_entry(which, i):
            flat = table_row[:, :, :, :].rearrange("o a g p -> o (a g p)")
            return flat[0:1, bass.ds(i + which * NG * P, 1)]

        def has(i, lag):
            return not isinstance(i, int) or 0 <= i - lag < NBLK

        with nc.Block() as block:

            @block.sync
            def _(sp):
                sp.dma_start(gu_sb[:, :, :], gu).then_inc(weights_loaded, 16)
                sp.dma_start(dw_sb[:, :, :], dw).then_inc(weights_loaded, 16)
                sp.dma_start(gb_sb[:, :, :], mod_rows[:, 4 * D:5 * D].partition_broadcast(P)).then_inc(weights_loaded, 16)
                sp.wait_ge(table_ready, 2)
                with nc.allow_non_contiguous_dma(reason="a small table is turned over"):
                    sp.dma_start(table_dram.rearrange("j p -> p j"), table_i[:, :, :].rearrange("p a g -> p (a g)"))\
                        .then_inc(table_stored, 16)
                sp.wait_ge(table_stored, 16)
                sp.dma_start(table_row[:, :, :, :].rearrange("o a g p -> o (a g p)"),
                             table_dram.rearrange("(o j) p -> o (j p)", o=1)).then_inc(table_loaded, 16)
                sp.wait_ge(pad_made, 2)
                with sp.Fori(0, E) as e:
                    row = sp.value_load(free_row[0:1, bass.ds(e, 1)], min_val=0, max_val=TRASH - P)
                    sp.dma_start(routed[bass.ds(row, P), :], pad_block[:, :]).then_inc(pads_stored, 16)
                sp.wait_ge(pads_stored, 16 * E)
                sp.wait_ge(table_loaded, 16)

                def load(i, j, q):
                    if not has(i, 0):
                        return
                    row = sp.value_load(table_entry(0, i), min_val=0, max_val=TRASH)
                    wait(sp, xeT_done, i - SLOTS + 1)
                    wait(sp, meta_read, i - SLOTS + 1)
                    sp.dma_start(xe[:, q, :], routed[bass.ds(row, P), :]).then_inc(xe_loaded[q], 16)
                block_steps(sp, load)

            @block.gpsimd
            def _(pool):
                pool.memset(pad_block[:, :], 0.0).then_inc(pad_made, 1)
                pool.memset(ones_f[:, :], 1.0).then_inc(bidx_ready, 1)
                pool.iota(bidx_i[:, :], pattern=[[P, NG]], base=0, channel_multiplier=1).then_inc(bidx_ready, 1)
                pool.wait_ge(pad_made, 1)
                pool.iota(pad_block[:, D + 1:D + 2].bitcast(I32), pattern=[[0, 1]], base=NO_ROW,
                          channel_multiplier=0).then_inc(pad_made, 1)

                def store(i, j, q):
                    if not has(i, 0):
                        return
                    wait_apart(pool, (pad_made, 2), (ye_ready, i + 1))
                    pool.indirect_dma_start(
                        out=weighted, out_offset=bass.IndirectOffsetOnAxis(ap=meta[:, q, 1:2].bitcast(U32), axis=0),
                        in_=ye[:, q, :], in_offset=None, bounds_check=N * TOP_K - 1, oob_is_err=False)\
                        .then_inc(y_stored[q], 16)
                block_steps(pool, store)

            @block.vector
            def _(dve):
                ch = Chain(dve, dve_table, 99)
                ch.begin(0)
                ch.then(dve.tensor_tensor(counts[:, :], base[:, :], region0[:, :], ALU.subtract))
                ch.done(dve.tensor_scalar(counts_i[:, :], counts[:, :], float(P - 1), None, ALU.add))
                dve.tensor_copy(free_row[:, :], base[0:1, :]).then_inc(table_ready, 1)
                ch.wait()
                ch.then(dve.tensor_scalar(blocks_i[:, :], counts_i[:, :], P.bit_length() - 1, None, ALU.logical_shift_right))
                ch.then(dve.tensor_copy(blocks[:, :], blocks_i[:, :]))
                dve.wait_ge(bidx_ready, 2)
                ch.done(dve.tensor_copy(bidx[:, :], bidx_i[:, :]))
                ch.then(dve.tensor_tensor_scan(ends[:, :], ones_f[:, :], blocks[:, :], 0.0, ALU.mult, ALU.add))
                ends_b = ends[:, :].unsqueeze(1).broadcast_to([P, NG, E])
                ch.then(dve.tensor_tensor(passed[:, :, :], ends_b, bidx[:, :].unsqueeze(2).broadcast_to([P, NG, E]), ALU.is_le))
                ch.done(dve.tensor_tensor(starts[:, :, :], passed[:, :, :], ends_b, ALU.mult))
                ch.then(dve.tensor_reduce(expert[:, :], passed[:, :, :], AX, ALU.add))
                ch.then(dve.tensor_reduce(first[:, :], starts[:, :, :], AX, ALU.max))
                ch.then(dve.tensor_tensor(first[:, :], bidx[:, :], first[:, :], ALU.subtract))
                ch.then(dve.tensor_scalar(first[:, :], first[:, :], float(P), None, ALU.mult))
                ch.then(dve.scalar_tensor_tensor(out=table[:, 0, :], in0=expert[:, :], scalar=float(REGION),
                                                 in1=first[:, :], op0=ALU.mult, op1=ALU.add))
                ch.done(dve.tensor_scalar(table[:, 0, :], table[:, 0, :], float(TRASH), None, ALU.min))
                ch.then(dve.tensor_scalar(table[:, 1, :], expert[:, :], float(E - 1), None, ALU.min))
                dve.tensor_copy(table_i[:, :, :], table[:, :, :]).then_inc(table_ready, 1)

                def step(i, j, q):
                    p1, p2 = (q - 1) % 2, q % 2
                    if has(i, 0):
                        dve.wait_ge(xeT_done, i + 1)
                        wait(dve, gu_done, i - 1)
                        if not (isinstance(j, int) and j == 0):
                            dve.wait_ge(y_stored[q], 16 * j)
                        dve.tensor_copy(meta[:, q, :].bitcast(I32), xe[:, q, D:D + 2].bitcast(I32)).then_inc(meta_read, 1)
                        dve.tensor_copy(xeT[:, q % 2, :, :].rearrange("p k t -> p (k t)"), bank[q % 2][:, 0:D])\
                            .then_inc(xeT_evac, 1)
                    if has(i, 1):
                        dve.wait_ge(silu_done, i)
                        wait(dve, hhT_done, i - 2)
                        dve.tensor_tensor(hh[:, p1, :], bank[2 + p1][:, I:2 * I], gate[:, p1, :], ALU.mult)\
                            .then_inc(hh_ready, 1)
                    if has(i, 2):
                        dve.wait_ge(hhT_done, i - 1)
                        wait(dve, ye_done, i - 3)
                        dve.tensor_copy(hhT[:, p2, :], bank[4 + p2][0:I, 0:P]).then_inc(hhT_evac, 1)
                block_steps(dve, step)

            @block.scalar
            def _(act):
                def step(i, j, q):
                    p1 = (q - 1) % 2
                    if has(i, 1):
                        act.wait_ge(gu_done, i)
                        wait(act, hh_ready, i - 2)
                        act.activation(gate[:, p1, :], bank[2 + p1][:, 0:I], ACT.Silu).then_inc(silu_done, 1)
                    if has(i, 3):
                        q3 = (q - 3) % SLOTS
                        act.wait_ge(ye_done, i - 2)
                        act.activation(ye[:, q3, :], bank[6 + p1][:, 0:D], ACT.Copy, scale=meta[:, q3, 0:1])\
                            .then_inc(ye_ready, 1)
                block_steps(act, step)

            @block.tensor
            def _(pe):
                pe.wait_ge(weights_loaded, 16 * 3)
                pe.wait_ge(table_loaded, 16)

                def step(i, j, q):
                    p0, p1 = q % 2, (q - 1) % 2
                    if has(i, 0):
                        pe.wait_ge(xe_loaded[q], 16 * (j + 1))
                        wait(pe, xeT_evac, i - 1)
                        for kt in range(KT):
                            ins = pe.transpose(bank[p0][:, kt * P:(kt + 1) * P], xe[:, q, kt * P:(kt + 1) * P], ident[:, :])
                        ins.then_inc(xeT_done, 1)
                    if has(i, 1):
                        e = pe.value_load(table_entry(1, i - 1), min_val=0, max_val=E - 1)
                        pe.wait_ge(xeT_evac, i)
                        wait(pe, hh_ready, i - 2)
                        for kt in range(KT):
                            ins = pe.matmul(bank[2 + p1][:, 0:2 * I], xeT[:, p1, kt, :],
                                            gu_sb[:, bass.ds(e, 1), kt * 2 * I:(kt + 1) * 2 * I].rearrange("p a f -> p (a f)"),
                                            start=kt == 0, stop=kt == KT - 1)
                        ins.then_inc(gu_done, 1)
                    if has(i, 2):
                        pe.wait_ge(hh_ready, i - 1)
                        wait(pe, hhT_evac, i - 3)
                        pe.transpose(bank[4 + p0][0:I, 0:P], hh[:, p0, :], ident[:, :]).then_inc(hhT_done, 1)
                    if has(i, 3):
                        e = pe.value_load(table_entry(1, i - 3), min_val=0, max_val=E - 1)
                        pe.wait_ge(hhT_evac, i - 2)
                        wait(pe, ye_ready, i - 4)
                        pe.matmul(bank[6 + p1][:, 0:D], hhT[:, p1, :],
                                  dw_sb[:, bass.ds(e, 1), :].rearrange("p a f -> p (a f)"), start=True, stop=True)\
                            .then_inc(ye_done, 1)
                block_steps(pe, step)

        with nc.Block() as block:

            @block.sync
            def _(sp):
                for q in range(SLOTS):
                    sp.wait_ge(y_stored[q], 16 * NBLK // SLOTS)

                def load(j, c):
                    if not isinstance(j, int):
                        sp.wait_ge(first_sum, NC * j + c - TAIL + 1)
                    sp.dma_start(yk[:, c, :], weighted[bass.ds((NC * j + c) * P * TOP_K, P * TOP_K), :]
                                 .rearrange("(p k) f -> p (k f)", k=TOP_K)).then_inc(g_loaded[c], 16)
                for c in range(NC):
                    load(0, c)
                with sp.Fori(1, NB) as j:
                    for c in range(NC):
                        load(j, c)

            @block.vector
            def _(dve):
                def combine(j, c):
                    t = NC * j + c
                    if not isinstance(j, int):
                        dve.wait_ge(second_sum, t - TAIL + 1)
                        dve.wait_ge(out_stored[c], 16 * j)
                    dve.wait_ge(g_loaded[c], 16 * j + 16)
                    dve.tensor_tensor(ysum[:, c, :], yk[:, c, 0:2 * D], yk[:, c, 2 * D:4 * D], ALU.add)\
                        .then_inc(first_sum, 1)
                    dve.wait_ge(first_sum, t + 1)
                    dve.tensor_tensor(ysum2[:, c, :], ysum[:, c, 0:D], ysum[:, c, D:2 * D], ALU.add)\
                        .then_inc(second_sum, 1)
                    dve.wait_ge(second_sum, t + 1)
                    dve.tensor_tensor(res[:, c:c + 1, :], ysum2[:, c:c + 1, :], gb_sb[:, bass.ds(j, 1), :], ALU.mult)\
                        .then_inc(gated, 1)
                    dve.wait_ge(gated, t + 1)
                    dve.tensor_tensor(res[:, c:c + 1, :], res[:, c:c + 1, :], x_all[:, bass.ds(t, 1), :], ALU.add)\
                        .then_inc(out_ready, 1)
                for c in range(NC):
                    combine(0, c)
                with dve.Fori(1, NB) as j:
                    for c in range(NC):
                        combine(j, c)

            @block.scalar
            def _(act):
                flat = out.rearrange("b t f -> (b t) f")
                with act.Fori(0, NB) as j:
                    for c in range(NC):
                        act.wait_ge(out_ready, NC * j + c + 1)
                        act.dma_start(flat[bass.ds((NC * j + c) * P, P), :], res[:, c, :]).then_inc(out_stored[c], 16)
                for c in range(NC):
                    act.wait_ge(out_stored[c], 16 * NB)
        phase_b.close()
    return nc


def kernel(L0_attn_x, L0_attn_Wq, L0_attn_bq, L0_attn_Wk, L0_attn_bk, L0_attn_Wv, L0_attn_bv, L0_attn_Wbeta,
           L0_attn_bbeta, L0_attn_Walpha, L0_attn_balpha, L0_ffn_router_w, L0_ffn_gate_w, L0_ffn_up_w,
           L0_ffn_down_w, L0_c, L0_wmod):
    import numpy as np
    import concourse.bacc as bacc
    from concourse.bass_utils import run_bass_kernel_spmd

    def on_partitions(w):
        w = np.asarray(w)
        return np.ascontiguousarray(w.reshape(-1, P, w.shape[-1]).transpose(1, 0, 2))

    D = L0_attn_x.shape[2]
    E, I, _ = L0_ffn_gate_w.shape
    gate_up = np.concatenate([np.asarray(L0_ffn_gate_w), np.asarray(L0_ffn_up_w)], axis=1)
    arrays = {
        "x": np.asarray(L0_attn_x),
        "wqk": on_partitions(np.concatenate([L0_attn_Wq, L0_attn_Wk], axis=1)),
        "wv": on_partitions(L0_attn_Wv),
        "wab": on_partitions(np.concatenate([L0_attn_Walpha, L0_attn_Wbeta], axis=1)),
        "bqk": np.ascontiguousarray(np.concatenate([L0_attn_bq, L0_attn_bk]).reshape(-1, P).T),
        "bv": np.asarray(L0_attn_bv).reshape(1, -1),
        "bab": np.concatenate([L0_attn_balpha, L0_attn_bbeta]).reshape(1, -1),
        "cT": on_partitions(np.asarray(L0_c).T),
        "wmod": on_partitions(L0_wmod),
        "rw": on_partitions(np.asarray(L0_ffn_router_w).T),
        "gu": np.ascontiguousarray(gate_up.transpose(2, 0, 1).reshape(D // P, P, E, 2 * I)
                                   .transpose(1, 2, 0, 3).reshape(P, E, D // P * 2 * I)),
        "dw": np.ascontiguousarray(np.asarray(L0_ffn_down_w).transpose(2, 0, 1)),
    }
    nc = bacc.Bacc("TRN2", target_bir_lowering=False, num_devices=1)
    aps = {n: nc.dram_tensor(f"in_{n}", a.shape, mybir.dt.from_np(a.dtype), kind="ExternalInput").ap()
           for n, a in arrays.items()}
    out = nc.dram_tensor("out", L0_attn_x.shape, F32, kind="ExternalOutput").ap()
    build(nc, **aps, out=out)
    r = run_bass_kernel_spmd(nc, [{f"in_{n}": a for n, a in arrays.items()}], core_ids=[0])
    return r.results[0]["out"]
```

```python
from contextlib import ExitStack

import concourse.bass as bass
from concourse import mybir

F32 = mybir.dt.float32
BF16 = mybir.dt.bfloat16
I32 = mybir.dt.int32
U32 = mybir.dt.uint32
ALU = mybir.AluOpType
ACT = mybir.ActivationFunctionType
AX = mybir.AxisListType.X

P = 128
TOP_K = 4
SLOTS = 8
GU_PARTS = 4
DW_PARTS = 2
TAIL = 4
NO_ROW = 1 << 20
LN_EPS = 1e-5
NORM_MIN_SQ = 1e-24
ALPHA_EPS = 1e-6


class Chain:

    def __init__(self, eng, sem, per):
        self.eng, self.sem, self.per = eng, sem, per

    def begin(self, round_):
        self.base, self.n = round_ * self.per, 0

    def done(self, ins):
        ins.then_inc(self.sem, 1)
        self.n += 1

    def reached(self):
        return self.sem, self.base + self.n

    def wait(self):
        self.eng.wait_ge(*self.reached())

    def then(self, ins):
        self.done(ins)
        self.wait()

    def end(self):
        assert self.n == self.per, (self.n, self.per)


def build(nc, x, wqk, wv, wab, bqk, bv, bab, cT, wmod, rw, gu, dw, out):
    NB, T, D = x.shape
    E = rw.shape[2]
    I = dw.shape[0]
    KT = D // P
    NC = T // P
    H = D // P
    NU = NC * H
    NT = NB * NC
    N = NB * T
    ROW = D + 2
    REGION = N + P
    TRASH = E * REGION
    NBLK = N * TOP_K // P + E
    NMOD = 5
    LOADS = 8
    assert KT == 2 and H == 2 and NC == 4 and NB == 8 and E == 32 and NBLK % SLOTS == 0

    routed = nc.dram_tensor("routed_rows", [TRASH + P, ROW], F32).ap()
    weighted = nc.dram_tensor("weighted_rows", [N * TOP_K, D], F32).ap()
    mod_rows = nc.dram_tensor("mod_rows", [NB, NMOD * D], F32).ap()

    ctx = ExitStack()
    with ctx:
        def sb(name, shape, dt=F32, c=ctx):
            return c.enter_context(nc.sbuf_tensor(name, shape, dt))

        def sem(name):
            return ctx.enter_context(nc.semaphore(name))

        bank = [ctx.enter_context(nc.psum_tensor(f"bank{i}", [P, 512], F32)) for i in range(8)]

        x_all = sb("x_all", [P, NT, D])
        ident = sb("ident", [P, P])
        base = sb("base", [P, E])
        region0 = sb("region0", [P, E])
        iota_i = sb("iota_i", [P, E], I32)
        iota_e = sb("iota_e", [P, E])

        ones_f = sb("ones_f", [P, E])
        NG = -(-NBLK // P)
        bidx_i = sb("bidx_i", [P, NG], I32)
        bidx = sb("bidx", [P, NG])
        table_row = sb("table_row", [1, 2, NG, P], I32)
        repeated = sb("repeated", [P, NG * P], I32)
        skip_id = sb("skip_id", [P, NG * P])
        table_dram = nc.dram_tensor("table_dram", [3 * NG, P], I32).ap()

        gu_sb = sb("gu_sb", [P, E, KT * 2 * I])
        mod_b = sb("mod_b", [P, NB, 4 * D])
        dw_sb = mod_b[0:I, :, :].rearrange("p b f -> p (b f)").rearrange("p (e f) -> p e f", e=E)
        gu_flat = gu_sb[:, :, :].rearrange("p e f -> p (e f)")
        taken = [0]

        def over(*shape):
            n = 1
            for extent in shape:
                n *= extent
            view = gu_flat[:, taken[0]:taken[0] + n]
            taken[0] += n
            assert taken[0] <= E * KT * 2 * I
            names = "abc"[:len(shape)]
            return view.rearrange(f"p ({' '.join(names)}) -> p {' '.join(names)}", **dict(zip(names, shape)))

        phase_a = ExitStack()

        def sa(name, shape, dt=F32):
            return sb(name, shape, dt, phase_a)

        wqk_sb = over(KT, 4 * P)
        wv_sb = over(KT, D)
        wvb = sa("wvb", [P, 2, KT, D + 4])
        bqk_sb = sa("bqk_sb", [P, 4])
        bv8 = sa("bv8", [NB, D])
        bab_sb = sa("bab_sb", [P, 4])
        cT_sb = sa("cT_sb", [P, KT, NB])
        c_act = sa("c_act", [P, 2, KT, NB])
        rw_sb = sa("rw_sb", [P, KT, E])
        mod8 = sa("mod8", [NB, NMOD, D])
        gate8 = sa("gate8", [NB, 2, 2, D])
        scaleT = sa("scaleT", [P, KT, NB])
        shiftT = sa("shiftT", [P, KT, NB])
        tri_incl = sa("tri_incl", [P, P])
        tri_strict = sa("tri_strict", [P, P], BF16)
        ones_bf = sa("ones_bf", [P, P], BF16)
        xn = over(NC, D)
        hT = over(KT, T)
        qT = over(2, H, T)
        kT = over(2, H, T)
        qsT = over(H, T)
        v_sb = over(2, NC, D)
        kw = over(NC, D)
        decay = sa("decay", [P, NU, P])
        cdecay = sa("cdecay", [P, NU, P])
        attnT = over(2, H, P)
        state = sa("state", [P, H, P])
        rows = sa("rows", [P, 2, NC, TOP_K, ROW])
        h2T = sa("h2T", [P, KT, T])
        xn2 = sa("xn2", [P, NC, D])
        pad_rows = sa("pad_rows", [P, ROW])
        zt = sa("zt", [P, NC, 4])
        zz = sa("zz", [P, NC, 4])
        ez = sa("ez", [P, NC, 4])
        lnin = sa("lnin", [P, NC, 4])
        lnout = sa("lnout", [P, NC, 4])
        beta = sa("beta", [P, NC, H])
        ncla = sa("ncla", [P, NU])
        s_attn = sa("s_attn", [P, NU])
        s_kw = sa("s_kw", [P, NU])
        end_diff = sa("end_diff", [P, NU])
        to_end = sa("to_end", [P, NU])
        stats = sa("stats", [P, NC, 6])
        mv = sa("mv", [P, NC, 2])
        stats2 = sa("stats2", [P, NC, 6])
        mv2 = sa("mv2", [P, NC, 2])
        ksum = sa("ksum", [P, NU])
        NR = NC + NU
        rs_in, rs_ln, rs_y, rs_t = (sa(n, [P, NR]) for n in ("rs_in", "rs_ln", "rs_y", "rs_t"))
        neg_mean = sa("neg_mean", [P, NC])
        rs2_in, rs2_ln, rs2_y, rs2_t = (sa(n, [P, NC]) for n in ("rs2_in", "rs2_ln", "rs2_y", "rs2_t"))
        logits = sa("logits", [P, NC, E])
        top8 = sa("top8", [P, NC, 8])
        idx8 = sa("idx8", [P, NC, 8], U32)
        idxf = sa("idxf", [P, NC, TOP_K])
        etop = sa("etop", [P, NC, TOP_K])
        esum = sa("esum", [P, NC])
        onehot = sa("onehot", [P, NC, TOP_K, E])
        picked = sa("picked", [P, NC, TOP_K, E])
        mask = sa("mask", [P, NC + 1, E], BF16)
        slot_e = sa("slot_e", [P, NC, E])
        slot_f = sa("slot_f", [P, NC, TOP_K])
        counts = sa("counts", [P, E])
        counts_i = sa("counts_i", [P, E], I32)
        blocks_i = sa("blocks_i", [P, E], I32)
        blocks = sa("blocks", [P, E])
        ends = sa("ends", [P, E])
        last_at = sa("last_at", [P, E])
        last_step = sa("last_step", [P, E])
        passed = sa("passed", [P, NG, E])
        starts = sa("starts", [P, NG, E])
        expert = sa("expert", [P, NG])
        first = sa("first", [P, NG])
        start = sa("start", [P, NG])
        table = sa("table", [P, 3, NG])
        table_i = sa("table_i", [P, 3, NG], I32)
        slot_u = sa("slot_u", [P, 2, NC * TOP_K], U32)
        ids = sa("ids", [P, NC, TOP_K], I32)

        squares = xn[:, :, :].rearrange("p c (h f) -> p (c h) f", h=H)

        wmod_sb = rows[:, :, :, :, :].rearrange("p a c k f -> p (a c k f)")[:, 0:KT * 6 * D]\
            .rearrange("p (k f) -> p k f", k=KT)

        after_exp = sem("after_exp")
        after_in = sem("after_in")
        after_ln = sem("after_ln")
        after_scaled = sem("after_scaled")
        attn_ready = sem("attn_ready")
        base_ready = sem("base_ready")
        bidx_ready = sem("bidx_ready")
        c_exp = sem("c_exp")
        c_loaded = sem("c_loaded")
        c_silu = sem("c_silu")
        cdecay_done = sem("cdecay_done")
        claB_done = sem("claB_done")
        clas_done = sem("clas_done")
        cols_mm = sem("cols_mm")
        cols_ready = sem("cols_ready")
        constants = sem("constants")
        decay_done = sem("decay_done")
        dest_ready = sem("dest_ready")
        diff_ready = sem("diff_ready")
        dve_after = sem("dve_after")
        dve_before = sem("dve_before")
        dve_h2 = sem("dve_h2")
        dve_pos = sem("dve_pos")
        dve_pre = sem("dve_pre")
        dve_scalars = sem("dve_scalars")
        dve_stats2 = sem("dve_stats2")
        dve_table = sem("dve_table")
        dve_top = sem("dve_top")
        etop_exp = sem("etop_exp")
        etop_ready = sem("etop_ready")
        expert_ready = sem("expert_ready")
        ez_ready = sem("ez_ready")
        first_sum = sem("first_sum")
        gate_rows_ready = sem("gate_rows_ready")
        gated = sem("gated")
        gb_loaded = sem("gb_loaded")
        gu_done = sem("gu_done")
        h2T_done = sem("h2T_done")
        h2T_evac = sem("h2T_evac")
        h2_ready = sem("h2_ready")
        hT_ready = sem("hT_ready")
        hhT_done = sem("hhT_done")
        hhT_evac = sem("hhT_evac")
        hh_ready = sem("hh_ready")
        kTk_done = sem("kTk_done")
        ksum_ready = sem("ksum_ready")
        kw_done = sem("kw_done")
        la_ready = sem("la_ready")
        lnin_ready = sem("lnin_ready")
        loaded = sem("loaded")
        logits_done = sem("logits_done")
        logits_read = sem("logits_read")
        mask_ready = sem("mask_ready")
        masked = sem("masked")
        mod_first = sem("mod_first")
        mod_spread = sem("mod_spread")
        mod_spread2 = sem("mod_spread2")
        mod_stored = sem("mod_stored")
        ncla_ready = sem("ncla_ready")
        norms_exp = sem("norms_exp")
        norms_in = sem("norms_in")
        norms_ln = sem("norms_ln")
        other_sum = sem("other_sum")
        out_ready = sem("out_ready")
        pads_ready = sem("pads_ready")
        pads_stored = sem("pads_stored")
        pool_made = sem("pool_made")
        pos_done = sem("pos_done")
        qk_done = sem("qk_done")
        qk_evac = sem("qk_evac")
        qs_ready = sem("qs_ready")
        rows8_ready = sem("rows8_ready")
        rows_copied = sem("rows_copied")
        rows_mm = sem("rows_mm")
        scores_done = sem("scores_done")
        second_sum = sem("second_sum")
        silu_done = sem("silu_done")
        skw_ready = sem("skw_ready")
        slots_ready = sem("slots_ready")
        state_ready = sem("state_ready")
        table_loaded = sem("table_loaded")
        table_ready = sem("table_ready")
        table_stored = sem("table_stored")
        to_end_ready = sem("to_end_ready")
        v_done = sem("v_done")
        v_evac = sem("v_evac")
        weights_loaded = sem("weights_loaded")
        wmod_loaded = sem("wmod_loaded")
        wmod_loaded2 = sem("wmod_loaded2")
        wvb_ready = sem("wvb_ready")
        x1_done = sem("x1_done")
        x_loaded = sem("x_loaded")
        xeT_done = sem("xeT_done")
        xeT_evac = sem("xeT_evac")
        xn2_ready = sem("xn2_ready")
        xnT_done = sem("xnT_done")
        xn_ready = sem("xn_ready")
        y_done = sem("y_done")
        ye_done = sem("ye_done")
        ye_ready = sem("ye_ready")
        z_ready = sem("z_ready")
        scattered = [sem(f"scattered{i}") for i in range(2)]
        xe_loaded = [sem(f"xe_loaded{i}") for i in range(SLOTS)]
        y_stored = [sem(f"y_stored{i}") for i in range(SLOTS)]
        g_loaded = [sem(f"g_loaded{i}") for i in range(TAIL)]
        out_stored = [sem(f"out_stored{i}") for i in range(TAIL)]

        def steps(eng, body):
            for s in (0, 1):
                body(s, s // 2, s % 2, True, s >= 1, False)
            with eng.Fori(1, NB // 2) as j:
                for par in range(2):
                    body(2 * j + par, j, par, True, True, True)
            for s in (NB, NB + 1):
                body(s, s // 2, s % 2, False, s == NB, True)

        def wait(eng, sem_, value):
            if not (isinstance(value, int) and value <= 0):
                eng.wait_ge(sem_, value)

        def wait_apart(eng, reached, *waits):
            waits = [(sem_, value if isinstance(value, int) else eng.to_reg(value)) for sem_, value in waits]
            eng.wait_ge(*reached)
            for sem_, value in waits:
                wait(eng, sem_, value)

        v_bank = [bank[i] for i in (0, 1, 4, 5)]

        def unit(u):
            return slice((u % 4) * P, (u % 4 + 1) * P)

        with nc.Block() as block:

            @block.sync
            def _(sp):
                sp.dma_start(cT_sb[:, :, :], cT).then_inc(c_loaded, 16)
                sp.dma_start(wmod_sb[:, :, 0:3 * D], wmod[:, :, 0:3 * D]).then_inc(wmod_loaded, 16)
                sp.dma_start(x_all[:, 0:NC, :], x[0].rearrange("(c p) f -> p c f", p=P)).then_inc(x_loaded, 16)
                sp.dma_start(wmod_sb[:, :, 3 * D:6 * D], wmod[:, :, 3 * D:6 * D]).then_inc(wmod_loaded2, 16)
                sp.dma_start(bqk_sb[:, :], bqk).then_inc(loaded, 16)
                sp.dma_start(bv8[:, :], bv.broadcast_to([NB, D])).then_inc(loaded, 16)
                sp.dma_start(wqk_sb[:, :, :], wqk).then_inc(loaded, 16)
                sp.dma_start(wv_sb[:, :, :], wv).then_inc(loaded, 16)
                for par in range(2):
                    sp.dma_start(wvb[:, par, :, D:D + 4], wab).then_inc(loaded, 16)
                sp.dma_start(bab_sb[:, :], bab.broadcast_to([P, 4])).then_inc(loaded, 16)
                sp.dma_start(rw_sb[:, :, :], rw).then_inc(loaded, 16)
                sp.wait_ge(x_loaded, 16)
                sp.dma_start(x_all[:, NC:2 * NC, :], x[1].rearrange("(c p) f -> p c f", p=P)).then_inc(x_loaded, 16)
                sp.wait_ge(gate_rows_ready, 1)
                sp.dma_start(mod_rows[:, 0:2 * D], mod8[:, 0:2, :].rearrange("p a b -> p (a b)")).then_inc(mod_stored, 16)
                sp.wait_ge(mod_stored, 16)
                sp.dma_start(mod_b[:, 0:1, 0:2 * D], mod_rows[0:1, 0:2 * D].partition_broadcast(P)).then_inc(mod_first, 16)
                sp.dma_start(mod_b[:, 1:NB, 0:2 * D], mod_rows[1:NB, 0:2 * D].partition_broadcast(P)).then_inc(mod_spread, 16)
                sp.wait_ge(rows8_ready, 1)
                sp.dma_start(mod_rows[:, 2 * D:5 * D], mod8[:, 2:5, :].rearrange("p a b -> p (a b)")).then_inc(mod_stored, 16)
                sp.wait_ge(mod_stored, 32)
                sp.dma_start(mod_b[:, :, 2 * D:4 * D], mod_rows[:, 2 * D:4 * D].partition_broadcast(P)).then_inc(mod_spread2, 16)
                sp.wait_ge(pads_ready, 2)
                sp.dma_start(routed[0:TRASH, :].rearrange("(e r) f -> r e f", r=REGION)[0:P],
                             pad_rows[:, :].unsqueeze(1).broadcast_to([P, E, ROW])).then_inc(pads_stored, 16)
                for b in range(2, NB):
                    sp.wait_ge(x_loaded, 16 * b)
                    sp.dma_start(x_all[:, b * NC:(b + 1) * NC, :],
                                 x[b].rearrange("(c p) f -> p c f", p=P)).then_inc(x_loaded, 16)
                sp.wait_ge(x1_done, NC * NB)
                sp.wait_ge(hT_ready, NB + 1)
                for n in range(GU_PARTS):
                    part = slice(n * E // GU_PARTS, (n + 1) * E // GU_PARTS)
                    sp.dma_start(gu_sb[:, part, :], gu[:, part, :]).then_inc(weights_loaded, 16)
                    sp.wait_ge(weights_loaded, 16 * (n + 1))
                sp.wait_ge(h2_ready, NB)
                for n in range(DW_PARTS):
                    part = slice(n * E // DW_PARTS, (n + 1) * E // DW_PARTS)
                    sp.dma_start(dw_sb[:, part, :], dw[:, part, :]).then_inc(weights_loaded, 16)
                    sp.wait_ge(weights_loaded, 16 * (GU_PARTS + n + 1))

            @block.gpsimd
            def _(pool):
                for t, v in ((ident, 0.0), (tri_incl, 1.0), (tri_strict, 1.0), (ones_bf, 1.0)):
                    pool.memset(t[:, :], v).then_inc(pool_made, 1)
                pool.memset(pad_rows[:, :], 0.0).then_inc(pads_ready, 1)
                pool.wait_ge(pool_made, 4)
                for t, op, fill, cm, st in ((ident, ALU.not_equal, 1.0, 1, -1), (tri_incl, ALU.is_ge, 0.0, -1, 1),
                                            (tri_strict, ALU.is_gt, 0.0, -1, 1)):
                    pool.affine_select(out=t[:, :], in_=t[:, :], compare_op=op, fill=fill, base=0,
                                       pattern=[[st, P]], channel_multiplier=cm).then_inc(pool_made, 1)
                pool.iota(iota_i[:, :], pattern=[[1, E]], base=0, channel_multiplier=0).then_inc(pool_made, 1)
                pool.iota(ids[:, :, :], pattern=[[P * TOP_K, NC], [1, TOP_K]], base=0,
                          channel_multiplier=TOP_K).then_inc(pool_made, 1)
                pool.wait_ge(pads_ready, 1)
                pool.iota(pad_rows[:, D + 1:D + 2].bitcast(I32), pattern=[[0, 1]], base=NO_ROW,
                          channel_multiplier=0).then_inc(pads_ready, 1)
                pool.wait_ge(pool_made, 9)
                pool.tensor_copy(iota_e[:, :], iota_i[:, :]).then_inc(constants, 1)

                pool.wait_ge(pads_ready, 2)
                for par in range(2):
                    half = slice(par * P // 2, (par + 1) * P // 2)
                    pool.dma_start(routed[TRASH:TRASH + P, :][half], pad_rows[half, :]).then_inc(scattered[par], 16)
                pool.memset(ones_f[:, :], 1.0).then_inc(bidx_ready, 1)
                pool.iota(bidx_i[:, :], pattern=[[P, NG]], base=0, channel_multiplier=1).then_inc(bidx_ready, 1)

                pool.wait_ge(loaded, 16 * LOADS)

                def step(s, j, par, f, a, r):
                    if f:
                        wait_apart(pool, (mod_spread, 16), (v_done, NC * s + 1))
                        pool.tensor_tensor(wvb[:, 1 - par, :, 0:D], wv_sb[:, :, :],
                                           mod_b[:, bass.ds((s + 1) % NB, 1), 0:D].broadcast_to([P, KT, D]), ALU.mult)\
                            .then_inc(wvb_ready, 1)
                        wait_apart(pool, (pool_made, 9), (decay_done, s + 1))
                        pool.affine_select(out=decay[:, :, :], in_=decay[:, :, :], compare_op=ALU.is_ge, fill=0.0,
                                           base=0, pattern=[[0, NU], [1, P]], channel_multiplier=-1)\
                            .then_inc(masked, 1)
                        pool.wait_ge(cdecay_done, s + 1)
                        if a:
                            pool.wait_ge(y_done, NC * s)
                        pool.tensor_tensor(
                            qsT[:, :, P:T].rearrange("p h (c t) -> p h c t", t=P),
                            qT[:, par, :, P:T].rearrange("p h (c t) -> p h c t", t=P),
                            cdecay[:, H:NU, :].rearrange("p (c h) t -> p h c t", h=H), ALU.mult).then_inc(qs_ready, 1)
                    if r:
                        wait_apart(pool, (pads_stored, 16), (slots_ready, s - 1), (rows_copied, s - 1))
                        for c in range(NC):
                            for k in range(TOP_K):
                                u = c * TOP_K + k
                                pool.indirect_dma_start(
                                    out=routed, out_offset=bass.IndirectOffsetOnAxis(ap=slot_u[:, par, u:u + 1], axis=0),
                                    in_=rows[:, par, c, k, :], in_offset=None).then_inc(scattered[par], 16)
                steps(pool, step)
                for par in range(2):
                    pool.wait_ge(scattered[par], 16 + 16 * NC * TOP_K * NB // 2)

            @block.scalar
            def _(act):
                act.preload_act_table_set("natural_log_exp_and_others")
                act.wait_ge(c_loaded, 16)
                act.activation(c_act[:, 0, :, :], cT_sb[:, :, :], ACT.Exp, scale=-1.0).then_inc(c_exp, 1)

                def rsqrt_start(value_in, ln, y, ready, ln_done, exp_done, round_):
                    act.wait_ge(ready, round_ + 1)
                    act.activation(ln[:, :], value_in[:, :], ACT.Ln).then_inc(ln_done, 1)
                    act.wait_ge(ln_done, round_ + 1)
                    act.activation(y[:, :], ln[:, :], ACT.Exp, scale=-0.5).then_inc(exp_done, 1)

                def modulate(b, at):
                    act.wait_ge(xnT_done, b + 1)
                    for kt in range(KT):
                        ins = act.activation(hT[:, kt, :], bank[kt][:, :], ACT.Identity,
                                             scale=scaleT[:, kt, bass.ds(at, 1)], bias=shiftT[:, kt, bass.ds(at, 1)])
                    ins.then_inc(hT_ready, 1)

                def projected(s, par, g):
                    act.wait_ge(qk_done, 4 * s + g + 1)
                    dst = (kT if g < H else qT)[:, par, g % H, :]
                    at = (g + H) % 4
                    act.activation(dst, bank[2 + g % 2][:, :], ACT.Identity, bias=bqk_sb[:, at:at + 1])\
                        .then_inc(qk_evac, 1)

                def copy_rows(par, tiles):
                    for c in tiles:
                        ins = act.activation(rows[:, par, c, 1:TOP_K, 0:D],
                                             rows[:, par, c, 0:1, 0:D].broadcast_to([P, TOP_K - 1, D]), ACT.Copy)
                    return ins

                rsqrt_start(rs_in, rs_ln, rs_y, norms_in, norms_ln, norms_exp, 0)
                act.wait_ge(cols_ready, 2)
                modulate(0, 0)
                act.wait_ge(loaded, 16 * LOADS)

                def step(s, j, par, f, a, r):
                    if r:
                        rsqrt_start(rs2_in, rs2_ln, rs2_y, after_in, after_ln, after_exp, s - 2)
                    if f:
                        if not a:
                            projected(s, par, 0)
                            projected(s, par, 1)
                        act.wait_ge(z_ready, s + 1)
                        act.activation(ez[:, :, :], zz[:, :, :], ACT.Exp, scale=-1.0).then_inc(ez_ready, 1)
                        if a:
                            projected(s, par, 0)
                    if r:
                        act.wait_ge(after_scaled, s - 1)
                        for c in range(NC):
                            ins = act.activation(xn2[:, c:c + 1, :], x_all[:, bass.ds(NC * (s - 2) + c, 1), :], ACT.Identity,
                                                 scale=rs2_y[:, c:c + 1], bias=neg_mean[:, c:c + 1])
                        ins.then_inc(xn2_ready, 1)
                    if f:
                        act.wait_ge(lnin_ready, s + 1)
                        act.activation(lnout[:, :, :], lnin[:, :, :], ACT.Ln).then_inc(la_ready, 1)
                        if a:
                            projected(s, par, 1)
                        act.wait_ge(diff_ready, s + 1)
                        act.activation(to_end[:, :], end_diff[:, :], ACT.Exp).then_inc(to_end_ready, 1)
                        act.wait_ge(kTk_done, s + 1)
                        act.wait_ge(norms_in, s + 1)
                        for u in range(NU):
                            ins = act.activation(squares[:, u, :], bank[u // 4][:, unit(u)],
                                                 ACT.Square, accum_out=ksum[:, u:u + 1])
                        ins.then_inc(ksum_ready, 1)
                    if r:
                        for kt in range(KT):
                            act.wait_ge(h2T_done, KT * (s - 2) + kt + 1)
                            act.activation(h2T[:, kt, :], bank[4][:, :], ACT.Copy).then_inc(h2T_evac, 1)
                    if f:
                        rsqrt_start(rs_in, rs_ln, rs_y, norms_in, norms_ln, norms_exp, s + 1)
                    if r:
                        copy_rows(par, (0, 1))
                    if f:
                        projected(s, par, 2)
                        act.wait_ge(skw_ready, s + 1)
                        if a:
                            act.wait_ge(y_done, NC * s - 1)
                        for u in range(NU):
                            ins = act.activation(kw[:, u // H, (u % H) * P:(u % H + 1) * P],
                                                 bank[u // 4][:, unit(u)], ACT.Copy, scale=s_kw[:, u:u + 1])
                        ins.then_inc(kw_done, 1)
                    if r:
                        copy_rows(par, (2, 3)).then_inc(rows_copied, 1)
                    if f:
                        projected(s, par, 3)
                    if r:
                        act.wait_ge(etop_ready, s - 1)
                        act.activation(etop[:, :, :], etop[:, :, :], ACT.Exp).then_inc(etop_exp, 1)
                    if f:
                        modulate(s + 1, (s + 1) % NB)
                        act.wait_ge(claB_done, s + 1)
                        act.wait_ge(ncla_ready, s + 1)
                        if a:
                            act.wait_ge(attn_ready, NC * s)
                        for u in range(NU):
                            ins = act.activation(decay[:, u, :], bank[2 + u // 4][:, unit(u)], ACT.Exp, bias=ncla[:, u:u + 1])
                        ins.then_inc(decay_done, 1)
                        if a:
                            act.wait_ge(x1_done, NC * s)
                        for q in range(2):
                            ins = act.activation(cdecay[:, 4 * q:4 * q + 4, :].rearrange("p a b -> p (a b)"),
                                                 bank[2 + q][:, :], ACT.Exp)
                        ins.then_inc(cdecay_done, 1)
                steps(act, step)
                act.preload_act_table(ACT.Silu)
                act.wait_ge(table_ready, 1)
                with nc.allow_non_contiguous_dma(reason="a small table is turned over"):
                    act.dma_start(table_dram.rearrange("j p -> p j"), table_i[:, :, :].rearrange("p a g -> p (a g)"))\
                        .then_inc(table_stored, 16)
                act.wait_ge(table_stored, 16)
                rows_and_experts = table_dram[0:2 * NG, :]
                act.dma_start(table_row[:, :, :, :].rearrange("o a g p -> o (a g p)"),
                             rows_and_experts.rearrange("(o j) p -> o (j p)", o=1)).then_inc(table_loaded, 16)
                act.dma_start(repeated[:, :], table_dram[2 * NG:3 * NG, :].rearrange("(o j) p -> o (j p)", o=1)
                             .broadcast_to([P, NG * P])).then_inc(table_loaded, 16)

            @block.tensor
            def _(pe):
                def transpose_input(b):
                    pe.wait_ge(xn_ready, b + 1)
                    wait(pe, kw_done, b)
                    for kt in range(KT):
                        for c in range(NC):
                            ins = pe.transpose(bank[kt][:, c * P:(c + 1) * P], xn[:, c, kt * P:(kt + 1) * P], ident[:, :])
                    ins.then_inc(xnT_done, 1)

                pe.wait_ge(constants, 1)
                pe.wait_ge(c_silu, 3)
                pe.wait_ge(wmod_loaded, 16)
                for i in range(4):
                    for kt in range(KT):
                        ins = pe.matmul(bank[3][:, i * NB:(i + 1) * NB], wmod_sb[:, kt, i * P:(i + 1) * P],
                                        c_act[:, 1, kt, :], start=kt == 0, stop=kt == KT - 1)
                ins.then_inc(cols_mm, 1)
                for i, (at, n) in enumerate(((2 * D, D), (3 * D, 2 * D), (5 * D, D))):
                    for kt in range(KT):
                        ins = pe.matmul(bank[4 + i][0:NB, 0:n], c_act[:, 1, kt, :], wmod_sb[:, kt, at:at + n],
                                        start=kt == 0, stop=kt == KT - 1)
                    ins.then_inc(rows_mm, 1)
                    if i == 0:
                        transpose_input(0)
                        pe.wait_ge(wmod_loaded2, 16)

                def scores(s, par, c):
                    wait(pe, attn_ready, NC * (s - 1) + c)
                    if c == 0:
                        pe.wait_ge(qk_evac, 4 * s)
                    for h in range(H):
                        ins = pe.matmul(bank[6][:, (c % 2) * D + h * P:(c % 2) * D + (h + 1) * P],
                                        kT[:, 1 - par, h, c * P:(c + 1) * P],
                                        qT[:, 1 - par, h, c * P:(c + 1) * P], start=True, stop=True)
                    ins.then_inc(scores_done, 1)

                def y_and_delta(s, par, c):
                    t = NC * (s - 1) + c
                    y = bank[5 if c % 2 else 7]
                    pe.wait_ge(attn_ready, t + 1)
                    wait(pe, x1_done, t - 1)
                    if c == 0:
                        pe.wait_ge(v_evac, NC * s)
                        pe.wait_ge(kw_done, s)
                    if c == 1:
                        pe.wait_ge(qs_ready, s)
                    if c > 0:
                        pe.wait_ge(state_ready, (NC - 1) * (s - 1) + c)
                    for h in range(H):
                        hs = slice(h * P, (h + 1) * P)
                        ins = pe.matmul(y[:, hs], attnT[:, c % 2, h, :], v_sb[:, 1 - par, c, hs],
                                        start=True, stop=c == 0)
                        if c > 0:
                            ins = pe.matmul(y[:, hs], qsT[:, h, c * P:(c + 1) * P], state[:, h, :],
                                            start=False, stop=True)
                    if c < NC - 1:
                        for h in range(H):
                            hs = slice(h * P, (h + 1) * P)
                            ins = pe.matmul(y[:, D + h * P:D + (h + 1) * P], kw[:, c, hs],
                                            v_sb[:, 1 - par, c, hs], start=True, stop=True)
                    ins.then_inc(y_done, 1)

                def project(s, g):
                    if g == 0:
                        wait(pe, cdecay_done, s)
                    if g >= 2:
                        pe.wait_ge(qk_evac, 4 * s + g - 1)
                    at = (g + H) % 4
                    for kt in range(KT):
                        ins = pe.matmul(bank[2 + g % 2][:, :], wqk_sb[:, kt, at * P:(at + 1) * P], hT[:, kt, :],
                                        start=kt == 0, stop=kt == KT - 1)
                    ins.then_inc(qk_done, 1)

                def h2_transpose(s, par, kt):
                    if kt == 0:
                        pe.wait_ge(h2_ready, s - 1)
                        pe.wait_ge(base_ready, s - 1)
                    else:
                        pe.wait_ge(h2T_evac, KT * (s - 2) + kt)
                    for c in range(NC):
                        ins = pe.transpose(bank[4][:, c * P:(c + 1) * P],
                                           rows[:, par, c, 0, kt * P:(kt + 1) * P], ident[:, :])
                    ins.then_inc(h2T_done, 1)

                def step(s, j, par, f, a, r):
                    if f and not a:
                        pe.wait_ge(hT_ready, 1)
                        pe.wait_ge(loaded, 16 * LOADS)
                        project(s, 0)
                        project(s, 1)
                        pe.wait_ge(rows8_ready, 1)
                    if f:
                        pe.wait_ge(hT_ready, s + 1)
                        pe.wait_ge(wvb_ready, s + 1)
                        for c in range(NC):
                            if r and c == 2:
                                pe.wait_ge(base_ready, s - 1)
                            if r and c == 3:
                                pe.wait_ge(x1_done, NC * (s - 1))
                            for kt in range(KT):
                                ins = pe.matmul(v_bank[c][:, 0:D + 4], hT[:, kt, c * P:(c + 1) * P], wvb[:, par, kt, :],
                                                start=kt == 0, stop=kt == KT - 1)
                            ins.then_inc(v_done, 1)
                    if a:
                        scores(s, par, 0)
                    if f and a:
                        project(s, 0)
                    if a:
                        y_and_delta(s, par, 0)
                        scores(s, par, 1)
                    if f and a:
                        project(s, 1)
                    if f:
                        pe.wait_ge(la_ready, s + 1)
                        pe.wait_ge(v_evac, NC * (s + 1))
                        pe.matmul(bank[4][:, 0:NU].rearrange("p (a b) -> p a b", b=H), tri_incl[:, :],
                                  lnout[:, :, 0:H], start=True, stop=True)
                        pe.matmul(bank[4][:, NU:2 * NU].rearrange("p (a b) -> p a b", b=H),
                                  tri_incl[:, P - 1:P].broadcast_to([P, P]),
                                  lnout[:, :, 0:H], start=True, stop=True).then_inc(clas_done, 1)
                    if a:
                        y_and_delta(s, par, 1)
                        scores(s, par, 2)
                    if f:
                        pe.wait_ge(qk_evac, 4 * s + 2)
                        for u in range(NU):
                            c, h = u // H, u % H
                            ins = pe.transpose(bank[u // 4][:, unit(u)], kT[:, par, h, c * P:(c + 1) * P], ident[:, :])
                        ins.then_inc(kTk_done, 1)
                        pe.wait_ge(diff_ready, s + 1)
                    if r:
                        h2_transpose(s, par, 0)
                    if a:
                        y_and_delta(s, par, 2)
                    if r:
                        h2_transpose(s, par, 1)
                    if a:
                        scores(s, par, 3)
                    if f:
                        project(s, 2)
                    if r:
                        pe.wait_ge(h2T_evac, KT * (s - 1))
                        for i in range(NC):
                            for kt in range(KT):
                                ins = pe.matmul(bank[4][:, i * E:(i + 1) * E],
                                                h2T[:, kt, i * P:(i + 1) * P], rw_sb[:, kt, :],
                                                start=kt == 0, stop=kt == KT - 1)
                        ins.then_inc(logits_done, 1)
                    if a:
                        y_and_delta(s, par, 3)
                    if f:
                        project(s, 3)
                        transpose_input(s + 1)
                    if f:
                        pe.wait_ge(qk_evac, 4 * s + 4)
                        for u in range(NU):
                            ins = pe.matmul(bank[2 + u // 4][:, unit(u)],
                                            lnout[:, u // H, u % H:u % H + 1].broadcast_to([P, P]), tri_incl[:, :],
                                            start=True, stop=True)
                        ins.then_inc(claB_done, 1)
                    if r:
                        pe.wait_ge(mask_ready, s - 1)
                        pe.wait_ge(logits_read, s - 1)
                        pos = bank[4][:, 0:(NC + 1) * E].rearrange("p (a b) -> p a b", b=E)
                        pe.matmul(pos, tri_strict[:, :], mask[:, :, :], start=True, stop=False)
                        for i in range(NC):
                            ins = pe.matmul(pos[:, i + 1:, :], ones_bf[:, :],
                                            mask[:, i:i + 1, :].broadcast_to([P, NC - i, E]),
                                            start=False, stop=i == NC - 1)
                        ins.then_inc(pos_done, 1)
                steps(pe, step)

            @block.vector
            def _(dve):
                before = Chain(dve, dve_before, 2 * NC + 4)
                after = Chain(dve, dve_after, NC + 3)
                stats2_chain = Chain(dve, dve_stats2, NC)
                pre = Chain(dve, dve_pre, 10)
                zc = Chain(dve, dve_scalars, 5)
                h2c = Chain(dve, dve_h2, 1)
                topc = Chain(dve, dve_top, 2 * NC + 2)
                posc = Chain(dve, dve_pos, 8)

                def newton(ch, x, y, t):
                    ch.then(dve.scalar_tensor_tensor(out=t[:, :], in0=y[:, :], scalar=-0.5, in1=y[:, :],
                                                     op0=ALU.mult, op1=ALU.mult))
                    ch.then(dve.tensor_tensor(t[:, :], t[:, :], x[:, :], ALU.mult))
                    ch.then(dve.scalar_tensor_tensor(out=y[:, :], in0=t[:, :], scalar=1.5, in1=y[:, :],
                                                     op0=ALU.add, op1=ALU.mult))

                def input_stats(b, at, keys):
                    ch = before
                    ch.begin(b)
                    wait_apart(dve, (constants, 1), (x_loaded, 16 * at + 16))
                    for c in range(NC):
                        ch.done(dve.bn_stats(stats[:, c, :], x_all[:, bass.ds(NC * at + c, 1), :]
                                             .rearrange("p a f -> p (a f)")))
                    wait_apart(dve, (constants, 1), ch.reached())
                    for c in range(NC):
                        ch.done(dve.bn_aggr(mv[:, c, :], stats[:, c, :]))
                    ch.wait()
                    ch.done(dve.tensor_scalar(rs_in[:, 0:NC], mv[:, :, 1], LN_EPS, None, ALU.add))
                    if keys:
                        dve.wait_ge(ksum_ready, b)
                        dve.tensor_scalar(rs_in[:, NC:NR], ksum[:, :], NORM_MIN_SQ, None, ALU.max).then_inc(norms_in, 1)
                    else:
                        dve.memset(rs_in[:, NC:NR], 1.0).then_inc(norms_in, 1)

                def input_rsqrt(b):
                    dve.wait_ge(norms_exp, b + 1)
                    newton(before, rs_in, rs_y, rs_t)
                    before.end()

                def normalise_input(b, at):
                    for c in range(NC):
                        ins = dve.tensor_scalar(xn[:, c:c + 1, :], x_all[:, bass.ds(NC * at + c, 1), :],
                                                mv[:, c, 0:1], rs_y[:, c:c + 1], ALU.subtract, ALU.mult)
                    ins.then_inc(xn_ready, 1)

                dve.wait_ge(c_exp, 1)
                dve.tensor_scalar(c_act[:, 0, :, :], c_act[:, 0, :, :], 1.0, None, ALU.add).then_inc(c_silu, 1)
                dve.wait_ge(c_silu, 1)
                dve.reciprocal(c_act[:, 1, :, :], c_act[:, 0, :, :]).then_inc(c_silu, 1)
                dve.wait_ge(c_silu, 2)
                dve.tensor_tensor(c_act[:, 1, :, :], c_act[:, 1, :, :], cT_sb[:, :, :], ALU.mult).then_inc(c_silu, 1)
                dve.memset(mask[:, NC, :], 0.0).then_inc(c_silu, 1)
                dve.wait_ge(constants, 1)
                pre.begin(0)
                pre.done(dve.tensor_scalar(region0[:, :], iota_e[:, :], float(REGION), None, ALU.mult))
                dve.tensor_scalar(base[:, :], iota_e[:, :], float(REGION), None, ALU.mult).then_inc(base_ready, 1)
                input_stats(0, 0, False)
                dve.wait_ge(cols_mm, 1)
                cols = bank[3][:, 0:4 * NB].rearrange("p (i k b) -> p i k b", i=2, b=NB)
                dve.tensor_copy(shiftT[:, :, :], cols[:, 0, :, :]).then_inc(cols_ready, 1)
                dve.tensor_scalar(scaleT[:, :, :], cols[:, 1, :, :], 1.0, None, ALU.add).then_inc(cols_ready, 1)
                input_rsqrt(0)
                normalise_input(0, 0)

                def gate(i, g, at):
                    pre.then(dve.tensor_scalar(gate8[:, i, 0, :], g, -1.0, None, ALU.mult))
                    pre.done(dve.scalar_tensor_tensor(out=gate8[:, i, 0, :], in0=g, scalar=0.25, in1=gate8[:, i, 0, :],
                                                      op0=ALU.max, op1=ALU.max))
                    pre.then(dve.tensor_scalar(gate8[:, i, 1, :], g, 0.0, 2.0, ALU.is_ge, ALU.mult))
                    pre.then(dve.scalar_tensor_tensor(out=mod8[:, at, :], in0=gate8[:, i, 1, :], scalar=-1.0,
                                                      in1=gate8[:, i, 0, :], op0=ALU.add, op1=ALU.mult))
                dve.wait_ge(rows_mm, 1)
                gate(0, bank[4][0:NB, 0:D], 0)
                dve.wait_ge(loaded, 16 * LOADS)
                dve.tensor_tensor(mod8[:, 1, :], mod8[:, 0, :], bv8[:, :], ALU.mult).then_inc(gate_rows_ready, 1)
                dve.wait_ge(rows_mm, 3)
                gate(1, bank[6][0:NB, 0:D], 4)
                pre.then(dve.tensor_scalar(mod8[:, 2, :], bank[5][0:NB, D:2 * D], 1.0, None, ALU.add))
                dve.tensor_copy(mod8[:, 3, :], bank[5][0:NB, 0:D]).then_inc(rows8_ready, 1)
                dve.wait_ge(mod_first, 16)
                dve.tensor_tensor(wvb[:, 0, :, 0:D], wv_sb[:, :, :], mod_b[:, 0:1, 0:D].broadcast_to([P, KT, D]), ALU.mult)\
                    .then_inc(wvb_ready, 1)

                def attend(s, c):
                    t = NC * (s - 1) + c
                    dve.wait_ge(scores_done, t + 1)
                    if c == 0:
                        dve.wait_ge(masked, s)
                        dve.wait_ge(skw_ready, s)
                    wait(dve, y_done, t - 1)
                    for h in range(H):
                        u = c * H + h
                        ins = dve.scalar_tensor_tensor(
                            out=attnT[:, c % 2, h, :], in0=bank[6][:, (c % 2) * D + h * P:(c % 2) * D + (h + 1) * P],
                            scalar=s_attn[:, u:u + 1], in1=decay[:, u, :], op0=ALU.mult, op1=ALU.mult)
                    ins.then_inc(attn_ready, 1)

                def update(s, c):
                    t = NC * (s - 1) + c
                    y = bank[5 if c % 2 else 7]
                    dve.wait_ge(y_done, t + 1)
                    if c < NC - 1:
                        wait(dve, state_ready, (NC - 1) * (s - 1) + c)
                        for h in range(H):
                            u = c * H + h
                            delta = y[:, D + h * P:D + (h + 1) * P]
                            if c == 0:
                                ins = dve.tensor_copy(state[:, h, :], delta)
                            else:
                                ins = dve.scalar_tensor_tensor(
                                    out=state[:, h, :], in0=state[:, h, :], scalar=cdecay[:, u, P - 1:P],
                                    in1=delta, op0=ALU.mult, op1=ALU.add)
                        ins.then_inc(state_ready, 1)
                    xt = x_all[:, bass.ds(t, 1), :]
                    dve.tensor_tensor(xt, y[:, 0:D].rearrange("p (a f) -> p a f", a=1), xt, ALU.add)\
                        .then_inc(x1_done, 1)

                def step(s, j, par, f, a, r):
                    if f:
                        zc.begin(s)
                        for c in range(NC // 2):
                            take_v(s, par, c)
                    if r:
                        ch = after
                        ch.begin(s - 2)
                        wait_apart(dve, (constants, 1), (dve_stats2, NC * (s - 1)))
                        for c in range(NC):
                            ch.done(dve.bn_aggr(mv2[:, c, :], stats2[:, c, :]))
                        ch.wait()
                        dve.tensor_scalar(rs2_in[:, :], mv2[:, :, 1], LN_EPS, None, ALU.add).then_inc(after_in, 1)
                    if f:
                        for c in range(NC // 2, NC):
                            take_v(s, par, c)
                        dve.wait_ge(v_evac, NC * (s + 1))
                        zc.done(dve.tensor_copy(zz[:, :, 0:H], zt[:, :, 0:H]))
                        dve.scalar_tensor_tensor(out=zz[:, :, H:4], in0=zt[:, :, H:4], scalar=-1.0, in1=zt[:, :, H:4],
                                                 op0=ALU.mult, op1=ALU.max).then_inc(z_ready, 1)
                    if a:
                        attend(s, 0)
                    if r:
                        dve.wait_ge(after_exp, s - 1)
                        newton(after, rs2_in, rs2_y, rs2_t)
                        after.end()
                        dve.scalar_tensor_tensor(out=neg_mean[:, :], in0=mv2[:, :, 0], scalar=-1.0, in1=rs2_y[:, :],
                                                 op0=ALU.mult, op1=ALU.mult).then_inc(after_scaled, 1)
                    if f:
                        dve.wait_ge(ez_ready, s + 1)
                        zc.then(dve.tensor_scalar(lnin[:, :, :], ez[:, :, :], 1.0, None, ALU.add))
                        zc.then(dve.reciprocal(lnin[:, :, 0:H], lnin[:, :, 0:H]))
                        dve.tensor_scalar(lnin[:, :, 0:H], lnin[:, :, 0:H], ALPHA_EPS, None, ALU.add)\
                            .then_inc(lnin_ready, 1)
                    if a:
                        update(s, 0)
                        attend(s, 1)
                    if f:
                        dve.wait_ge(la_ready, s + 1)
                        zc.done(dve.scalar_tensor_tensor(out=beta[:, :, :], in0=zt[:, :, H:4], scalar=0.0,
                                                         in1=lnout[:, :, H:4], op0=ALU.max, op1=ALU.add))
                    if r:
                        h2c.begin(s - 2)
                        dve.wait_ge(xn2_ready, s - 1)
                        dve.wait_ge(mod_spread2, 16)
                        h2c.done(dve.tensor_tensor(xn2[:, :, :], xn2[:, :, :],
                                                   mod_b[:, bass.ds(s - 2, 1), 2 * D:3 * D].broadcast_to([P, NC, D]),
                                                   ALU.mult))
                    if f:
                        dve.wait_ge(clas_done, s + 1)
                        dve.tensor_scalar(ncla[:, :], bank[4][:, 0:NU], -1.0, None, ALU.mult).then_inc(ncla_ready, 1)
                        dve.wait_ge(ncla_ready, s + 1)
                        dve.tensor_tensor(end_diff[:, :], bank[4][:, NU:2 * NU], ncla[:, :], ALU.add)\
                            .then_inc(diff_ready, 1)
                    if r:
                        h2c.wait()
                        dve.wait_ge(scattered[par], 16 + 16 * NC * TOP_K * (j - 1))
                        dve.tensor_tensor(rows[:, par, :, 0, 0:D], xn2[:, :, :],
                                          mod_b[:, bass.ds(s - 2, 1), 3 * D:4 * D].broadcast_to([P, NC, D]),
                                          ALU.add).then_inc(h2_ready, 1)
                        h2c.end()
                    if a:
                        update(s, 1)
                        attend(s, 2)
                    if f:
                        input_stats(s + 1, (s + 1) % NB, True)
                    if a:
                        update(s, 2)
                        attend(s, 3)
                    if f:
                        input_rsqrt(s + 1)
                        zc.done(dve.tensor_tensor(s_attn[:, :], beta[:, :, :].rearrange("p a b -> p (a b)"),
                                                  rs_y[:, NC:NR], ALU.mult))
                        zc.wait()
                        dve.wait_ge(to_end_ready, s + 1)
                        dve.tensor_tensor(s_kw[:, :], s_attn[:, :], to_end[:, :], ALU.mult).then_inc(skw_ready, 1)
                        zc.end()
                    if a:
                        stats_after(s, range(NC - 1))
                    if r:
                        dve.wait_ge(logits_done, s - 1)
                        dve.tensor_copy(logits[:, :, :].rearrange("p a b -> p (a b)"), bank[4][:, 0:NC * E])\
                            .then_inc(logits_read, 1)
                    if f:
                        normalise_input(s + 1, (s + 1) % NB)
                    if r:
                        top_experts(s, par)
                    if a:
                        update(s, 3)
                    if r:
                        places(s, par)
                    if a:
                        stats_after(s, (NC - 1,))

                def take_v(s, par, c):
                    dve.wait_ge(v_done, NC * s + c + 1)
                    dve.tensor_tensor(v_sb[:, par, c:c + 1, :], v_bank[c][:, 0:D].rearrange("p (a f) -> p a f", a=1),
                                      mod_b[:, bass.ds(s, 1), D:2 * D], ALU.add)
                    dve.tensor_tensor(zt[:, c, :], v_bank[c][:, D:D + 4], bab_sb[:, :], ALU.add)\
                        .then_inc(v_evac, 1)

                def stats_after(s, tiles):
                    ch = stats2_chain
                    if 0 in tiles:
                        ch.begin(s - 1)
                    wait_apart(dve, (constants, 1), (x1_done, NC * (s - 1) + tiles[-1] + 1))
                    for c in tiles:
                        ch.done(dve.bn_stats(stats2[:, c, :], x_all[:, bass.ds(NC * (s - 1) + c, 1), :]
                                             .rearrange("p a f -> p (a f)")))
                    if NC - 1 in tiles:
                        ch.end()

                def block_table():
                    ch = Chain(dve, dve_table, 19)
                    ch.begin(0)
                    dve.wait_ge(base_ready, NB + 1)
                    ch.then(dve.tensor_tensor(counts[:, :], base[:, :], region0[:, :], ALU.subtract))
                    ch.then(dve.tensor_scalar(counts_i[:, :], counts[:, :], float(P - 1), None, ALU.add))
                    ch.done(dve.tensor_scalar(last_at[:, :], counts[:, :], float(P), 0.0, ALU.subtract, ALU.max))
                    ch.then(dve.tensor_scalar(blocks_i[:, :], counts_i[:, :], P.bit_length() - 1, None, ALU.logical_shift_right))
                    ch.done(dve.tensor_tensor(last_step[:, 0:E - 1], last_at[:, 1:E], last_at[:, 0:E - 1], ALU.subtract))
                    ch.done(dve.tensor_scalar(last_step[:, E - 1:E], last_at[:, E - 1:E], -1.0, None, ALU.mult))
                    ch.then(dve.tensor_copy(blocks[:, :], blocks_i[:, :]))
                    dve.wait_ge(bidx_ready, 2)
                    ch.done(dve.tensor_copy(bidx[:, :], bidx_i[:, :]))
                    ch.then(dve.tensor_tensor_scan(ends[:, :], ones_f[:, :], blocks[:, :], 0.0, ALU.mult, ALU.add))
                    ends_b = ends[:, :].unsqueeze(1).broadcast_to([P, NG, E])
                    ch.then(dve.tensor_tensor(passed[:, :, :], ends_b, bidx[:, :].unsqueeze(2).broadcast_to([P, NG, E]), ALU.is_le))
                    ch.then(dve.tensor_tensor(starts[:, :, :], passed[:, :, :], ends_b, ALU.mult))
                    dve.tensor_reduce(expert[:, :], passed[:, :, :], AX, ALU.add).then_inc(expert_ready, 1)
                    ch.then(dve.tensor_reduce(first[:, :], starts[:, :, :], AX, ALU.max))
                    dve.wait_ge(expert_ready, 1)
                    ch.then(dve.tensor_tensor(starts[:, :, :], passed[:, :, :],
                                              last_step[:, :].unsqueeze(1).broadcast_to([P, NG, E]), ALU.mult))
                    ch.done(dve.tensor_reduce(start[:, :], starts[:, :, :], AX, ALU.add))
                    ch.then(dve.tensor_tensor(first[:, :], bidx[:, :], first[:, :], ALU.subtract))
                    dve.tensor_scalar(start[:, :], start[:, :], last_at[:, 0:1], None, ALU.add).then_inc(expert_ready, 1)
                    ch.then(dve.tensor_scalar(first[:, :], first[:, :], float(P), None, ALU.mult))
                    dve.wait_ge(expert_ready, 2)
                    ch.then(dve.tensor_tensor(start[:, :], start[:, :], first[:, :], ALU.min))
                    ch.done(dve.tensor_tensor(table[:, 2, :], first[:, :], start[:, :], ALU.subtract))
                    dve.tensor_scalar(table[:, 1, :], expert[:, :], float(E - 1), None, ALU.min).then_inc(expert_ready, 1)
                    ch.then(dve.scalar_tensor_tensor(out=table[:, 0, :], in0=expert[:, :], scalar=float(REGION),
                                                     in1=start[:, :], op0=ALU.mult, op1=ALU.add))
                    dve.wait_ge(expert_ready, 3)
                    dve.tensor_copy(table_i[:, :, :], table[:, :, :]).then_inc(table_ready, 1)
                    ch.end()
                    dve.wait_ge(table_loaded, 32)
                    dve.tensor_scalar(skip_id[:, :], repeated[:, :], bidx[:, 0:1], float(NO_ROW), ALU.is_gt, ALU.mult)\
                        .then_inc(table_ready, 1)

                def top_experts(s, par):
                    ch = topc
                    ch.begin(s - 2)
                    wait_apart(dve, (constants, 1), (logits_read, s - 1))
                    for c in range(NC):
                        ch.done(dve.max(top8[:, c, :], logits[:, c, :]))
                    wait_apart(dve, (constants, 1), ch.reached())
                    dve.tensor_tensor(etop[:, :, :], top8[:, :, 0:TOP_K],
                                      top8[:, :, 0:1].broadcast_to([P, NC, TOP_K]), ALU.subtract).then_inc(etop_ready, 1)
                    for c in range(NC):
                        ch.done(dve.max_index(idx8[:, c, :], top8[:, c, :], logits[:, c, :]))
                    ch.wait()
                    ch.then(dve.tensor_copy(idxf[:, :, :], idx8[:, :, 0:TOP_K]))
                    ch.then(dve.tensor_tensor(
                        onehot[:, :, :, :].rearrange("p c k e -> p (c k) e"),
                        iota_e[:, :].unsqueeze(1).broadcast_to([P, NC * TOP_K, E]),
                        idxf[:, :, :].rearrange("p c k -> p (c k)").unsqueeze(2).broadcast_to([P, NC * TOP_K, E]),
                        ALU.is_equal))
                    dve.tensor_reduce(mask[:, 0:NC, :], onehot[:, :, :, :].rearrange("p c k e -> p c e k"), AX, ALU.max)\
                        .then_inc(mask_ready, 1)
                    ch.end()

                def places(s, par):
                    ch = posc
                    ch.begin(s - 2)
                    dve.wait_ge(etop_exp, s - 1)
                    ch.then(dve.tensor_reduce(esum[:, :], etop[:, :, :], AX, ALU.add))
                    ch.then(dve.reciprocal(esum[:, :], esum[:, :]))
                    ch.done(dve.tensor_tensor(rows[:, par, :, :, D], etop[:, :, :],
                                              esum[:, :].unsqueeze(2).broadcast_to([P, NC, TOP_K]), ALU.mult))
                    ch.then(dve.tensor_copy(rows[:, par, :, :, D + 1:D + 2].rearrange("p c k o -> p (c k o)").bitcast(I32),
                                            ids[:, :, :].rearrange("p c k -> p (c k)")))
                    ch.done(dve.tensor_scalar(ids[:, :, :], ids[:, :, :], float(T * TOP_K), None, ALU.add))
                    dve.wait_ge(pos_done, s - 1)
                    dve.wait_ge(base_ready, s - 1)
                    ch.then(dve.tensor_tensor(slot_e[:, :, :], bank[4][:, 0:NC * E].rearrange("p (a b) -> p a b", b=E),
                                              base[:, :].unsqueeze(1).broadcast_to([P, NC, E]), ALU.add))
                    dve.tensor_tensor(base[:, :], bank[4][:, NC * E:(NC + 1) * E], base[:, :], ALU.add)\
                        .then_inc(base_ready, 1)
                    ch.then(dve.tensor_tensor(picked[:, :, :, :], onehot[:, :, :, :],
                                              slot_e[:, :, :].unsqueeze(2).broadcast_to([P, NC, TOP_K, E]), ALU.mult))
                    ch.then(dve.tensor_reduce(slot_f[:, :, :], picked[:, :, :, :], AX, ALU.add))
                    dve.tensor_copy(slot_u[:, par, :], slot_f[:, :, :].rearrange("p c k -> p (c k)"))\
                        .then_inc(slots_ready, 1)
                    ch.end()

                steps(dve, step)
                block_table()
        phase_a.close()

        phase_b = ExitStack()

        def se(name, shape, dt=F32):
            return sb(name, shape, dt, phase_b)

        gb_sb = se("gb_sb", [P, NB, D])
        xe = se("xe", [P, SLOTS, ROW])
        dest = se("dest", [P, SLOTS], I32)
        xeT = se("xeT", [P, 2, KT, P])
        gate = se("gate", [P, 2, I])
        hh = se("hh", [P, 2, I])
        hhT = se("hhT", [I, 2, P])
        ye = se("ye", [P, SLOTS, D])
        yk = se("yk", [P, TAIL, TOP_K * D])
        ysum = se("ysum", [P, TAIL, 2 * D])
        ysum2 = se("ysum2", [P, TAIL, D])
        res = se("res", [P, TAIL, D])

        def block_steps(eng, body, which=None, lag=0):
            flat = table_row[:, :, :, :].rearrange("o a g p -> o (a g p)")

            def entries(i, back, count):
                if which is None:
                    return None
                _, values = nc.values_load_multi_w_load_instructions(
                    flat[0:1, bass.ds(i - back + which * NG * P, back + count)], engines=[eng.engine],
                    min_val=0, max_val=E - 1 if which else TRASH,
                    skip_runtime_bounds_check_because="the table's entries are clamped when it is made")
                return lambda q, behind: values[q - behind + back]

            found = entries(0, 0, SLOTS)
            for i in range(SLOTS):
                body(i, 0, i, found)
            with eng.Fori(1, NBLK // SLOTS) as j:
                found = entries(SLOTS * j, lag, SLOTS)
                for q in range(SLOTS):
                    body(SLOTS * j + q, j, q, found)
            found = entries(NBLK, lag, 0) if lag else None
            for q in range(3):
                body(NBLK + q, NBLK // SLOTS, q, found)

        def has(i, lag):
            return not isinstance(i, int) or 0 <= i - lag < NBLK

        with nc.Block() as block:

            @block.sync
            def _(sp):
                def load(i, j, q, found):
                    if not has(i, 0):
                        return
                    wait(sp, ye_ready, i - SLOTS + 1)
                    sp.dma_start(xe[:, q, :], routed[bass.ds(found(q, 0), P), :]).then_inc(xe_loaded[q], 16)
                block_steps(sp, load, which=0)
                sp.dma_start(gb_sb[:, :, :], mod_rows[:, 4 * D:5 * D].partition_broadcast(P)).then_inc(gb_loaded, 16)

            @block.gpsimd
            def _(pool):
                def store(i, j, q, found):
                    if not has(i, 0):
                        return
                    wait_apart(pool, (bidx_ready, 2), (ye_ready, i + 1))
                    pool.indirect_dma_start(
                        out=weighted, out_offset=bass.IndirectOffsetOnAxis(ap=dest[:, q:q + 1].bitcast(U32), axis=0),
                        in_=ye[:, q, :], in_offset=None, bounds_check=N * TOP_K - 1, oob_is_err=False)\
                        .then_inc(y_stored[q], 16)
                block_steps(pool, store)

            @block.vector
            def _(dve):
                dve.wait_ge(table_ready, 2)

                def step(i, j, q, found):
                    p1, p2 = (q - 1) % 2, q % 2
                    if has(i, 0):
                        dve.wait_ge(xeT_done, i + 1)
                        wait(dve, gu_done, i - 1)
                        dve.tensor_copy(xeT[:, q % 2, :, :].rearrange("p k t -> p (k t)"), bank[q % 2][:, 0:D])\
                            .then_inc(xeT_evac, 1)
                        if not (isinstance(j, int) and j == 0):
                            dve.wait_ge(y_stored[q], 16 * j)
                        dve.tensor_scalar(dest[:, q:q + 1], xe[:, q, D + 1:D + 2].bitcast(I32), skip_id[:, bass.ds(i, 1)],
                                          None, ALU.add).then_inc(dest_ready, 1)
                    if has(i, 1):
                        dve.wait_ge(silu_done, i)
                        wait(dve, hhT_done, i - 2)
                        dve.tensor_tensor(hh[:, p1, :], bank[2 + p1][:, I:2 * I], gate[:, p1, :], ALU.mult)\
                            .then_inc(hh_ready, 1)
                    if has(i, 2):
                        dve.wait_ge(hhT_done, i - 1)
                        wait(dve, ye_done, i - 3)
                        dve.tensor_copy(hhT[:, p2, :], bank[4 + p2][0:I, 0:P]).then_inc(hhT_evac, 1)
                block_steps(dve, step)

            @block.scalar
            def _(act):
                def step(i, j, q, found):
                    p1 = (q - 1) % 2
                    if has(i, 1):
                        act.wait_ge(gu_done, i)
                        wait(act, hh_ready, i - 2)
                        act.activation(gate[:, p1, :], bank[2 + p1][:, 0:I], ACT.Silu).then_inc(silu_done, 1)
                    if has(i, 3):
                        q3 = (q - 3) % SLOTS
                        act.wait_ge(ye_done, i - 2)
                        act.wait_ge(dest_ready, i - 2)
                        act.activation(ye[:, q3, :], bank[6 + p1][:, 0:D], ACT.Copy, scale=xe[:, q3, D:D + 1])\
                            .then_inc(ye_ready, 1)
                block_steps(act, step)

            @block.tensor
            def _(pe):
                pe.wait_ge(weights_loaded, 16 * (GU_PARTS + DW_PARTS))

                def step(i, j, q, found):
                    p0, p1 = q % 2, (q - 1) % 2
                    if has(i, 0):
                        pe.wait_ge(xe_loaded[q], 16 * (j + 1))
                        wait(pe, xeT_evac, i - 1)
                        for kt in range(KT):
                            ins = pe.transpose(bank[p0][:, kt * P:(kt + 1) * P], xe[:, q, kt * P:(kt + 1) * P], ident[:, :])
                        ins.then_inc(xeT_done, 1)
                    if has(i, 1):
                        pe.wait_ge(xeT_evac, i)
                        wait(pe, hh_ready, i - 2)
                        for kt in range(KT):
                            ins = pe.matmul(bank[2 + p1][:, 0:2 * I], xeT[:, p1, kt, :],
                                            gu_sb[:, bass.ds(found(q, 1), 1), kt * 2 * I:(kt + 1) * 2 * I]
                                            .rearrange("p a f -> p (a f)"), start=kt == 0, stop=kt == KT - 1)
                        ins.then_inc(gu_done, 1)
                    if has(i, 2):
                        pe.wait_ge(hh_ready, i - 1)
                        wait(pe, hhT_evac, i - 3)
                        pe.transpose(bank[4 + p0][0:I, 0:P], hh[:, p0, :], ident[:, :]).then_inc(hhT_done, 1)
                    if has(i, 3):
                        pe.wait_ge(hhT_evac, i - 2)
                        wait(pe, ye_ready, i - 4)
                        pe.matmul(bank[6 + p1][:, 0:D], hhT[:, p1, :],
                                  dw_sb[:, bass.ds(found(q, 3), 1), :].rearrange("p a f -> p (a f)"), start=True, stop=True)\
                            .then_inc(ye_done, 1)
                block_steps(pe, step, which=1, lag=3)

        with nc.Block() as block:

            @block.sync
            def _(sp):
                for q in range(SLOTS):
                    sp.wait_ge(y_stored[q], 16 * NBLK // SLOTS)

                def load(j, c):
                    if not isinstance(j, int):
                        sp.wait_ge(first_sum, NC * j + c - TAIL + 1)
                        sp.wait_ge(other_sum, NC * j + c - TAIL + 1)
                    sp.dma_start(yk[:, c, :], weighted[bass.ds((NC * j + c) * P * TOP_K, P * TOP_K), :]
                                 .rearrange("(p k) f -> p (k f)", k=TOP_K)).then_inc(g_loaded[c], 16)
                for c in range(NC):
                    load(0, c)
                with sp.Fori(1, NB) as j:
                    for c in range(NC):
                        load(j, c)

            @block.gpsimd
            def _(pool):
                def combine(j, c):
                    t = NC * j + c
                    pool.wait_ge(g_loaded[c], 16 * j + 16)
                    if not isinstance(j, int):
                        pool.wait_ge(second_sum, t - TAIL + 1)
                    pool.tensor_tensor(ysum[:, c, 0:D], yk[:, c, 0:D], yk[:, c, D:2 * D], ALU.add).then_inc(first_sum, 1)
                for c in range(NC):
                    combine(0, c)
                with pool.Fori(1, NB) as j:
                    for c in range(NC):
                        combine(j, c)

            @block.vector
            def _(dve):
                dve.wait_ge(gb_loaded, 16)

                def combine(j):
                    for c0 in range(0, NC, 2):
                        for c in (c0, c0 + 1):
                            dve.wait_ge(g_loaded[c], 16 * j + 16)
                            dve.tensor_tensor(ysum[:, c, D:2 * D], yk[:, c, 2 * D:3 * D], yk[:, c, 3 * D:4 * D], ALU.add)\
                                .then_inc(other_sum, 1)
                        for c in (c0, c0 + 1):
                            t = NC * j + c
                            dve.wait_ge(first_sum, t + 1)
                            dve.wait_ge(other_sum, t + 1)
                            dve.tensor_tensor(ysum2[:, c, :], ysum[:, c, 0:D], ysum[:, c, D:2 * D], ALU.add)\
                                .then_inc(second_sum, 1)
                        for c in (c0, c0 + 1):
                            dve.wait_ge(second_sum, NC * j + c + 1)
                            if not isinstance(j, int):
                                dve.wait_ge(out_stored[c], 16 * j)
                            dve.tensor_tensor(res[:, c:c + 1, :], ysum2[:, c:c + 1, :], gb_sb[:, bass.ds(j, 1), :], ALU.mult)\
                                .then_inc(gated, 1)
                        for c in (c0, c0 + 1):
                            t = NC * j + c
                            dve.wait_ge(gated, t + 1)
                            dve.tensor_tensor(res[:, c:c + 1, :], res[:, c:c + 1, :], x_all[:, bass.ds(t, 1), :], ALU.add)\
                                .then_inc(out_ready, 1)
                combine(0)
                with dve.Fori(1, NB) as j:
                    combine(j)

            @block.scalar
            def _(act):
                flat = out.rearrange("b t f -> (b t) f")
                with act.Fori(0, NB) as j:
                    for c in range(NC):
                        act.wait_ge(out_ready, NC * j + c + 1)
                        act.dma_start(flat[bass.ds((NC * j + c) * P, P), :], res[:, c, :]).then_inc(out_stored[c], 16)
                for c in range(NC):
                    act.wait_ge(out_stored[c], 16 * NB)
        phase_b.close()
    return nc


def kernel(L0_attn_x, L0_attn_Wq, L0_attn_bq, L0_attn_Wk, L0_attn_bk, L0_attn_Wv, L0_attn_bv, L0_attn_Wbeta,
           L0_attn_bbeta, L0_attn_Walpha, L0_attn_balpha, L0_ffn_router_w, L0_ffn_gate_w, L0_ffn_up_w,
           L0_ffn_down_w, L0_c, L0_wmod):
    import numpy as np
    import concourse.bacc as bacc
    from concourse.bass_utils import run_bass_kernel_spmd

    def on_partitions(w):
        w = np.asarray(w)
        return np.ascontiguousarray(w.reshape(-1, P, w.shape[-1]).transpose(1, 0, 2))

    D = L0_attn_x.shape[2]
    E, I, _ = L0_ffn_gate_w.shape
    gate_up = np.concatenate([np.asarray(L0_ffn_gate_w), np.asarray(L0_ffn_up_w)], axis=1)
    arrays = {
        "x": np.asarray(L0_attn_x),
        "wqk": on_partitions(np.concatenate([L0_attn_Wq, L0_attn_Wk], axis=1)),
        "wv": on_partitions(L0_attn_Wv),
        "wab": on_partitions(np.concatenate([L0_attn_Walpha, L0_attn_Wbeta], axis=1)),
        "bqk": np.ascontiguousarray(np.concatenate([L0_attn_bq, L0_attn_bk]).reshape(-1, P).T),
        "bv": np.asarray(L0_attn_bv).reshape(1, -1),
        "bab": np.concatenate([L0_attn_balpha, L0_attn_bbeta]).reshape(1, -1),
        "cT": on_partitions(np.asarray(L0_c).T),
        "wmod": on_partitions(L0_wmod),
        "rw": on_partitions(np.asarray(L0_ffn_router_w).T),
        "gu": np.ascontiguousarray(gate_up.transpose(2, 0, 1).reshape(D // P, P, E, 2 * I)
                                   .transpose(1, 2, 0, 3).reshape(P, E, D // P * 2 * I)),
        "dw": np.ascontiguousarray(np.asarray(L0_ffn_down_w).transpose(2, 0, 1)),
    }
    nc = bacc.Bacc("TRN2", target_bir_lowering=False, num_devices=1)
    aps = {n: nc.dram_tensor(f"in_{n}", a.shape, mybir.dt.from_np(a.dtype), kind="ExternalInput").ap()
           for n, a in arrays.items()}
    out = nc.dram_tensor("out", L0_attn_x.shape, F32, kind="ExternalOutput").ap()
    build(nc, **aps, out=out)
    r = run_bass_kernel_spmd(nc, [{f"in_{n}": a for n, a in arrays.items()}], core_ids=[0])
    return r.results[0]["out"]
```
